# Optimizing a Trainium2 kernel written in Bass

```python
import numpy as np
import jax
import jax.numpy as jnp

def _softmax(x, axis=-1):
    return jax.nn.softmax(x, axis=axis)

def _gelu(x):
    return jax.nn.gelu(x, approximate=True)

def _silu(x):
    return jax.nn.silu(x)

def _sigmoid(x):
    return jax.nn.sigmoid(x)

def _layernorm(x, axis=-1, eps=1e-05):
    m = jnp.mean(x, axis=axis, keepdims=True)
    v = jnp.var(x, axis=axis, keepdims=True)
    return (x - m) / jnp.sqrt(v + eps)

def _scatter_add(tgt, idx, src, axis=0):
    return tgt.at[idx].add(src)

def _segment_sum(src, seg, n):
    return jax.ops.segment_sum(src, seg, n)
kernel_name = 'mk_conv_attn_hybrid_d4_conv_nchw1024_r4_a5df83'

def setup_inputs(seed: int=0):
    np.random.seed(seed)
    _w = jnp.asarray

    def _rec_inputs():
        import jax
        import jax.numpy as jnp
        _gk = jax.random.key(seed)
        x = -0.0003929 + 0.9999 * jax.random.normal(jax.random.fold_in(_gk, 1), (4, 256, 16, 16), jnp.float32)
        return x
    x = _rec_inputs()

    def _L0_conv_setup():
        import jax, jax.numpy as jnp
        import numpy as np

        def conv(x, w, stride=1, pad=0):
            return jax.lax.conv_general_dilated(x, w, (stride, stride), [(pad, pad), (pad, pad)], dimension_numbers=('NCHW', 'OIHW', 'NCHW'))

        def group_norm(x, scale, bias, groups=32, eps=1e-05):
            B, C, H, W = x.shape
            xg = x.reshape(B, groups, C // groups, H, W)
            m = xg.mean(axis=(2, 3, 4), keepdims=True)
            v = xg.var(axis=(2, 3, 4), keepdims=True)
            xn = ((xg - m) * jax.lax.rsqrt(v + eps)).reshape(B, C, H, W)
            return xn * scale[None, :, None, None] + bias[None, :, None, None]

        def bilinear_sample(x, py, px):
            B, C, H, W = x.shape
            y0 = jnp.floor(py)
            x0 = jnp.floor(px)
            wy1 = py - y0
            wx1 = px - x0
            xf = x.reshape(B, C, H * W)
            Ksp = py.shape[1:]

            def corner(yi, xi, wy, wx):
                valid = (yi >= 0) & (yi < H) & (xi >= 0) & (xi < W)
                yc = jnp.clip(yi, 0, H - 1).astype(jnp.int32)
                xc = jnp.clip(xi, 0, W - 1).astype(jnp.int32)
                idx = (yc * W + xc).reshape(B, 1, -1)
                v = jnp.take_along_axis(xf, idx, axis=2).reshape(B, C, *Ksp)
                w = (wy * wx * valid).astype(x.dtype)[:, None]
                return v * w
            return corner(y0, x0, 1.0 - wy1, 1.0 - wx1) + corner(y0, x0 + 1, 1.0 - wy1, wx1) + corner(y0 + 1, x0, wy1, 1.0 - wx1) + corner(y0 + 1, x0 + 1, wy1, wx1)
        key = jax.random.key(seed)
        ks = jax.random.split(key, 8)
        B, Cin, H, W = (4, 256, 16, 16)
        Cb = 64
        x = jax.random.normal(ks[0], (B, Cin, H, W), dtype=jnp.float32)
        w1 = jax.random.normal(ks[1], (Cb, Cin, 1, 1), dtype=jnp.float32) * (1.0 / np.sqrt(Cin))
        w_off = jax.random.normal(ks[2], (27, Cb, 3, 3), dtype=jnp.float32) * 0.01
        b_off = jnp.zeros((27,), dtype=jnp.float32)
        w2 = jax.random.normal(ks[3], (Cb, Cb, 3, 3), dtype=jnp.float32) * (1.0 / np.sqrt(Cb * 9))
        w3 = jax.random.normal(ks[4], (Cin, Cb, 1, 1), dtype=jnp.float32) * (1.0 / np.sqrt(Cb))
        return {'x': x, 'w1': w1, 'gn1_scale': jnp.ones((Cb,), jnp.float32), 'gn1_bias': jnp.zeros((Cb,), jnp.float32), 'w_off': w_off, 'b_off': b_off, 'w2': w2, 'gn2_scale': jnp.ones((Cb,), jnp.float32), 'gn2_bias': jnp.zeros((Cb,), jnp.float32), 'w3': w3, 'gn3_scale': jnp.ones((Cin,), jnp.float32), 'gn3_bias': jnp.zeros((Cin,), jnp.float32), 'stride': 4}
    _L0_conv_all = _L0_conv_setup()
    _L0_conv_in = {k: v for k, v in _L0_conv_all.items() if k in ('w1', 'gn1_scale', 'gn1_bias', 'w_off', 'b_off', 'w2', 'gn2_scale', 'gn2_bias', 'w3', 'gn3_scale', 'gn3_bias')}
    del _L0_conv_all

    def _L1_conv_setup():
        import jax, jax.numpy as jnp
        import numpy as np
        from jax import lax
        C1 = 256
        C2 = 256
        D_STATE = 8
        HEADS = 2
        D_INNER = 256
        D_HEAD = D_INNER // HEADS

        def _mobius_perm(mobius, H, W):
            ys, xs = jnp.meshgrid(jnp.linspace(-1.0, 1.0, H), jnp.linspace(-1.0, 1.0, W), indexing='ij')
            z = (xs + 1j * ys).reshape(-1).astype(jnp.complex64)
            perms = []
            for h in range(mobius.shape[0]):
                a, b, c, d = (mobius[h, 0], mobius[h, 1], mobius[h, 2], mobius[h, 3])
                s = jnp.sqrt(jnp.clip(jnp.abs(a * d - b * c), 0.001))
                a, b, c, d = (a / s, b / s, c / s, d / s)
                w = (a * z + b) / (c * z + d + 1e-06)
                score = jnp.real(w) + 1.3 * jnp.imag(w)
                perms.append(jnp.argsort(score))
            return jnp.stack(perms, 0)

        def _gather_last(v, idx):
            return jnp.take_along_axis(v, jnp.broadcast_to(idx, v.shape[:-1] + (idx.shape[-1],)), axis=-1)

        def _selective_scan(x, dt, A, Bt, Ct, D):
            Bsz, Hh, Dh, N = x.shape
            S = A.shape[-1]
            dA = jnp.exp(dt[:, :, None, :] * A[None, :, :, None])
            dB = dt[:, :, None, :] * Bt

            def step(h, inp):
                dA_t, dB_t, x_t, C_t = inp
                h = dA_t[:, :, None, :] * h + dB_t[:, :, None, :] * x_t[..., None]
                y_t = jnp.einsum('bhds,bhs->bhd', h, C_t)
                return (h, y_t)
            h0 = jnp.zeros((Bsz, Hh, Dh, S), x.dtype)
            inputs = (jnp.moveaxis(dA, -1, 0), jnp.moveaxis(dB, -1, 0), jnp.moveaxis(x, -1, 0), jnp.moveaxis(Ct, -1, 0))
            _, ys = lax.scan(step, h0, inputs)
            return jnp.moveaxis(ys, 0, -1) + D[None, :, None, None] * x
        key = jax.random.key(seed)
        ks = jax.random.split(key, 8)
        S = D_STATE
        x = jax.random.normal(ks[0], (8, C1, 32, 32), jnp.float32)
        in_proj_w = jax.random.normal(ks[1], (3 * D_INNER, C1), jnp.float32) / np.sqrt(C1)
        in_proj_b = jnp.zeros((3 * D_INNER,), jnp.float32)
        dw_w = jax.random.normal(ks[2], (D_INNER, 1, 3), jnp.float32) / np.sqrt(3.0)
        dw_b = jnp.zeros((D_INNER,), jnp.float32)
        dbc_w = jax.random.normal(ks[3], (HEADS * (1 + 2 * S), D_INNER), jnp.float32) / np.sqrt(D_INNER)
        dbc_b = jnp.zeros((HEADS * (1 + 2 * S),), jnp.float32)
        A_log = jnp.log(jnp.tile(jnp.arange(1, S + 1, dtype=jnp.float32), (HEADS, 1)))
        Dparam = jnp.ones((HEADS,), jnp.float32)
        mobius = jnp.tile(jnp.array([[1.0, 0.0, 0.0, 1.0]], jnp.float32), (HEADS, 1)) + 0.05 * jax.random.normal(ks[4], (HEADS, 4), jnp.float32)
        out_proj_w = jax.random.normal(ks[5], (C2, D_INNER), jnp.float32) / np.sqrt(D_INNER)
        out_proj_b = jnp.zeros((C2,), jnp.float32)
        return dict(x=x, in_proj_w=in_proj_w, in_proj_b=in_proj_b, dw_w=dw_w, dw_b=dw_b, dbc_w=dbc_w, dbc_b=dbc_b, A_log=A_log, Dparam=Dparam, mobius=mobius, out_proj_w=out_proj_w, out_proj_b=out_proj_b)
    _L1_conv_all = _L1_conv_setup()
    _L1_conv_in = {k: v for k, v in _L1_conv_all.items() if k in ('in_proj_w', 'in_proj_b', 'dw_w', 'dw_b', 'dbc_w', 'dbc_b', 'A_log', 'Dparam', 'mobius', 'out_proj_w', 'out_proj_b')}
    del _L1_conv_all

    def _L2_attn_setup():
        import jax, jax.numpy as jnp
        import numpy as np
        B, N, DIM, H = (4, 512, 256, 16)
        HEAD_DIM = DIM // H
        SCALE = HEAD_DIM ** (-0.5)
        key = jax.random.key(seed)
        k1, k2, k3 = jax.random.split(key, 3)
        x = jax.random.normal(k1, (B, N, DIM), dtype=jnp.float32)
        w_qkv = jax.random.normal(k2, (DIM, 3 * DIM), dtype=jnp.float32) * DIM ** (-0.5)
        w_proj = jax.random.normal(k3, (DIM, DIM), dtype=jnp.float32) * DIM ** (-0.5)
        b_proj = jnp.zeros((DIM,), dtype=jnp.float32)
        return {'x': x, 'w_qkv': w_qkv, 'w_proj': w_proj, 'b_proj': b_proj}
    _L2_attn_all = _L2_attn_setup()
    _L2_attn_in = {k: v for k, v in _L2_attn_all.items() if k in ('w_qkv', 'w_proj', 'b_proj')}
    del _L2_attn_all

    def _L2_ffn_setup():
        import jax, jax.numpy as jnp
        import numpy as np
        B, T, D, H, E, TOPK = (2, 512, 256, 512, 8, 2)
        key = jax.random.key(seed)
        ks = jax.random.split(key, 5)
        s_in = 1.0 / np.sqrt(D)
        s_hid = 1.0 / np.sqrt(H)
        return {'x': jax.random.normal(ks[0], (B, T, D), dtype=jnp.float32), 'gate_w': jax.random.normal(ks[1], (E, D), dtype=jnp.float32) * s_in, 'w1': jax.random.normal(ks[2], (E, H, D), dtype=jnp.float32) * s_in, 'w2': jax.random.normal(ks[3], (E, D, H), dtype=jnp.float32) * s_hid, 'w3': jax.random.normal(ks[4], (E, H, D), dtype=jnp.float32) * s_in}
    _L2_ffn_all = _L2_ffn_setup()
    _L2_ffn_in = {k: v for k, v in _L2_ffn_all.items() if k in ('gate_w', 'w1', 'w2', 'w3')}
    del _L2_ffn_all

    def _L3_attn_setup():
        import jax, jax.numpy as jnp
        import numpy as np
        B, S, D, H = (4, 512, 256, 16)
        HD = D // H
        key = jax.random.key(seed)
        ks = jax.random.split(key, 6)
        scale = 1.0 / np.sqrt(D)
        return {'x': jax.random.normal(ks[0], (B, S, D), dtype=jnp.float32), 'Wq': jax.random.normal(ks[1], (D, D), dtype=jnp.float32) * scale, 'Wk': jax.random.normal(ks[2], (D, D), dtype=jnp.float32) * scale, 'Wv': jax.random.normal(ks[3], (D, D), dtype=jnp.float32) * scale, 'Wo': jax.random.normal(ks[4], (D, D), dtype=jnp.float32) * scale, 'bo': jnp.zeros((D,), dtype=jnp.float32)}
    _L3_attn_all = _L3_attn_setup()
    _L3_attn_in = {k: v for k, v in _L3_attn_all.items() if k in ('Wq', 'Wk', 'Wv', 'Wo', 'bo')}
    del _L3_attn_all

    def _L3_ffn_setup():
        import jax, jax.numpy as jnp
        import numpy as np
        NUM_EXPERTS = 8
        TOP_K = 2
        key = jax.random.key(seed)
        ks = jax.random.split(key, 5)
        B, S, D, H, E = (2, 512, 256, 1024, NUM_EXPERTS)
        scale = 0.02
        return {'x': jax.random.normal(ks[0], (B, S, D), dtype=jnp.float32), 'Wg': jax.random.normal(ks[1], (D, E), dtype=jnp.float32) * scale, 'W1': jax.random.normal(ks[2], (E, D, H), dtype=jnp.float32) * scale, 'W2': jax.random.normal(ks[3], (E, D, H), dtype=jnp.float32) * scale, 'W3': jax.random.normal(ks[4], (E, H, D), dtype=jnp.float32) * scale}
    _L3_ffn_all = _L3_ffn_setup()
    _L3_ffn_in = {k: v for k, v in _L3_ffn_all.items() if k in ('Wg', 'W1', 'W2', 'W3')}
    del _L3_ffn_all
    return {'x': x, 'L0_conv_w1': _L0_conv_in['w1'], 'L0_conv_gn1_scale': _L0_conv_in['gn1_scale'], 'L0_conv_gn1_bias': _L0_conv_in['gn1_bias'], 'L0_conv_w_off': _L0_conv_in['w_off'], 'L0_conv_b_off': _L0_conv_in['b_off'], 'L0_conv_w2': _L0_conv_in['w2'], 'L0_conv_gn2_scale': _L0_conv_in['gn2_scale'], 'L0_conv_gn2_bias': _L0_conv_in['gn2_bias'], 'L0_conv_w3': _L0_conv_in['w3'], 'L0_conv_gn3_scale': _L0_conv_in['gn3_scale'], 'L0_conv_gn3_bias': _L0_conv_in['gn3_bias'], 'L1_conv_in_proj_w': _L1_conv_in['in_proj_w'], 'L1_conv_in_proj_b': _L1_conv_in['in_proj_b'], 'L1_conv_dw_w': _L1_conv_in['dw_w'], 'L1_conv_dw_b': _L1_conv_in['dw_b'], 'L1_conv_dbc_w': _L1_conv_in['dbc_w'], 'L1_conv_dbc_b': _L1_conv_in['dbc_b'], 'L1_conv_A_log': _L1_conv_in['A_log'], 'L1_conv_Dparam': _L1_conv_in['Dparam'], 'L1_conv_mobius': _L1_conv_in['mobius'], 'L1_conv_out_proj_w': _L1_conv_in['out_proj_w'], 'L1_conv_out_proj_b': _L1_conv_in['out_proj_b'], 'L2_attn_w_qkv': _L2_attn_in['w_qkv'], 'L2_attn_w_proj': _L2_attn_in['w_proj'], 'L2_attn_b_proj': _L2_attn_in['b_proj'], 'L2_ffn_gate_w': _L2_ffn_in['gate_w'], 'L2_ffn_w1': _L2_ffn_in['w1'], 'L2_ffn_w2': _L2_ffn_in['w2'], 'L2_ffn_w3': _L2_ffn_in['w3'], 'L3_attn_Wq': _L3_attn_in['Wq'], 'L3_attn_Wk': _L3_attn_in['Wk'], 'L3_attn_Wv': _L3_attn_in['Wv'], 'L3_attn_Wo': _L3_attn_in['Wo'], 'L3_attn_bo': _L3_attn_in['bo'], 'L3_ffn_Wg': _L3_ffn_in['Wg'], 'L3_ffn_W1': _L3_ffn_in['W1'], 'L3_ffn_W2': _L3_ffn_in['W2'], 'L3_ffn_W3': _L3_ffn_in['W3']}

def reference(x, L0_conv_w1, L0_conv_gn1_scale, L0_conv_gn1_bias, L0_conv_w_off, L0_conv_b_off, L0_conv_w2, L0_conv_gn2_scale, L0_conv_gn2_bias, L0_conv_w3, L0_conv_gn3_scale, L0_conv_gn3_bias, L1_conv_in_proj_w, L1_conv_in_proj_b, L1_conv_dw_w, L1_conv_dw_b, L1_conv_dbc_w, L1_conv_dbc_b, L1_conv_A_log, L1_conv_Dparam, L1_conv_mobius, L1_conv_out_proj_w, L1_conv_out_proj_b, L2_attn_w_qkv, L2_attn_w_proj, L2_attn_b_proj, L2_ffn_gate_w, L2_ffn_w1, L2_ffn_w2, L2_ffn_w3, L3_attn_Wq, L3_attn_Wk, L3_attn_Wv, L3_attn_Wo, L3_attn_bo, L3_ffn_Wg, L3_ffn_W1, L3_ffn_W2, L3_ffn_W3):
    import jax
    import jax.numpy as jnp

    def _L0_conv_ref(x, w1, gn1_scale, gn1_bias, w_off, b_off, w2, gn2_scale, gn2_bias, w3, gn3_scale, gn3_bias, stride):
        import jax, jax.numpy as jnp
        import numpy as np

        def conv(x, w, stride=1, pad=0):
            return jax.lax.conv_general_dilated(x, w, (stride, stride), [(pad, pad), (pad, pad)], dimension_numbers=('NCHW', 'OIHW', 'NCHW'))

        def group_norm(x, scale, bias, groups=32, eps=1e-05):
            B, C, H, W = x.shape
            xg = x.reshape(B, groups, C // groups, H, W)
            m = xg.mean(axis=(2, 3, 4), keepdims=True)
            v = xg.var(axis=(2, 3, 4), keepdims=True)
            xn = ((xg - m) * jax.lax.rsqrt(v + eps)).reshape(B, C, H, W)
            return xn * scale[None, :, None, None] + bias[None, :, None, None]

        def bilinear_sample(x, py, px):
            B, C, H, W = x.shape
            y0 = jnp.floor(py)
            x0 = jnp.floor(px)
            wy1 = py - y0
            wx1 = px - x0
            xf = x.reshape(B, C, H * W)
            Ksp = py.shape[1:]

            def corner(yi, xi, wy, wx):
                valid = (yi >= 0) & (yi < H) & (xi >= 0) & (xi < W)
                yc = jnp.clip(yi, 0, H - 1).astype(jnp.int32)
                xc = jnp.clip(xi, 0, W - 1).astype(jnp.int32)
                idx = (yc * W + xc).reshape(B, 1, -1)
                v = jnp.take_along_axis(xf, idx, axis=2).reshape(B, C, *Ksp)
                w = (wy * wx * valid).astype(x.dtype)[:, None]
                return v * w
            return corner(y0, x0, 1.0 - wy1, 1.0 - wx1) + corner(y0, x0 + 1, 1.0 - wy1, wx1) + corner(y0 + 1, x0, wy1, 1.0 - wx1) + corner(y0 + 1, x0 + 1, wy1, wx1)
        out = conv(x, w1)
        out = jax.nn.relu(group_norm(out, gn1_scale, gn1_bias))
        om = conv(out, w_off, pad=1) + b_off[None, :, None, None]
        K = 9
        off_x = om[:, :K]
        off_y = om[:, K:2 * K]
        mask = jax.nn.sigmoid(om[:, 2 * K:])
        B, C, H, W = out.shape
        ky, kx = jnp.meshgrid(jnp.arange(3), jnp.arange(3), indexing='ij')
        ky = (ky.reshape(K) - 1).astype(om.dtype)
        kx = (kx.reshape(K) - 1).astype(om.dtype)
        grid_y = jnp.arange(H, dtype=om.dtype)[None, :, None] + ky[:, None, None]
        grid_x = jnp.arange(W, dtype=om.dtype)[None, None, :] + kx[:, None, None]
        py = grid_y[None] + off_y
        px = grid_x[None] + off_x
        sampled = bilinear_sample(out, py, px) * mask[:, None]
        out = jnp.einsum('bckhw,ock->bohw', sampled, w2.reshape(w2.shape[0], w2.shape[1], K))
        out = jax.nn.relu(group_norm(out, gn2_scale, gn2_bias))
        out = conv(out, w3)
        out = group_norm(out, gn3_scale, gn3_bias)
        return jax.nn.relu(out + x)

    def _L1_conv_ref(x, in_proj_w, in_proj_b, dw_w, dw_b, dbc_w, dbc_b, A_log, Dparam, mobius, out_proj_w, out_proj_b):
        import jax, jax.numpy as jnp
        import numpy as np
        from jax import lax
        C1 = 256
        C2 = 256
        D_STATE = 8
        HEADS = 2
        D_INNER = 256
        D_HEAD = D_INNER // HEADS

        def _mobius_perm(mobius, H, W):
            ys, xs = jnp.meshgrid(jnp.linspace(-1.0, 1.0, H), jnp.linspace(-1.0, 1.0, W), indexing='ij')
            z = (xs + 1j * ys).reshape(-1).astype(jnp.complex64)
            perms = []
            for h in range(mobius.shape[0]):
                a, b, c, d = (mobius[h, 0], mobius[h, 1], mobius[h, 2], mobius[h, 3])
                s = jnp.sqrt(jnp.clip(jnp.abs(a * d - b * c), 0.001))
                a, b, c, d = (a / s, b / s, c / s, d / s)
                w = (a * z + b) / (c * z + d + 1e-06)
                score = jnp.real(w) + 1.3 * jnp.imag(w)
                perms.append(jnp.argsort(score))
            return jnp.stack(perms, 0)

        def _gather_last(v, idx):
            return jnp.take_along_axis(v, jnp.broadcast_to(idx, v.shape[:-1] + (idx.shape[-1],)), axis=-1)

        def _selective_scan(x, dt, A, Bt, Ct, D):
            Bsz, Hh, Dh, N = x.shape
            S = A.shape[-1]
            dA = jnp.exp(dt[:, :, None, :] * A[None, :, :, None])
            dB = dt[:, :, None, :] * Bt

            def step(h, inp):
                dA_t, dB_t, x_t, C_t = inp
                h = dA_t[:, :, None, :] * h + dB_t[:, :, None, :] * x_t[..., None]
                y_t = jnp.einsum('bhds,bhs->bhd', h, C_t)
                return (h, y_t)
            h0 = jnp.zeros((Bsz, Hh, Dh, S), x.dtype)
            inputs = (jnp.moveaxis(dA, -1, 0), jnp.moveaxis(dB, -1, 0), jnp.moveaxis(x, -1, 0), jnp.moveaxis(Ct, -1, 0))
            _, ys = lax.scan(step, h0, inputs)
            return jnp.moveaxis(ys, 0, -1) + D[None, :, None, None] * x
        Bsz, _, H, W = x.shape
        N = H * W
        heads, S = A_log.shape
        d_inner = dw_w.shape[0]
        d_head = d_inner // heads
        xz = jax.nn.silu(jnp.einsum('oc,bchw->bohw', in_proj_w, x) + in_proj_b[None, :, None, None])
        x_ssm, res, gate = jnp.split(xz, 3, axis=1)
        xf = x_ssm.reshape(Bsz, d_inner, N)
        xf = lax.conv_general_dilated(xf, dw_w, (1,), [(1, 1)], dimension_numbers=('NCH', 'OIH', 'NCH'), feature_group_count=d_inner) + dw_b[None, :, None]
        xf = jax.nn.silu(xf)
        x_h = xf.reshape(Bsz, heads, d_head, N)
        perm = _mobius_perm(mobius, H, W)
        x_h = _gather_last(x_h, perm[None, :, None, :])
        dbc = (jnp.einsum('oc,bcn->bon', dbc_w, xf) + dbc_b[None, :, None]).reshape(Bsz, heads, 1 + 2 * S, N)
        dt = jax.nn.softplus(dbc[:, :, 0])
        B_t = dbc[:, :, 1:1 + S]
        C_t = dbc[:, :, 1 + S:]
        dt = _gather_last(dt, perm[None, :, :])
        B_t = _gather_last(B_t, perm[None, :, None, :])
        C_t = _gather_last(C_t, perm[None, :, None, :])
        A = -jnp.exp(A_log)
        y_h = _selective_scan(x_h, dt, A, B_t, C_t, Dparam)
        inv = jnp.argsort(perm, axis=-1)
        y_h = _gather_last(y_h, inv[None, :, None, :])
        y = y_h.reshape(Bsz, d_inner, H, W)
        y = y * jax.nn.silu(gate) + res
        return jax.nn.silu(jnp.einsum('oc,bchw->bohw', out_proj_w, y) + out_proj_b[None, :, None, None])

    def _L2_attn_ref(x, w_qkv, w_proj, b_proj):
        import jax, jax.numpy as jnp
        import numpy as np
        B, N, DIM, H = (4, 512, 256, 16)
        HEAD_DIM = DIM // H
        SCALE = HEAD_DIM ** (-0.5)
        Bs, Ns, C = x.shape
        qkv = x @ w_qkv
        q, k, v = jnp.split(qkv, 3, axis=-1)

        def heads(t):
            return t.reshape(Bs, Ns, H, HEAD_DIM).transpose(0, 2, 1, 3)
        q, k, v = (heads(q), heads(k), heads(v))
        attn = jnp.einsum('bhnd,bhmd->bhnm', q, k) * SCALE
        attn = jax.nn.softmax(attn, axis=-1)
        out = jnp.einsum('bhnm,bhmd->bhnd', attn, v)
        out = out.transpose(0, 2, 1, 3).reshape(Bs, Ns, C)
        return out @ w_proj + b_proj

    def _L2_ffn_ref(x, gate_w, w1, w2, w3):
        import jax, jax.numpy as jnp
        import numpy as np
        B, T, D, H, E, TOPK = (2, 512, 256, 512, 8, 2)
        b, t, d = x.shape
        flat = x.reshape(-1, d)
        probs = jax.nn.softmax(flat @ gate_w.T, axis=-1)
        weights, idx = jax.lax.top_k(probs, TOPK)
        weights = weights / jnp.sum(weights, axis=-1, keepdims=True)
        combine = jnp.sum(jax.nn.one_hot(idx, E, dtype=flat.dtype) * weights[..., None], axis=1)
        h1 = jnp.einsum('nd,ehd->neh', flat, w1)
        h3 = jnp.einsum('nd,ehd->neh', flat, w3)
        y = jnp.einsum('neh,edh->ned', jax.nn.silu(h1) * h3, w2)
        out = jnp.einsum('ned,ne->nd', y, combine)
        return out.reshape(b, t, d)

    def _L3_attn_ref(x, Wq, Wk, Wv, Wo, bo):
        import jax, jax.numpy as jnp
        import numpy as np
        B, S, D, H = (4, 512, 256, 16)
        HD = D // H
        b, s, d = x.shape
        q = (x @ Wq).reshape(b, s, H, HD).transpose(0, 2, 1, 3)
        k = (x @ Wk).reshape(b, s, H, HD).transpose(0, 2, 1, 3)
        v = (x @ Wv).reshape(b, s, H, HD).transpose(0, 2, 1, 3)
        scores = jnp.einsum('bhqd,bhkd->bhqk', q, k)
        causal = jnp.tril(jnp.ones((s, s), dtype=bool))
        scores = jnp.where(causal, scores, -jnp.inf)
        attn = jax.nn.softmax(scores / np.sqrt(HD), axis=-1)
        ctx = jnp.einsum('bhqk,bhkd->bhqd', attn, v)
        ctx = ctx.transpose(0, 2, 1, 3).reshape(b, s, d)
        return ctx @ Wo + bo

    def _L3_ffn_ref(x, Wg, W1, W2, W3):
        import jax, jax.numpy as jnp
        import numpy as np
        NUM_EXPERTS = 8
        TOP_K = 2
        score = jnp.einsum('bsd,de->bse', x, Wg)
        topk_score, topk_idx = jax.lax.top_k(score, TOP_K)
        topk_prob = jax.nn.softmax(topk_score, axis=-1)
        h1 = jnp.einsum('bsd,edh->bseh', x, W1)
        h2 = jnp.einsum('bsd,edh->bseh', x, W2)
        expert_out = jnp.einsum('bseh,ehd->bsed', jax.nn.silu(h1) * h2, W3)
        onehot = jax.nn.one_hot(topk_idx, NUM_EXPERTS, dtype=x.dtype)
        gate_prob = jnp.einsum('bske,bsk->bse', onehot, topk_prob)
        out = jnp.einsum('bsed,bse->bsd', expert_out, gate_prob)
        return out

    def _gn(v, G=32, eps=1e-05):
        B_, C_, H_, W_ = v.shape
        g = v.reshape(B_, G, C_ // G, H_, W_)
        m = jnp.mean(g, axis=(2, 3, 4), keepdims=True)
        s = jnp.var(g, axis=(2, 3, 4), keepdims=True)
        return ((g - m) / jnp.sqrt(s + eps)).reshape(v.shape)

    def _ln_c(v, eps=1e-06):
        m = jnp.mean(v, axis=1, keepdims=True)
        s = jnp.var(v, axis=1, keepdims=True)
        return (v - m) / jnp.sqrt(s + eps)

    def _ln_t(v, eps=1e-05):
        m = jnp.mean(v, axis=-1, keepdims=True)
        s = jnp.var(v, axis=-1, keepdims=True)
        return (v - m) / jnp.sqrt(s + eps)

    def _to_tokens(v):
        B_, C_, H_, W_ = v.shape
        return v.reshape(B_, C_, H_ * W_).transpose(0, 2, 1)

    def _from_tokens(t, like):
        B_, C_, H_, W_ = like.shape
        return t.transpose(0, 2, 1).reshape(B_, C_, H_, W_)
    x = _L0_conv_ref(x, L0_conv_w1, L0_conv_gn1_scale, L0_conv_gn1_bias, L0_conv_w_off, L0_conv_b_off, L0_conv_w2, L0_conv_gn2_scale, L0_conv_gn2_bias, L0_conv_w3, L0_conv_gn3_scale, L0_conv_gn3_bias, 4)
    x = x + _L1_conv_ref(_gn(x), L1_conv_in_proj_w, L1_conv_in_proj_b, L1_conv_dw_w, L1_conv_dw_b, L1_conv_dbc_w, L1_conv_dbc_b, L1_conv_A_log, L1_conv_Dparam, L1_conv_mobius, L1_conv_out_proj_w, L1_conv_out_proj_b)
    t = _to_tokens(x)
    t = t + _L2_attn_ref(_ln_t(t), L2_attn_w_qkv, L2_attn_w_proj, L2_attn_b_proj)
    t = t + _L2_ffn_ref(_ln_t(t), L2_ffn_gate_w, L2_ffn_w1, L2_ffn_w2, L2_ffn_w3)
    t = t + _L3_attn_ref(_ln_t(t), L3_attn_Wq, L3_attn_Wk, L3_attn_Wv, L3_attn_Wo, L3_attn_bo)
    t = t + _L3_ffn_ref(_ln_t(t), L3_ffn_Wg, L3_ffn_W1, L3_ffn_W2, L3_ffn_W3)
    x = _from_tokens(t, x)
    return x

_drawn_inputs = setup_inputs


def setup_inputs(seed=0):
    import zlib

    import numpy as np

    out = dict(_drawn_inputs(seed))
    spreads = {'L0_conv_gn1_scale': (1.0, 0.2),
     'L0_conv_gn1_bias': (0.0, 0.1),
     'L0_conv_b_off': (0.0, 0.1),
     'L0_conv_gn2_scale': (1.0, 0.2),
     'L0_conv_gn2_bias': (0.0, 0.1),
     'L0_conv_gn3_scale': (1.0, 0.2),
     'L0_conv_gn3_bias': (0.0, 0.1),
     'L1_conv_in_proj_b': (0.0, 0.1),
     'L1_conv_dw_b': (0.0, 0.1),
     'L1_conv_dbc_b': (0.0, 0.407),
     'L1_conv_Dparam': (1.0, 0.6),
     'L1_conv_out_proj_b': (0.0, 0.1),
     'L2_attn_b_proj': (0.0, 0.1),
     'L3_attn_bo': (0.0, 0.1)}
    factors = {'L1_conv_A_log': 4.175,
     'L1_conv_mobius': 3.466,
     'L3_ffn_Wg': 3.716,
     'L3_ffn_W1': 3.39,
     'L3_ffn_W2': 3.374,
     'L3_ffn_W3': 3.352}
    for name, (base, spread) in spreads.items():
        noise = np.random.default_rng([zlib.crc32(name.encode()), seed]).standard_normal(out[name].shape)
        drawn = base * np.exp(spread * noise) if base else spread * noise
        out[name] = jnp.asarray(drawn.astype(out[name].dtype))
    for name, factor in factors.items():
        out[name] = (out[name] * factor).astype(out[name].dtype)
    return out
```

```python
from contextlib import ExitStack

import numpy as np

import concourse.bass as bass
from concourse import mybir

F32 = mybir.dt.float32
BF16 = mybir.dt.bfloat16
I32 = mybir.dt.int32
U32 = mybir.dt.uint32
ACT = mybir.ActivationFunctionType
ALU = mybir.AluOpType
AX_X = mybir.AxisListType.X

P = 128
B, C, HW = 4, 256, 16
N = HW * HW
TOK = B * N
CT = C // P
NT = N // P
TT = TOK // P
CB = 64
TAPS = 9
S = 8
HEADS = 2
AH, HD = 16, 16
E = 8
MAXBLK = (2 * TOK + E * (P - 1)) // P
SLOTS = MAXBLK * P
BANK = 512


class GroupNorm:

    def __init__(self, name, sb, sem, parts, cols, eps):
        self.parts, self.cols, self.eps = parts, cols, eps
        self.raw = sb(f"{name}_raw", [parts, cols, 6])
        self.moments = sb(f"{name}_moments", [parts, cols, 2])
        self.square = sb(f"{name}_square", [parts, cols])
        self.group = sb(f"{name}_group", [parts, cols, 2])
        self.var = sb(f"{name}_var", [parts, cols])
        self.sd = sb(f"{name}_sd", [parts, cols])
        self.scale = sb(f"{name}_scale", [parts, cols])
        self.shift = sb(f"{name}_shift", [parts, cols])
        self.s_stats = sem(f"{name}_stats")
        self.s_moments = sem(f"{name}_moments")
        self.s_grouped = sem(f"{name}_grouped")
        self.s_var = sem(f"{name}_var")
        self.s_sd = sem(f"{name}_sd")
        self.s_affine = sem(f"{name}_affine")

    def stats(self, dve, column, source):
        dve.bn_stats(self.raw[:, column, :], source).then_inc(self.s_stats, 1)

    def partition_moments(self, dve):
        dve.wait_ge(self.s_stats, self.cols)
        for c in range(self.cols):
            last = dve.bn_aggr(self.moments[:, c, :], self.raw[:, c, :])
        last.then_inc(self.s_moments, 1)
        dve.wait_ge(self.s_moments, 1)
        dve.tensor_tensor(self.square[:], self.moments[:, :, 0], self.moments[:, :, 0],
                          ALU.mult).then_inc(self.s_moments, 1)
        dve.wait_ge(self.s_moments, 2)
        dve.tensor_tensor(self.moments[:, :, 1], self.moments[:, :, 1], self.square[:],
                          ALU.add).then_inc(self.s_moments, 1)

    def group_mean(self, pe, psum, averaging):
        pe.wait_ge(self.s_moments, 3)
        pe.matmul(psum, averaging, self.moments[:].rearrange("p c k -> p (c k)"),
                  start=True, stop=True).then_inc(self.s_grouped, 1)

    def variance(self, dve, psum):
        dve.wait_ge(self.s_grouped, 1)
        dve.tensor_copy(self.group[:].rearrange("p c k -> p (c k)"), psum).then_inc(self.s_var, 1)
        dve.wait_ge(self.s_var, 1)
        dve.tensor_tensor(self.square[:], self.group[:, :, 0], self.group[:, :, 0],
                          ALU.mult).then_inc(self.s_var, 1)
        dve.wait_ge(self.s_var, 2)
        dve.scalar_tensor_tensor(self.var[:], self.group[:, :, 1], self.eps, self.square[:],
                                 ALU.add, ALU.subtract).then_inc(self.s_var, 1)

    def deviation(self, act):
        act.wait_ge(self.s_var, 3)
        act.activation(self.sd[:], self.var[:], ACT.Sqrt).then_inc(self.s_sd, 1)

    def affine(self, dve, gamma=None, beta=None):
        dve.wait_ge(self.s_sd, 1)
        dve.reciprocal(self.scale[:], self.sd[:]).then_inc(self.s_affine, 1)
        if gamma is not None:
            dve.wait_ge(self.s_affine, 1)
            dve.tensor_tensor(self.scale[:], self.scale[:], gamma, ALU.mult).then_inc(self.s_affine, 1)
        else:
            dve.engine_nop().then_inc(self.s_affine, 1)
        dve.wait_ge(self.s_affine, 2)
        dve.tensor_tensor(self.shift[:], self.group[:, :, 0], self.scale[:], ALU.mult).then_inc(self.s_affine, 1)
        dve.wait_ge(self.s_affine, 3)
        if beta is not None:
            dve.tensor_tensor(self.shift[:], beta, self.shift[:], ALU.subtract).then_inc(self.s_affine, 1)
        else:
            dve.tensor_scalar(self.shift[:], self.shift[:], -1.0, None, ALU.mult).then_inc(self.s_affine, 1)

    READY = 4


def deformable_conv(nc, sem, sbuf, psum, k):
    with ExitStack() as ctx:
        def sb(name, shape, dt=F32):
            return ctx.enter_context(nc.sbuf_tensor(name, shape, dt))

        x = sb("x_in", [P, CT, B, N])
        w1 = sb("w1", [P, CT, CB])
        image = sb("image", [CB, 3, B, HW + 2, HW])
        w_off = sb("w_off", [CB, TAPS, 27])
        b_off = sb("b_off", [1, 27])
        w2 = sb("w2", [CB, TAPS * CB])
        w3 = sb("w3", [CB, C])
        gn64 = sb("gn64", [CB, 4, B])
        gn256 = sb("gn256", [P, 2, CT * B])
        pair = sb("pair", [CB, CB])
        grid = sb("grid", [P, TT, 2 * TAPS])
        iota = sb("iota", [P, HW])
        ones = sb("ones_row", [1, P])
        om = sb("om", [P, TT, 3 * TAPS])
        pos = sb("pos", [P, TT, 2 * TAPS])
        deformed = sb("deformed", [CB, B, N])
        mask = sb("mask", [P, TT, TAPS])
        hat = sb("hat", [P, TT, 2 * TAPS, HW])
        weights = sb("weights", [P, 2, NT, TAPS, N])
        weights_t = k.ring_late[:, 0:2 * NT * TAPS * N].rearrange("p (b k n) -> p b k n", b=2, n=N)
        mixed = sb("mixed", [P, 2, NT, TAPS, CB])
        r2 = sb("r2", [CB, B, N])
        pre = k.h[:].rearrange("p t b n -> p (t b) n")
        zeros = sb("zeros", [P, 2 * C])

        g1 = GroupNorm("gn1", sb, sem, CB, B, 1e-5)
        g2 = GroupNorm("gn2", sb, sem, CB, B, 1e-5)
        g3 = GroupNorm("gn3", sb, sem, P, CT * B, 1e-5)
        g4 = GroupNorm("gn4", sb, sem, P, CT * B, 1e-5)

        s_x = sem("x_loaded")
        s_w = sem("l0_weights_loaded")
        s_c1 = sem("conv1")
        s_pad = sem("padding_zeroed")
        s_img = sem("image_ready")
        s_moved = sem("moved_images_ready")
        s_om = sem("offsets")
        s_oms = sem("offsets_on_sbuf")
        s_yo = sem("deformed_out")
        s_mask = sem("mask_ready")
        s_hat = sem("hat_steps")
        s_wd = sem("weights_dve")
        s_wp = sem("weights_pool")
        s_tr = sem("weights_transposed")
        s_ea = sem("transpose_out_act")
        s_ed = sem("transpose_out_dve")
        s_mix = sem("mixed_product")
        s_mo = sem("mixed_out")
        s_y = sem("deformed")
        s_r2 = sem("r2_ready")
        s_c3 = sem("conv3")
        s_pre = sem("pre_residual")
        s_x1 = sem("x1_ready")
        s_h1 = sem("h1_ready")

        GROUP = 2
        BANKS = NT * TAPS // GROUP
        y_banks = 6
        block = ctx.enter_context(nc.Block())

        @block.sync
        def _(sp):
            sp.dma_start(w1[:], k.dram["w1"]).then_inc(s_w, 16)
            sp.dma_start(x[:], k.dram["x"]).then_inc(s_x, 16)
            for dst, src in ((k.ident_sb, k.dram["ident"]), (k.avg8_sb, k.dram["avg8"]), (w_off, k.dram["w_off"]), (b_off, k.dram["b_off"]), (w2, k.dram["w2"]),
                             (w3, k.dram["w3"]), (gn64, k.dram["gn64"]), (gn256, k.dram["gn256"]), (pair, k.dram["pair"]),
                             (grid, k.dram["grid"]), (iota, k.dram["iota"]), (ones, k.dram["ones"])):
                sp.dma_start(dst[:], src).then_inc(s_w, 16)

            load_experts(sp, k, k.dram["f2_experts"], 1, range(RING_CHUNKS // 2), k.s_ring2)
            sp.wait_ge(s_pad, 2)
            sp.dma_start(k.rows_in.rearrange("(p a) c -> p (a c)", p=P).rearrange("p (a c) -> p a c", c=2 * C),
                         zeros[:].unsqueeze(1).broadcast_to([P, PAIRED // 2, 2 * C])).then_inc(k.s_cleared, 16)

        LOADED = 16 * 13

        @block.gpsimd
        def _(pool):
            pool.memset(image[:], 0.0).then_inc(s_pad, 1)
            pool.memset(zeros[:], 0.0).then_inc(s_pad, 1)
            for b in range(B):
                T = NT * b + 1
                pool.wait_ge(s_hat, 3)
                if b >= 2:
                    pool.wait_ge(s_tr, BANKS * (b - 1))
                pool.tensor_tensor(weights[:, b % 2, 1, :, :].rearrange("p k (y x) -> p k y x", y=HW),
                                   hat[:, T, TAPS:, :].unsqueeze(3).broadcast_to([P, TAPS, HW, HW]),
                                   hat[:, T, :TAPS, :].unsqueeze(2).broadcast_to([P, TAPS, HW, HW]),
                                   ALU.mult).then_inc(s_wp, 1)

        @block.vector
        def _(dve):
            dve.wait_ge(s_c1, 1)
            for b in range(B):
                g1.stats(dve, b, psum[0:CB, y_banks + b // 2, (b % 2) * N:(b % 2) * N + N])
            g1.partition_moments(dve)
            g1.variance(dve, psum[0:CB, 4, 0:2 * B])
            dve.wait_ge(s_w, LOADED)
            g1.affine(dve, gn64[:, 0, :], gn64[:, 1, :])
            dve.wait_ge(s_img, B)
            dve.tensor_copy(image[:, 2, :, 1:HW + 1, 0:HW - 1], image[:, 1, :, 1:HW + 1, 1:HW]).then_inc(s_moved, 1)
            dve.wait_ge(s_om, 1)
            dve.tensor_copy(om[:].rearrange("p t o -> p (t o)"), psum[:, 5, 0:TT * 3 * TAPS]).then_inc(s_oms, 1)
            dve.wait_ge(s_oms, 1)
            dve.tensor_tensor(pos[:], om[:, :, 0:2 * TAPS], grid[:], ALU.add).then_inc(s_hat, 1)
            dve.wait_ge(s_hat, 1)
            shape = [P, TT * 2 * TAPS, HW]
            hats = hat[:].rearrange("p t k i -> p (t k) i")
            dve.tensor_tensor(hats, pos[:].rearrange("p t k -> p (t k)").unsqueeze(2).broadcast_to(shape),
                              iota[:].unsqueeze(1).broadcast_to(shape), ALU.subtract).then_inc(s_hat, 1)
            dve.wait_ge(s_mask, 3)
            dve.tensor_tensor(hat[:, :, TAPS:, :], hat[:, :, TAPS:, :],
                              mask[:].unsqueeze(3).broadcast_to([P, TT, TAPS, HW]), ALU.mult).then_inc(s_hat, 1)
            dve.wait_ge(s_hat, 3)

            def sampling(b):
                if b >= 2:
                    dve.wait_ge(s_tr, BANKS * (b - 1))
                T = NT * b
                dve.tensor_tensor(weights[:, b % 2, 0, :, :].rearrange("p k (y x) -> p k y x", y=HW),
                                  hat[:, T, TAPS:, :].unsqueeze(3).broadcast_to([P, TAPS, HW, HW]),
                                  hat[:, T, :TAPS, :].unsqueeze(2).broadcast_to([P, TAPS, HW, HW]),
                                  ALU.mult).then_inc(s_wd, 1)

            def take(b):
                dve.wait_ge(s_y, b + 1)
                dve.tensor_copy(deformed[:, b, :], psum[0:CB, y_banks + b % 2, 0:N]).then_inc(s_yo, 1)
                dve.wait_ge(s_yo, b + 1)
                g2.stats(dve, b, deformed[:, b, :])

            sampling(0)
            for b in range(B):
                if b + 1 < B:
                    sampling(b + 1)
                for j in range(BANKS):
                    J = BANKS * b + j
                    if J % 2 == 1:
                        dve.wait_ge(s_tr, J + 1)
                        if b >= 2:
                            dve.wait_ge(s_y, b - 1)
                        dve.tensor_copy(weights_t[:, b % 2, GROUP * j:GROUP * j + GROUP, :].rearrange("p a n -> p (a n)"),
                                        psum[:, J % 4, :]).then_inc(s_ed, 1)
                if b >= 1:
                    take(b - 1)
            take(B - 1)
            g2.partition_moments(dve)
            g2.variance(dve, psum[0:CB, 4, 0:2 * B])
            g2.affine(dve, gn64[:, 2, :], gn64[:, 3, :])
            dve.wait_ge(s_c3, 1)
            for i in range(CT * B):
                g3.stats(dve, i, psum[:, i // 2, (i % 2) * N:(i % 2) * N + N])
            g3.partition_moments(dve)
            g3.variance(dve, psum[:, 4, 0:2 * CT * B])
            g3.affine(dve, gn256[:, 0, :], gn256[:, 1, :])
            dve.wait_ge(g3.s_affine, g3.READY)
            xs = x[:].rearrange("p t b n -> p (t b) n")
            for i in range(CT * B):
                dve.scalar_tensor_tensor(pre[:, i, :], psum[:, i // 2, (i % 2) * N:(i % 2) * N + N],
                                         g3.scale[:, i:i + 1], xs[:, i, :], ALU.mult, ALU.add).then_inc(s_pre, 1)
            for i in range(CT * B):
                dve.wait_ge(s_x1, i + 1)
                g4.stats(dve, i, k.x1[:].rearrange("p t b n -> p (t b) n")[:, i, :])
            g4.partition_moments(dve)
            g4.variance(dve, psum[:, 5, 0:2 * CT * B])
            g4.affine(dve)
            dve.wait_ge(g4.s_affine, g4.READY)
            for i in range(CT * B):
                dve.tensor_scalar(k.h[:].rearrange("p t b n -> p (t b) n")[:, i, :],
                                  k.x1[:].rearrange("p t b n -> p (t b) n")[:, i, :],
                                  g4.scale[:, i:i + 1], g4.shift[:, i:i + 1], ALU.mult, ALU.add).then_inc(s_h1, 1)

        @block.scalar
        def _(act):
            g1.deviation(act)
            act.wait_ge(g1.s_affine, g1.READY)
            act.wait_ge(s_pad, 1)
            for b in range(B):
                act.activation(image[:, 1, b, 1:HW + 1, :],
                               psum[0:CB, y_banks + b // 2, (b % 2) * N:(b % 2) * N + N].rearrange("p (y x) -> p y x", y=HW),
                               ACT.Relu, bias=g1.shift[:, b:b + 1], scale=g1.scale[:, b:b + 1]).then_inc(s_img, 1)
            act.wait_ge(s_img, B)
            act.activation(image[:, 0, :, 1:HW + 1, 1:HW], image[:, 1, :, 1:HW + 1, 0:HW - 1],
                           ACT.Copy).then_inc(s_moved, 1)
            act.wait_ge(s_oms, 1)
            act.activation(mask[:], om[:, :, 2 * TAPS:], ACT.Sigmoid).then_inc(s_mask, 1)
            act.wait_ge(s_hat, 2)
            hats = hat[:].rearrange("p t k i -> p (t k i)")
            act.activation(hats, hats, ACT.Abs).then_inc(s_mask, 1)
            act.wait_ge(s_mask, 2)
            act.activation(hats, hats, ACT.Relu, bias=1.0, scale=-1.0).then_inc(s_mask, 1)
            for b in range(B):
                for s in range(NT):
                    i = NT * b + s
                    act.wait_ge(s_mix, i + 1)
                    if b >= 2:
                        act.wait_ge(s_y, b - 1)
                    act.activation(mixed[:, b % 2, s, :, :].rearrange("p k o -> p (k o)").rearrange("p (a n) -> p a n", a=2),
                                   psum[:, 4:6, 0:TAPS * CB // 2], ACT.Copy).then_inc(s_mo, 1)
                for j in range(BANKS):
                    J = BANKS * b + j
                    if J % 2 == 0:
                        act.wait_ge(s_tr, J + 1)
                        if b >= 2:
                            act.wait_ge(s_y, b - 1)
                        act.activation(weights_t[:, b % 2, GROUP * j:GROUP * j + GROUP, :].rearrange("p a n -> p (a n)"),
                                       psum[:, J % 4, :], ACT.Copy).then_inc(s_ea, 1)
            g2.deviation(act)
            act.wait_ge(g2.s_affine, g2.READY)
            for b in range(B):
                act.activation(r2[:, b, :], deformed[:, b, :], ACT.Relu,
                               bias=g2.shift[:, b:b + 1], scale=g2.scale[:, b:b + 1]).then_inc(s_r2, 1)
            g3.deviation(act)
            act.wait_ge(g3.s_affine, g3.READY)
            for i in range(CT * B):
                act.wait_ge(s_pre, i + 1)
                act.activation(k.x1[:].rearrange("p t b n -> p (t b) n")[:, i, :], pre[:, i, :], ACT.Relu,
                               bias=g3.shift[:, i:i + 1]).then_inc(s_x1, 1)
            g4.deviation(act)

        @block.tensor
        def _(pe):
            pe.wait_ge(s_w, 16)
            pe.wait_ge(s_x, 16)
            pe.wait_ge(s_w, LOADED)
            for half in range(2):
                for t in range(CT):
                    last = pe.matmul(psum[0:CB, y_banks + half, :], w1[:, t, :],
                                     x[:, t, 2 * half:2 * half + 2, :].rearrange("p b n -> p (b n)"),
                                     start=(t == 0), stop=(t == CT - 1))
            last.then_inc(s_c1, 1)
            g1.group_mean(pe, psum[0:CB, 4, 0:2 * B], pair[:])
            pe.wait_ge(s_moved, 2)

            def rows(dx, b, y):
                return image[:, dx, b, y:y + HW // NT, :].rearrange("p y x -> p (y x)")

            for T in range(TT):
                b, y0 = T // NT, (T % NT) * HW // NT
                out = psum[:, 5, 27 * T:27 * T + 27]
                for tap in range(TAPS):
                    dy, dx = tap // 3, tap % 3
                    pe.matmul(out, rows(dx, b, y0 + dy), w_off[:, tap, :],
                              start=(tap == 0), stop=False)
                last = pe.matmul(out, ones[:], b_off[:], start=False, stop=True)
            last.then_inc(s_om, 1)
            for b in range(B):
                for s in range(NT):
                    i = NT * b + s
                    if i >= 1:
                        pe.wait_ge(s_mo, i)
                    else:
                        pe.wait_ge(s_oms, 1)
                    for a in range(2):
                        last = pe.matmul(psum[:, 4 + a, 0:TAPS * CB // 2], rows(1, b, 1 + s * HW // NT),
                                         w2[:, a * TAPS * CB // 2:(a + 1) * TAPS * CB // 2], start=True, stop=True)
                    last.then_inc(s_mix, 1)
                pe.wait_ge(s_wd, b + 1)
                pe.wait_ge(s_wp, b + 1)
                for j in range(BANKS):
                    J = BANKS * b + j
                    if J >= 4:
                        pe.wait_ge(s_ea if J % 2 == 0 else s_ed, (J - 4) // 2 + 1)
                    for a in range(GROUP):
                        s, tap = (GROUP * j + a) // TAPS, (GROUP * j + a) % TAPS
                        for t in range(NT):
                            last = pe.transpose(psum[:, J % 4, a * N + P * t:a * N + P * t + P],
                                                weights[:, b % 2, t, tap, P * s:P * s + P], k.ident_sb[:])
                    last.then_inc(s_tr, 1)
                pe.wait_ge(s_mo, NT * (b + 1))
                pe.wait_ge(s_ea, (BANKS * (b + 1) + 1) // 2)
                pe.wait_ge(s_ed, BANKS * (b + 1) // 2)
                if b >= 2:
                    pe.wait_ge(s_yo, b - 1)
                for i in range(NT * TAPS):
                    last = pe.matmul(psum[0:CB, y_banks + b % 2, 0:N],
                                     mixed[:, b % 2, i // TAPS, i % TAPS, :], weights_t[:, b % 2, i, :],
                                     start=(i == 0), stop=(i == NT * TAPS - 1))
                last.then_inc(s_y, 1)
            g2.group_mean(pe, psum[0:CB, 4, 0:2 * B], pair[:])
            pe.wait_ge(s_r2, B)
            for t in range(CT):
                for half in range(2):
                    last = pe.matmul(psum[:, 2 * t + half, :], w3[:, P * t:P * t + P],
                                     r2[:, 2 * half:2 * half + 2, :].rearrange("p b n -> p (b n)"),
                                     start=True, stop=True)
            last.then_inc(s_c3, 1)
            g3.group_mean(pe, psum[:, 4, 0:2 * CT * B], k.avg8_sb[:])
            g4.group_mean(pe, psum[:, 5, 0:2 * CT * B], k.avg8_sb[:])


def selective_scan(nc, sem, sbuf, psum, k):
    QROWS = 32
    DEEP = 3
    ROWS = 3 * S
    with ExitStack() as ctx:
        def sb(name, shape, dt=F32):
            return ctx.enter_context(nc.sbuf_tensor(name, shape, dt))

        w_in = sb("w_in", [P, CT, 3 * C])
        b_in = sb("b_in", [P, 3 * CT])
        dw = sb("dw", [P, CT, 4])
        w_dbc = sb("w_dbc", [P, CT, 2 * (2 * S + 1)])
        b_dbc = sb("b_dbc", [1, 2 * (2 * S + 1)])
        a_log = sb("a_log", [P, HEADS * S])
        d_skip = sb("d_skip", [P, HEADS])
        mobius = sb("mobius", [P, HEADS, 4])
        w_out = sb("w_out", [P, CT, C])
        b_out = sb("b_out", [1, C])
        z = sb("z", [P, 2, N + NT])
        before = sb("before", [P, NT, N])
        iota = sb("iota_n", [P, N])
        ones = sb("ones_row1", [1, P])
        select = sb("select", [3 * QROWS, ROWS, P], BF16)

        xs = sb("xs", [P, CT, B, N + 2])
        res, gate, x_perm, y_scan = (k.ring_late[:, i * CT * TOK:(i + 1) * CT * TOK].rearrange("p (t n) -> p t n", t=CT)
                                     for i in range(4))
        conv = y_scan.rearrange("p t (b n) -> p t b n", b=B)
        xf = sb("xf", [P, CT, TOK])
        xf_t = sb("xf_t", [P, TT, C])
        mob = sb("mob", [P, HEADS, 4])
        det = sb("det", [P, 3, HEADS])
        cplx = sb("cplx", [P, 6, N + NT])
        score = sb("score", [P, HEADS, N + NT])
        less = sb("less", [P, HEADS, NT, N])
        rank = sb("rank", [P, HEADS, NT])
        order = sb("order", [P, HEADS, NT, N])
        order_t = sb("order_t", [P, HEADS, NT, N])
        tie = order_t
        dbc = sb("dbc", [P, TT, HEADS, 2 * S + 1])
        soft = sb("soft", [P, 6, TT, HEADS])
        a_neg = sb("a_neg", [P, HEADS * S])
        rows = sb("rows", [P, TT, HEADS, 3, QROWS])
        parts = sb("parts", [3 * QROWS, HEADS, TOK], BF16)
        rest = sb("rest", [3 * QROWS, TOK])
        middle = sb("middle", [3 * QROWS, TOK], BF16)
        dtb = sb("dtb", [P, DEEP, BANK])
        u = sb("u", [P, DEEP, BANK])
        state = sb("state", [P, DEEP, BANK])
        prod = sb("prod", [P, DEEP, BANK])
        y_t = xf_t
        y = x_perm
        silu_out = u

        s_w = sem("l1_weights_loaded")
        s_zero = sem("l1_zeroed")
        s_in = sem("in_proj")
        s_silu = sem("in_proj_silu")
        s_gate = sem("gate_silu")
        s_cv = sem("depthwise_steps")
        s_xf = sem("xf_ready")
        s_xt = sem("xf_transposed")
        s_xto = sem("xf_t_out")
        s_mob = sem("mobius_steps")
        s_det = sem("mobius_root")
        s_rank = sem("rank_steps")
        s_ord = sem("order_ready")
        s_ot = sem("order_transposed")
        s_oto = sem("order_t_out")
        s_dbc = sem("dbc_product")
        s_so = sem("softplus_dve")
        s_sa = sem("softplus_act")
        s_rows = sem("rows_ready")
        s_rp = sem("rows_permuted")
        s_hi = sem("high_part")
        s_rest = sem("rest_of_parts")
        s_mid = sem("middle_part")
        s_parts = sem("parts_ready")
        s_xp = sem("x_permuted")
        s_xpo = sem("x_perm_out")
        s_bdt = sem("dt_b_spread")
        s_bda = sem("decay_spread")
        s_bc = sem("c_spread")
        s_dtb = sem("dtb_out")
        s_u = sem("scan_input")
        s_scan = sem("scanned")
        s_cm = sem("times_c")
        s_acc = sem("summed_over_states")
        s_ys = sem("y_scan_out")
        s_yt = sem("y_transposed")
        s_yto = sem("y_t_out")
        s_un = sem("y_unpermuted")
        s_y = sem("gating_steps")
        s_op = sem("out_proj")
        s_so2 = sem("out_proj_silu")
        s_t = sem("tokens_ready")

        PAIRS = HEADS * B // 2
        STEPS = PAIRS * S
        block = ctx.enter_context(nc.Block())
        DT, AB, EX, U1, LN, TMP = range(6)

        @block.sync
        def _(sp):
            for dst, src in ((w_in, k.dram["w_in"]), (b_in, k.dram["b_in"]), (mobius, k.dram["mobius"]), (z, k.dram["z"]), (before, k.dram["before"]),
                             (iota, k.dram["iota_n"]), (dw, k.dram["dw"]), (w_dbc, k.dram["w_dbc"]), (b_dbc, k.dram["b_dbc"]), (a_log, k.dram["a_log"]),
                             (d_skip, k.dram["d_skip"]), (w_out, k.dram["w_out"]), (b_out, k.dram["b_out"]), (ones, k.dram["ones"]),
                             (select, k.dram["select"])):
                sp.dma_start(dst[:], src).then_inc(s_w, 16)

        LOADED = 16 * 15

        @block.gpsimd
        def _(pool):
            pool.memset(xs[:, :, :, 0:1], 0.0).then_inc(s_zero, 1)
            pool.memset(xs[:, :, :, N + 1:N + 2], 0.0).then_inc(s_zero, 1)
            pool.memset(rows[:], 0.0).then_inc(s_zero, 1)
            for h in range(HEADS):
                pool.wait_ge(s_parts, h + 1)
                pool.wait_ge(s_mid, 2 * (h + 1))
                for q in range(3):
                    last = pool.memset(parts[QROWS * q:QROWS * q + S, h, :].rearrange("p (b n) -> p b n", b=B)[:, :, 0:1], 0.0)
                last.then_inc(s_zero, 1)
            for i in range(STEPS):
                h, half = i // S // 2, i // S % 2
                if i % (2 * S) == 0:
                    pool.wait_ge(s_xpo, h + 1)
                pool.wait_ge(s_dtb, i + 1)
                if i >= DEEP:
                    pool.wait_ge(s_scan, i - DEEP + 1)
                pool.tensor_tensor(u[:, i % DEEP, :], dtb[:, i % DEEP, :], x_perm[:, h, BANK * half:BANK * half + BANK],
                                   ALU.mult).then_inc(s_u, 1)

        @block.vector
        def _(dve):
            dve.wait_ge(s_w, LOADED)
            n = 0

            def step(ins):
                nonlocal n
                n += 1
                ins.then_inc(s_mob, 1)
                dve.wait_ge(s_mob, n)

            step(dve.tensor_tensor(det[:, 0, :], mobius[:, :, 0], mobius[:, :, 3], ALU.mult))
            step(dve.tensor_tensor(det[:, 1, :], mobius[:, :, 1], mobius[:, :, 2], ALU.mult))
            step(dve.tensor_tensor(det[:, 2, :], det[:, 0, :], det[:, 1, :], ALU.subtract))
            dve.wait_ge(s_det, 1)
            step(dve.tensor_scalar(det[:, 0, :], det[:, 0, :], 0.001, None, ALU.max))
            dve.wait_ge(s_det, 2)
            step(dve.reciprocal(det[:, 2, :], det[:, 1, :]))
            step(dve.tensor_tensor(mob[:], mobius[:], det[:, 2, :].unsqueeze(2).broadcast_to([P, HEADS, 4]), ALU.mult))
            step(dve.tensor_scalar(det[:, 0, :], mob[:, :, 3], 1e-6, None, ALU.add))
            for h in range(HEADS):
                a, bb, c, dd = mob[:, h, 0:1], mob[:, h, 1:2], mob[:, h, 2:3], det[:, 0, h:h + 1]
                NR, NI, DR, DI, RE, IM = (cplx[:, i, :] for i in range(6))
                step(dve.tensor_scalar(NR, z[:, 0, :], a, bb, ALU.mult, ALU.add))
                step(dve.tensor_scalar(NI, z[:, 1, :], a, None, ALU.mult))
                step(dve.tensor_scalar(DR, z[:, 0, :], c, dd, ALU.mult, ALU.add))
                step(dve.tensor_scalar(DI, z[:, 1, :], c, None, ALU.mult))
                step(dve.tensor_tensor(RE, NR, DR, ALU.mult))
                step(dve.tensor_tensor(IM, NI, DI, ALU.mult))
                step(dve.tensor_tensor(RE, RE, IM, ALU.add))
                step(dve.tensor_tensor(NI, NI, DR, ALU.mult))
                step(dve.tensor_tensor(NR, NR, DI, ALU.mult))
                step(dve.tensor_tensor(IM, NI, NR, ALU.subtract))
                step(dve.scalar_tensor_tensor(RE, IM, 1.3, RE, ALU.mult, ALU.add))
                step(dve.tensor_tensor(DR, DR, DR, ALU.mult))
                step(dve.tensor_tensor(DI, DI, DI, ALU.mult))
                step(dve.tensor_tensor(DR, DR, DI, ALU.add))
                step(dve.reciprocal(DI, DR))
                step(dve.tensor_tensor(score[:, h, :], RE, DI, ALU.mult))
            for h in range(HEADS):
                for t in range(NT):
                    own = score[:, h, N + t:N + t + 1]
                    dve.tensor_scalar(less[:, h, t, :], score[:, h, 0:N], own, None, ALU.is_lt).then_inc(s_rank, 1)
                    dve.scalar_tensor_tensor(tie[:, h, t, :], score[:, h, 0:N], own, before[:, t, :],
                                             ALU.is_equal, ALU.mult).then_inc(s_rank, 1)
            dve.wait_ge(s_rank, 2 * HEADS * NT)
            flat = "p h t n -> p (h t) n"
            dve.tensor_tensor(less[:].rearrange(flat), less[:].rearrange(flat), tie[:].rearrange(flat),
                              ALU.add).then_inc(s_rank, 1)
            dve.wait_ge(s_rank, 2 * HEADS * NT + 1)
            dve.tensor_reduce(rank[:].rearrange("p h t -> p (h t)"), less[:].rearrange(flat), AX_X, ALU.add).then_inc(s_rank, 1)
            dve.wait_ge(s_rank, 2 * HEADS * NT + 2)
            for h in range(HEADS):
                for t in range(NT):
                    dve.tensor_scalar(order[:, h, t, :], iota[:], rank[:, h, t:t + 1], None,
                                      ALU.is_equal).then_inc(s_ord, 1)
            for t in range(CT):
                dve.wait_ge(s_silu, t + 1)
                dve.wait_ge(s_zero, 2)
                dve.tensor_scalar(conv[:, t], xs[:, t, :, 0:N], dw[:, t, 0:1], dw[:, t, 3:4], ALU.mult, ALU.add).then_inc(s_cv, 1)
                dve.wait_ge(s_cv, 3 * t + 1)
                dve.scalar_tensor_tensor(conv[:, t], xs[:, t, :, 1:N + 1], dw[:, t, 1:2], conv[:, t],
                                         ALU.mult, ALU.add).then_inc(s_cv, 1)
                dve.wait_ge(s_cv, 3 * t + 2)
                dve.scalar_tensor_tensor(conv[:, t], xs[:, t, :, 2:N + 2], dw[:, t, 2:3], conv[:, t],
                                         ALU.mult, ALU.add).then_inc(s_cv, 1)
            for h in range(HEADS):
                dve.wait_ge(s_ot, h + 1)
                dve.tensor_copy(order_t[:, h].rearrange("p t n -> p (t n)"), psum[:, 4 + h, :]).then_inc(s_oto, 1)
            dve.wait_ge(s_dbc, 1)
            flat_dbc = dbc[:].rearrange("p t h j -> p (t h j)")
            dve.tensor_copy(flat_dbc, psum[:, 6, 0:TT * HEADS * (2 * S + 1)]).then_inc(s_so, 1)
            dve.wait_ge(s_so, 1)
            dve.wait_ge(s_sa, 2)
            dve.tensor_scalar(soft[:, U1], soft[:, EX], 1.0, None, ALU.add).then_inc(s_so, 1)
            dve.wait_ge(s_sa, 3)
            dve.tensor_scalar(soft[:, U1], soft[:, U1], 1.0, None, ALU.subtract).then_inc(s_so, 1)
            dve.tensor_tensor(soft[:, LN], soft[:, LN], soft[:, EX], ALU.mult).then_inc(s_so, 1)
            dve.wait_ge(s_so, 4)
            dve.tensor_scalar(soft[:, AB], soft[:, U1], 1e-30, None, ALU.max).then_inc(s_so, 1)
            dve.wait_ge(s_so, 5)
            dve.reciprocal(soft[:, TMP], soft[:, AB]).then_inc(s_so, 1)
            dve.wait_ge(s_so, 6)
            dve.tensor_tensor(soft[:, LN], soft[:, LN], soft[:, TMP], ALU.mult).then_inc(s_so, 1)
            dve.scalar_tensor_tensor(soft[:, EX], soft[:, U1], 0.0, soft[:, EX], ALU.is_equal, ALU.mult).then_inc(s_so, 1)
            dve.wait_ge(s_so, 8)
            dve.tensor_tensor(soft[:, LN], soft[:, LN], soft[:, EX], ALU.add).then_inc(s_so, 1)
            dve.wait_ge(s_so, 9)
            dve.scalar_tensor_tensor(soft[:, DT], dbc[:, :, :, 0], 0.0, soft[:, LN], ALU.max, ALU.add).then_inc(s_so, 1)
            dve.wait_ge(s_so, 10)
            dve.wait_ge(s_sa, 4)
            dve.wait_ge(s_zero, 3)
            dt_wide = soft[:, DT].unsqueeze(3).broadcast_to([P, TT, HEADS, S])
            dve.tensor_tensor(rows[:, :, :, 0, 0:S], dt_wide,
                              a_neg[:].rearrange("p (h s) -> p h s", h=HEADS).unsqueeze(1).broadcast_to([P, TT, HEADS, S]),
                              ALU.mult).then_inc(s_rows, 1)
            dve.tensor_tensor(rows[:, :, :, 0, S:2 * S], dt_wide, dbc[:, :, :, 1:1 + S], ALU.mult).then_inc(s_rows, 1)
            dve.tensor_copy(rows[:, :, :, 0, 2 * S:3 * S], dbc[:, :, :, 1 + S:]).then_inc(s_rows, 1)
            dve.wait_ge(s_sa, 5)
            dve.wait_ge(s_rows, 3)
            for q in (1, 2):
                for h in range(HEADS):
                    dve.tensor_copy(rows[:, :, h, q, 0:ROWS], rows[:, :, h, 0, 0:ROWS]).then_inc(s_rows, 1)
            for h in range(HEADS):
                dve.wait_ge(s_hi, h + 1)
                if h:
                    dve.wait_ge(s_mid, 2)
                    dve.wait_ge(s_parts, 1)
                permuted = psum[0:3 * QROWS, 2 * h:2 * h + 2, :].rearrange("p a n -> p (a n)")
                dve.tensor_tensor(rest[:], permuted, parts[:, h, :], ALU.subtract).then_inc(s_rest, 1)
                dve.wait_ge(s_mid, 2 * h + 2)
                dve.tensor_tensor(parts[2 * QROWS:3 * QROWS, h, :], rest[2 * QROWS:3 * QROWS], middle[2 * QROWS:3 * QROWS],
                                  ALU.subtract).then_inc(s_parts, 1)
            def times_c(i):
                dve.wait_ge(s_scan, i + 1)
                dve.wait_ge(s_bc, i + 1)
                if i >= DEEP:
                    dve.wait_ge(s_acc, i - DEEP + 1)
                dve.tensor_tensor(prod[:, i % DEEP, :], state[:, i % DEEP, :], psum[:, 4 + i % 2, :], ALU.mult).then_inc(s_cm, 1)

            for i in range(STEPS):
                dve.wait_ge(s_bda, i + 1)
                dve.wait_ge(s_u, i + 1)
                if i >= DEEP:
                    dve.wait_ge(s_cm, i - DEEP + 1)
                dve.tensor_tensor_scan(state[:, i % DEEP, :], psum[:, i % 2, :], u[:, i % DEEP, :], 0.0,
                                       ALU.mult, ALU.add).then_inc(s_scan, 1)
                if i >= 1:
                    times_c(i - 1)
            times_c(STEPS - 1)
            dve.wait_ge(s_silu, 3 * CT)
            dve.wait_ge(s_gate, CT)
            for h in range(HEADS):
                for half in range(2):
                    i = 2 * h + half
                    cols = slice(BANK * half, BANK * half + BANK)
                    dve.wait_ge(s_un, i + 1)
                    dve.scalar_tensor_tensor(y[:, h, cols], xf[:, h, cols], d_skip[:, h:h + 1], psum[:, 4 + i, :],
                                             ALU.mult, ALU.add).then_inc(s_y, 1)
                    dve.wait_ge(s_y, 3 * i + 1)
                    dve.tensor_tensor(y[:, h, cols], y[:, h, cols], gate[:, h, cols], ALU.mult).then_inc(s_y, 1)
                    dve.wait_ge(s_y, 3 * i + 2)
                    dve.tensor_tensor(y[:, h, cols], y[:, h, cols], res[:, h, cols], ALU.add).then_inc(s_y, 1)
            for i in range(TT // 2):
                dve.wait_ge(s_so2, i + 1)
                dve.tensor_tensor(k.t[:, 2 * i:2 * i + 2, :].rearrange("p a n -> p (a n)"), silu_out[:, i % 2, :],
                                  psum[:, 2 + i % 2, :], ALU.add).then_inc(s_t, 1)

        def scanned(act, pair):
            h, half = pair // 2, pair % 2
            act.wait_ge(s_acc, S * (pair + 1))
            act.activation(y_scan[:, h, BANK * half:BANK * half + BANK], psum[:, 6 + pair % 2, :],
                           ACT.Copy).then_inc(s_ys, 1)

        @block.scalar
        def _(act):
            act.wait_ge(s_w, LOADED)
            act.wait_ge(s_mob, 3)
            act.activation(det[:, 0, :], det[:, 2, :], ACT.Abs).then_inc(s_det, 1)
            act.wait_ge(s_mob, 4)
            act.activation(det[:, 1, :], det[:, 0, :], ACT.Sqrt).then_inc(s_det, 1)
            for i in range(3 * CT):
                act.wait_ge(s_in, i + 1)
                source = psum[:, 2 * (i % 2):2 * (i % 2) + 2, :].rearrange("p a n -> p (a n)")
                if i < CT:
                    target = xs[:, i, :, 1:N + 1]
                    source = source.rearrange("p (b n) -> p b n", b=B)
                    act.wait_ge(s_zero, 2)
                else:
                    target = (res if i < 2 * CT else gate)[:, i % CT, :]
                act.activation(target, source, ACT.Silu, bias=b_in[:, i:i + 1]).then_inc(s_silu, 1)
                if CT <= i < 2 * CT:
                    act.wait_ge(s_cv, 3 * (i - CT + 1))
                    act.activation(xf[:, i - CT, :], conv[:, i - CT].rearrange("p b n -> p (b n)"), ACT.Silu).then_inc(s_xf, 1)
            act.wait_ge(s_silu, 3 * CT)
            for i in range(CT):
                act.activation(gate[:, i, :], gate[:, i, :], ACT.Silu).then_inc(s_gate, 1)
            for i in range(TT // 2):
                act.wait_ge(s_xt, i + 1)
                act.activation(xf_t[:, 2 * i:2 * i + 2, :].rearrange("p a n -> p (a n)"), psum[:, i, :], ACT.Copy).then_inc(s_xto, 1)
            act.wait_ge(s_so, 1)
            act.activation(soft[:, AB], dbc[:, :, :, 0], ACT.Abs).then_inc(s_sa, 1)
            act.wait_ge(s_sa, 1)
            act.activation(soft[:, EX], soft[:, AB], ACT.Exp, scale=-1.0).then_inc(s_sa, 1)
            act.wait_ge(s_so, 2)
            act.activation(soft[:, LN], soft[:, U1], ACT.Ln).then_inc(s_sa, 1)
            act.activation(a_neg[:], a_log[:], ACT.Exp).then_inc(s_sa, 1)
            act.wait_ge(s_rows, 1)
            act.activation(rows[:, :, :, 0, 0:S], rows[:, :, :, 0, 0:S], ACT.Exp, scale=-1.0).then_inc(s_sa, 1)
            for h in range(HEADS):
                act.wait_ge(s_rp, h + 1)
                act.activation(parts[:, h, :], psum[0:3 * QROWS, 2 * h:2 * h + 2, :].rearrange("p a n -> p (a n)"),
                               ACT.Copy).then_inc(s_hi, 1)
                act.wait_ge(s_rest, h + 1)
                act.activation(parts[QROWS:2 * QROWS, h, :], rest[QROWS:2 * QROWS], ACT.Copy).then_inc(s_mid, 1)
                act.activation(middle[2 * QROWS:3 * QROWS], rest[2 * QROWS:3 * QROWS], ACT.Copy).then_inc(s_mid, 1)
                act.wait_ge(s_xp, h + 1)
                act.activation(x_perm[:, h, :], psum[:, 4 + 2 * h:6 + 2 * h, :].rearrange("p a n -> p (a n)"),
                               ACT.Copy).then_inc(s_xpo, 1)
            for i in range(STEPS):
                act.wait_ge(s_bdt, i + 1)
                if i >= DEEP:
                    act.wait_ge(s_u, i - DEEP + 1)
                act.activation(dtb[:, i % DEEP, :], psum[:, 2 + i % 2, :], ACT.Copy).then_inc(s_dtb, 1)
                if i % S == 4 and i > S:
                    scanned(act, i // S - 1)
            scanned(act, PAIRS - 1)
            for i in range(TT // 2):
                act.wait_ge(s_yt, i + 1)
                act.activation(y_t[:, 2 * i:2 * i + 2, :].rearrange("p a n -> p (a n)"), psum[:, i, :], ACT.Copy).then_inc(s_yto, 1)
            for i in range(TT // 2):
                act.wait_ge(s_op, i + 1)
                if i >= 2:
                    act.wait_ge(s_t, i - 1)
                act.activation(silu_out[:, i % 2, :], psum[:, i % 2, :], ACT.Silu).then_inc(s_so2, 1)

        @block.tensor
        def _(pe):
            pe.wait_ge(s_w, LOADED)
            for i in range(3 * CT):
                if i >= 2:
                    pe.wait_ge(s_silu, i - 1)
                for half in range(2):
                    for t in range(CT):
                        last = pe.matmul(psum[:, 2 * (i % 2) + half, :], w_in[:, t, P * i:P * i + P],
                                         k.h[:, t, 2 * half:2 * half + 2, :].rearrange("p b n -> p (b n)"),
                                         start=(t == 0), stop=(t == CT - 1))
                last.then_inc(s_in, 1)
            pe.wait_ge(s_ord, HEADS * NT)
            for h in range(HEADS):
                for r in range(NT):
                    for t in range(NT):
                        last = pe.transpose(psum[:, 4 + h, N * r + P * t:N * r + P * t + P],
                                            order[:, h, t, P * r:P * r + P], k.ident_sb[:])
                last.then_inc(s_ot, 1)
            pe.wait_ge(s_xf, CT)
            W = HEADS * (2 * S + 1)
            for T in range(TT):
                out = psum[:, 6, W * T:W * T + W]
                for t in range(CT):
                    pe.matmul(out, xf[:, t, P * T:P * T + P], w_dbc[:, t, :], start=(t == 0), stop=False)
                last = pe.matmul(out, ones[:], b_dbc[:], start=False, stop=True)
            last.then_inc(s_dbc, 1)
            pe.wait_ge(s_silu, 3 * CT)
            for i in range(TT // 2):
                for a in range(2):
                    for t in range(CT):
                        last = pe.transpose(psum[:, i, C * a + P * t:C * a + P * t + P],
                                            xf[:, t, P * (2 * i + a):P * (2 * i + a) + P], k.ident_sb[:])
                last.then_inc(s_xt, 1)
            pe.wait_ge(s_rows, 3 + 2 * HEADS)
            pe.wait_ge(s_xto, TT // 2)
            pe.wait_ge(s_oto, HEADS)
            pe.wait_ge(s_so, 1)
            for h in range(HEADS):
                for b in range(B):
                    for t in range(NT):
                        last = pe.matmul(psum[0:3 * QROWS, 2 * h + b // 2, N * (b % 2):N * (b % 2) + N],
                                         rows[:, NT * b + t, h].rearrange("p q j -> p (q j)"), order[:, h, t, :],
                                         start=(t == 0), stop=(t == NT - 1))
                last.then_inc(s_rp, 1)
                for b in range(B):
                    for t in range(NT):
                        last = pe.matmul(psum[:, 4 + 2 * h + b // 2, N * (b % 2):N * (b % 2) + N],
                                         xf_t[:, NT * b + t, P * h:P * h + P], order[:, h, t, :],
                                         start=(t == 0), stop=(t == NT - 1))
                last.then_inc(s_xp, 1)
            pe.wait_ge(s_zero, 3 + HEADS)
            pe.wait_ge(s_xpo, HEADS)
            pe.wait_ge(s_parts, HEADS)

            def sum_states(i):
                pair, s = i // S, i % S
                pe.wait_ge(s_cm, i + 1)
                if pair >= 2 and s == 0:
                    pe.wait_ge(s_ys, pair - 1)
                pe.matmul(psum[:, 6 + pair % 2, :], k.ident_sb[:], prod[:, i % DEEP, :],
                          start=(s == 0), stop=(s == S - 1)).then_inc(s_acc, 1)

            def spread(i, row, bank, done):
                h, half = i // S // 2, i // S % 2
                pe.matmul(psum[:, bank + i % 2, :], select[:, row * S + i % S, :],
                          parts[:, h, BANK * half:BANK * half + BANK], start=True, stop=True).then_inc(done, 1)

            spread(0, 1, 2, s_bdt)
            spread(1, 1, 2, s_bdt)
            spread(0, 0, 0, s_bda)
            for i in range(STEPS):
                if i + 2 < STEPS:
                    pe.wait_ge(s_dtb, i + 1)
                    spread(i + 2, 1, 2, s_bdt)
                if i + 1 < STEPS:
                    if i >= 1:
                        pe.wait_ge(s_scan, i)
                    spread(i + 1, 0, 0, s_bda)
                if i >= 2:
                    pe.wait_ge(s_cm, i - 1)
                spread(i, 2, 4, s_bc)
                if i >= 2:
                    sum_states(i - 2)
            sum_states(STEPS - 2)
            sum_states(STEPS - 1)
            pe.wait_ge(s_ys, PAIRS)
            for i in range(TT // 2):
                for a in range(2):
                    for h in range(HEADS):
                        last = pe.transpose(psum[:, i, C * a + P * h:C * a + P * h + P],
                                            y_scan[:, h, P * (2 * i + a):P * (2 * i + a) + P], k.ident_sb[:])
                last.then_inc(s_yt, 1)
            pe.wait_ge(s_yto, TT // 2)
            for h in range(HEADS):
                for half in range(2):
                    for b in range(2 * half, 2 * half + 2):
                        for t in range(NT):
                            last = pe.matmul(psum[:, 4 + 2 * h + half, N * (b % 2):N * (b % 2) + N],
                                             y_t[:, NT * b + t, P * h:P * h + P], order_t[:, h, t, :],
                                             start=(t == 0), stop=(t == NT - 1))
                    last.then_inc(s_un, 1)
            for i in range(TT // 2):
                pe.wait_ge(s_y, 3 * 2 * HEADS)
                if i >= 2:
                    pe.wait_ge(s_so2, i - 1)
                    pe.wait_ge(s_t, i - 1)
                for a in range(2):
                    T = 2 * i + a
                    for t in range(CT):
                        pe.matmul(psum[:, i % 2, C * a:C * a + C], y[:, t, P * T:P * T + P], w_out[:, t, :],
                                  start=(t == 0), stop=False)
                    pe.matmul(psum[:, i % 2, C * a:C * a + C], ones[:], b_out[:], start=False, stop=True)
                    for t in range(CT):
                        last = pe.transpose(psum[:, 2 + i % 2, C * a + P * t:C * a + P * t + P],
                                            k.x1[:, t].rearrange("p b n -> p (b n)")[:, P * T:P * T + P], k.ident_sb[:])
                last.then_inc(s_op, 1)


class LayerNorm:

    def __init__(self, name, sb, sem, eps):
        self.eps = eps
        self.raw = sb(f"{name}_raw", [P, TT, 6])
        self.moments = sb(f"{name}_moments", [P, TT, 2])
        self.var = sb(f"{name}_var", [P, TT])
        self.sd = sb(f"{name}_sd", [P, TT])
        self.rstd = sb(f"{name}_rstd", [P, TT])
        self.s_raw = sem(f"{name}_raw")
        self.s_moments = sem(f"{name}_moments")
        self.s_sd = sem(f"{name}_sd")
        self.s_rstd = sem(f"{name}_rstd")
        self.s_out = sem(f"{name}_out")

    def statistics(self, dve, t):
        for T in range(TT):
            dve.bn_stats(self.raw[:, T, :], t[:, T, :]).then_inc(self.s_raw, 1)
        for T in range(TT):
            dve.wait_ge(self.s_raw, T + 1)
            last = dve.bn_aggr(self.moments[:, T, :], self.raw[:, T, :])
        last.then_inc(self.s_moments, 1)
        dve.wait_ge(self.s_moments, 1)
        dve.tensor_scalar(self.var[:], self.moments[:, :, 1], self.eps, None, ALU.add).then_inc(self.s_moments, 1)

    def deviation(self, act):
        act.wait_ge(self.s_moments, 2)
        act.activation(self.sd[:], self.var[:], ACT.Sqrt).then_inc(self.s_sd, 1)

    def normalise(self, dve, t, out):
        dve.wait_ge(self.s_sd, 1)
        dve.reciprocal(self.rstd[:], self.sd[:]).then_inc(self.s_rstd, 1)
        dve.wait_ge(self.s_rstd, 1)
        for T in range(TT):
            dve.tensor_scalar(out[:, T, :], t[:, T, :], self.moments[:, T, 0:1], self.rstd[:, T:T + 1],
                              ALU.subtract, ALU.mult).then_inc(self.s_out, 1)


COMBOS = ((0, 0), (0, 1), (1, 0), (1, 1), (0, 2), (2, 0))
STACK = len(COMBOS) * HD
MAXROWS = 2


def attention(nc, sem, sbuf, psum, k, w, causal, tag, prefetch=None):
    with ExitStack() as ctx:
        def sb(name, shape, dt=F32):
            return ctx.enter_context(nc.sbuf_tensor(f"{tag}_{name}", shape, dt))

        def sm(name):
            return sem(f"{tag}_{name}")

        wqkv = sb("wqkv", [P, CT, 3 * C])
        w_proj = sb("w_proj", [P, AH // 4, C])
        b_proj = sb("b_proj", [1, C])
        ones = sb("ones_row", [1, P])
        ident16 = sb("ident16", [P, P], BF16)
        bans = sb("bans", [P, 3, P], BF16)
        h_t = k.x1[:].rearrange("p t b n -> p t (b n)")
        normed = k.h[:].rearrange("p t b n -> p (t b n)").rearrange("p (t c) -> p t c", c=C)
        rest = sb("rest", [P, 2, TOK])
        parts = sb("parts", [P, 2, 3, CT, TOK], BF16)
        stack_q = sb("stack_q", [STACK + MAXROWS, 2, AH, N], BF16)
        stack_k = sb("stack_k", [STACK + MAXROWS, 2, AH, N], BF16)
        values = sb("values", [P, TT, AH, 2 * HD])
        maxima = sb("maxima", [P, B, NT, AH])
        negated = sb("negated", [AH, B, MAXROWS, N], BF16)
        expo = sb("expo", [P, 2, 2, BANK])
        sums = sb("sums", [P, 2, 2 * N])
        ctxn = rest[:].rearrange("p b (g n) -> p b g n", n=N)
        ln = LayerNorm(f"{tag}_ln", sb, sem, 1e-5)

        s_w = sm("weights_loaded")
        s_ones = sm("constants_set")
        s_ht = sm("h_transposed")
        s_hto = sm("h_t_out")
        s_qk = sm("qk_projected")
        s_hi = sm("high_part")
        s_r = sm("remainder")
        s_mid = sm("middle_part")
        s_lo = sm("low_part")
        s_v = sm("v_projected")
        s_vo = sm("v_out")
        s_pd = sm("parts_in_dram")
        s_st = [sm("stack_loaded_even"), sm("stack_loaded_odd")]
        s_sc = sm("scores_for_max")
        s_mx = sm("maxima")
        s_mt = sm("maxima_transposed")
        s_nh = sm("negated_high")
        s_nl = sm("negated_low")
        s_mr = [sm("max_rows_even"), sm("max_rows_odd")]
        s_s2 = sm("scores_less_max")
        s_ex = sm("exponentials")
        s_av = sm("values_weighted")
        s_sum = sm("sums_moved")
        s_rec = sm("sums_inverted")
        s_cn = sm("context_normalised")
        s_pj = sm("projected")
        s_res = sm("residual_added")

        READS = 2 * len(COMBOS)
        UNITS = AH // 2
        n1 = P if causal else 0
        WIDTH = 2 * N - n1
        block = ctx.enter_context(nc.Block())

        @block.sync
        def _(sp):
            for dst, src in ((wqkv, w["wqkv"]), (w_proj, w["w_proj"]), (b_proj, w["b_proj"]), (ones, k.dram["ones"]),
                             (ident16, k.dram["ident16"]), (bans, k.dram["bans"])):
                sp.dma_start(dst[:], src).then_inc(s_w, 16)
            if prefetch is not None:
                prefetch(sp)
            for i in range(2):
                for part, (done, count) in enumerate(((s_hi, 2), (s_mid, 2), (s_lo, 2))):
                    sp.wait_ge(done, count * (i + 1))
                    sp.dma_start(k.parts_dram[i, part].rearrange("(t p) n -> p t n", p=P),
                                 parts[:, i, part]).then_inc(s_pd, 16)
            sp.wait_ge(s_pd, 16 * 6)

            def load_stacks(b):
                for i, stack in enumerate((stack_q, stack_k)):
                    for g, combo in enumerate(COMBOS):
                        sp.dma_start(stack[HD * g:HD * g + HD, b % 2],
                                     k.parts_dram[i, combo[i]].rearrange("(h d) n -> d h n", d=HD)[:, :, N * b:N * b + N]
                                     ).then_inc(s_st[b % 2], 16)

            load_stacks(0)
            load_stacks(1)
            for b in range(B):
                sp.wait_ge(s_nl, b + 1)
                sp.wait_ge(s_nh, b + 1)
                for q in range(MAXROWS):
                    sp.dma_start(stack_q[STACK + q:STACK + q + 1, b % 2], negated[:, b, q, :]).then_inc(s_mr[b % 2], 16)
                if b >= 1 and b + 1 < B:
                    sp.wait_ge(s_s2, UNITS * b)
                    load_stacks(b + 1)

        @block.gpsimd
        def _(pool):
            pool.memset(values[:, :, :, HD:], 1.0).then_inc(s_ones, 1)
            pool.wait_ge(s_ones, 1)
            pool.memset(stack_k[STACK:, :, :, :], 1.0).then_inc(s_ones, 1)

        @block.vector
        def _(dve):
            ln.statistics(dve, k.t)
            ln.normalise(dve, k.t, normed)
            for i in range(TT // 2):
                dve.wait_ge(s_ht, i + 1)
                if i % 2:
                    dve.tensor_copy(h_t[:, :, N * i:N * i + N], psum[:, i, :].rearrange("p (t n) -> p t n", t=CT)).then_inc(s_hto, 1)
            for i in range(2 * CT):
                source = psum[:, 2 * (i % 2):2 * (i % 2) + 2, :].rearrange("p a n -> p (a n)")
                which, t = i // CT, i % CT
                dve.wait_ge(s_hi, i + 1)
                dve.tensor_tensor(rest[:, i % 2, :], source, parts[:, which, 0, t, :], ALU.subtract).then_inc(s_r, 1)
                dve.wait_ge(s_mid, i + 1)
                dve.tensor_tensor(parts[:, which, 2, t, :], rest[:, i % 2, :], parts[:, which, 1, t, :],
                                  ALU.subtract).then_inc(s_lo, 1)
            for i in range(TT // 2):
                dve.wait_ge(s_v, i + 1)
                dve.tensor_copy(values[:, 2 * i:2 * i + 2, :, 0:HD],
                                psum[:, 4 + i % 2, :].rearrange("p (a h d) -> p a h d", a=2, h=AH)).then_inc(s_vo, 1)

            def take_max(i):
                b, h = i // AH, i % AH
                dve.wait_ge(s_sc, i + 1)
                dve.tensor_reduce(maxima[:, b, :, h], psum[:, i % 2, :].rearrange("p (t m) -> p t m", t=NT),
                                  AX_X, ALU.max).then_inc(s_mx, 1)

            def negate(b):
                dve.wait_ge(s_nh, b + 1)
                dve.scalar_tensor_tensor(negated[:, b, 1, :], psum[0:AH, 0, 0:N], -1.0, negated[:, b, 0, :],
                                         ALU.mult, ALU.subtract).then_inc(s_nl, 1)

            def normalise(i):
                b, half = i // 2, i % 2
                source = psum[:, 6 + half, :]
                dve.wait_ge(s_av, UNITS // 2 * (i + 1))
                if i >= 2:
                    dve.wait_ge(s_cn, i - 1)
                dve.stream_shuffle(sums[:, half, :], source, [16 + j % 16 for j in range(32)]).then_inc(s_sum, 1)
                dve.wait_ge(s_sum, i + 1)
                dve.reciprocal(sums[:, half, :], sums[:, half, :]).then_inc(s_rec, 1)
                dve.wait_ge(s_rec, i + 1)
                if b >= 2 and half == 0:
                    dve.wait_ge(s_pj, b - 1)
                dve.tensor_tensor(ctxn[:, b % 2, 2 * half:2 * half + 2, :].rearrange("p g n -> p (g n)"), source,
                                  sums[:, half, :], ALU.mult).then_inc(s_cn, 1)

            def add_residual(b):
                dve.wait_ge(s_pj, b + 1)
                tile = k.t[:, NT * b:NT * b + NT, :].rearrange("p a n -> p (a n)")
                dve.tensor_tensor(tile, tile, psum[:, 6, :], ALU.add).then_inc(s_res, 1)

            for h in range(AH):
                take_max(h)
            negate(0)
            for b in range(B):
                for unit in range(UNITS):
                    if b + 1 < B:
                        take_max(AH * (b + 1) + 2 * unit)
                        take_max(AH * (b + 1) + 2 * unit + 1)
                    if unit == UNITS // 2:
                        normalise(2 * b)
                if b + 1 < B:
                    negate(b + 1)
                normalise(2 * b + 1)
                add_residual(b)

        @block.scalar
        def _(act):
            ln.deviation(act)
            for i in range(0, TT // 2, 2):
                act.wait_ge(s_ht, i + 1)
                act.activation(h_t[:, :, N * i:N * i + N], psum[:, i, :].rearrange("p (t n) -> p t n", t=CT),
                               ACT.Copy).then_inc(s_hto, 1)
            for i in range(2 * CT):
                source = psum[:, 2 * (i % 2):2 * (i % 2) + 2, :].rearrange("p a n -> p (a n)")
                which, t = i // CT, i % CT
                act.wait_ge(s_qk, i + 1)
                act.activation(parts[:, which, 0, t, :], source, ACT.Copy).then_inc(s_hi, 1)
                act.wait_ge(s_r, i + 1)
                act.activation(parts[:, which, 1, t, :], rest[:, i % 2, :], ACT.Copy).then_inc(s_mid, 1)

            def negate(b):
                act.wait_ge(s_mt, b + 1)
                act.activation(negated[:, b, 0, :], psum[0:AH, 0, 0:N], ACT.Copy, scale=-1.0).then_inc(s_nh, 1)

            negate(0)
            for b in range(B):
                for unit in range(UNITS):
                    i = UNITS * b + unit
                    act.wait_ge(s_s2, i + 1)
                    if i >= 2:
                        act.wait_ge(s_av, i - 1)
                    act.activation(expo[:, i % 2, :, 0:WIDTH], psum[:, 2 + 2 * (i % 2):4 + 2 * (i % 2), 0:WIDTH],
                                   ACT.Exp, scale=HD ** -0.5).then_inc(s_ex, 1)
                if b + 1 < B:
                    negate(b + 1)

        @block.tensor
        def _(pe):
            for i in range(TT // 2):
                pe.wait_ge(ln.s_out, 2 * i + 2)
                for t in range(CT):
                    for a in range(2):
                        last = pe.transpose(psum[:, i, N * t + P * a:N * t + P * a + P],
                                            normed[:, 2 * i + a, P * t:P * t + P], k.ident_sb[:])
                last.then_inc(s_ht, 1)
            pe.wait_ge(s_w, 16 * 6)
            pe.wait_ge(s_hto, TT // 2)
            for i in range(2 * CT):
                if i >= 2:
                    pe.wait_ge(s_r, i - 1)
                for half in range(2):
                    for t in range(CT):
                        last = pe.matmul(psum[:, 2 * (i % 2) + half, :], wqkv[:, t, P * i:P * i + P],
                                         h_t[:, t, BANK * half:BANK * half + BANK], start=(t == 0), stop=(t == CT - 1))
                last.then_inc(s_qk, 1)
            for i in range(TT // 2):
                if i >= 2:
                    pe.wait_ge(s_vo, i - 1)
                for a in range(2):
                    T = 2 * i + a
                    for t in range(CT):
                        last = pe.matmul(psum[:, 4 + i % 2, C * a:C * a + C], h_t[:, t, P * T:P * T + P],
                                         wqkv[:, t, 2 * C:], start=(t == 0), stop=(t == CT - 1))
                last.then_inc(s_v, 1)
            pe.wait_ge(s_ones, 2)
            pe.wait_ge(s_vo, TT // 2)

            def scores_for_max(i):
                b, h = i // AH, i % AH
                if h == 0:
                    pe.wait_ge(s_st[b % 2], 16 * READS * (b // 2 + 1))
                if i >= 2:
                    pe.wait_ge(s_mx, i - 1)
                if h == 0 and b >= 1:
                    pe.wait_ge(s_nl, b)
                for t in range(NT):
                    keys = P if causal and t == 0 else N
                    out = psum[:, i % 2, N * t:N * t + keys]
                    last = pe.matmul(out, stack_q[0:STACK, b % 2, h, P * t:P * t + P],
                                     stack_k[0:STACK, b % 2, h, 0:keys], start=True, stop=not causal)
                    if causal:
                        last = pe.matmul(psum[:, i % 2, N * t + P * t:N * t + P * t + P], ident16[:], bans[:, 0, :],
                                         start=False, stop=True)
                        if t == 0:
                            pe.matmul(psum[:, i % 2, P:N], ident16[:], bans[:, 2, :], start=True, stop=True)
                last.then_inc(s_sc, 1)

            def turn_maxima(b):
                pe.wait_ge(s_mx, AH * (b + 1))
                for t in range(NT):
                    last = pe.transpose(psum[0:AH, 0, P * t:P * t + P], maxima[:, b, t, :], k.ident_sb[:])
                last.then_inc(s_mt, 1)

            def scores_less_max(i):
                b, unit = i // UNITS, i % UNITS
                if unit == 0:
                    pe.wait_ge(s_mr[b % 2], 16 * MAXROWS * (b // 2 + 1))
                if i >= 2:
                    pe.wait_ge(s_ex, i - 1)
                for j in range(2):
                    h, bank = 2 * unit + j, 2 + 2 * (i % 2) + j
                    for m in range(NT):
                        first = n1 if m else 0
                        col = N * m
                        last = pe.matmul(psum[:, bank, col:col + N - first],
                                         stack_k[:, b % 2, h, P * m:P * m + P], stack_q[:, b % 2, h, first:N],
                                         start=True, stop=not causal)
                        if causal:
                            last = pe.matmul(psum[:, bank, col:col + P], ident16[:], bans[:, 1, :], start=False, stop=True)
                last.then_inc(s_s2, 1)

            def weigh_values(i):
                b, unit = i // UNITS, i % UNITS
                pe.wait_ge(s_ex, i + 1)
                if unit == 0 and b >= 1:
                    pe.wait_ge(s_res, b)
                if unit == UNITS // 2 and b >= 1:
                    pe.wait_ge(s_cn, 2 * b)
                for j in range(2):
                    h = 2 * unit + j
                    q, g = 32 * (h % 4), h // 4
                    for m in range(NT):
                        first = n1 if m else 0
                        last = pe.matmul(psum[q:q + 32, 6 + g // 2, N * (g % 2) + first:N * (g % 2) + N],
                                         values[:, NT * b + m, h, :], expo[:, i % 2, j, N * m:N * m + N - first],
                                         start=(m == 0), stop=(m == NT - 1))
                last.then_inc(s_av, 1)

            def project(b):
                pe.wait_ge(s_cn, 2 * b + 2)
                for a in range(NT):
                    out = psum[:, 6, C * a:C * a + C]
                    for g in range(AH // 4):
                        pe.matmul(out, ctxn[:, b % 2, g, P * a:P * a + P], w_proj[:, g, :], start=(g == 0), stop=False)
                    last = pe.matmul(out, ones[:], b_proj[:], start=False, stop=True)
                last.then_inc(s_pj, 1)

            for h in range(AH):
                scores_for_max(h)
            turn_maxima(0)
            for b in range(B):
                for unit in range(UNITS):
                    i = UNITS * b + unit
                    scores_less_max(i)
                    if b + 1 < B:
                        scores_for_max(AH * (b + 1) + 2 * unit)
                        scores_for_max(AH * (b + 1) + 2 * unit + 1)
                    if unit:
                        weigh_values(i - 1)
                if b + 1 < B:
                    turn_maxima(b + 1)
                weigh_values(UNITS * (b + 1) - 1)
                project(b)


CHUNK = 512
CHUNK_COLS = 2 * CT * CHUNK + CHUNK // P * C
RING_CHUNKS = 6
PAIRED = (MAXBLK + 1) // 2 * 2


def above_zero(count):
    return not isinstance(count, int) or count > 0


def load_experts(sp, k, weights, chunks, experts, loaded):
    for e in experts:
        slot = e % (RING_CHUNKS // chunks) * chunks
        sp.dma_start(k.ring[:, CHUNK_COLS * slot:CHUNK_COLS * (slot + chunks)], weights[e]).then_inc(loaded, 16)


def experts_ffn(nc, sem, sbuf, psum, k, w, chunks, preloaded, s_loaded, tag, finish=None):
    RING_EXPERTS = RING_CHUNKS // chunks
    with ExitStack() as ctx:
        def sb(name, shape, dt=F32):
            return ctx.enter_context(nc.sbuf_tensor(f"{tag}_{name}", shape, dt))

        def sm(name):
            return sem(f"{tag}_{name}")

        gate_w = sb("gate_w", [P, CT, E])
        iota_e = sb("iota_e", [P, E])
        iota_b = sb("iota_b", [P, PAIRED])
        steps = sb("steps", [P, TT])
        earlier = sb("earlier", [P, 2, P], BF16)
        h_t = k.x1[:].rearrange("p t b n -> p t (b n)")
        normed = k.h[:].rearrange("p t b n -> p (t b n)").rearrange("p (t c) -> p t c", c=C)
        logits = sb("logits", [P, TT, E])
        top = sb("top", [P, TT, E])
        top_at = sb("top_at", [P, TT, E], U32)
        choice = sb("choice", [P, TT, 2])
        chosen = sb("chosen", [P, 2, TT, E])
        either = sb("either", [P, TT, E], BF16)
        share = sb("share", [P, 4, TT])
        count = sb("count", [P, E])
        over = sb("over", [P, E, TT])
        blocks = sb("blocks", [P, E])
        block_end = sb("block_end", [P, E])
        unit = sb("unit", [P, E])
        base = sb("base", [P, E])
        place = sb("place", [P, TT, E])
        taken = sb("taken", [P, 2, TT, E])
        slot = sb("slot", [P, 2, TT])
        slot_at = sb("slot_at", [P, 2, TT], U32)
        past = sb("past", [P, PAIRED, E])
        expert = sb("expert", [P, 3, PAIRED])
        table = sb("table", [P, 2, PAIRED], I32)
        free_at = sb("free_at", [P, E], I32)
        xs = sb("xs", [P, 2, C])
        x_t = sb("x_t", [P, 2, CT, P])
        silu = sb("silu", [P, 2, CHUNK])
        gated = sb("gated", [P, 2, CHUNK])
        gated_t = sb("gated_t", [P, 2, CHUNK])
        y = sb("y", [P, 2, C])
        got = sb("got", [P, 4, 2, C])
        ln = LayerNorm(f"{tag}_ln", sb, sem, 1e-5)

        s_w = sm("weights_loaded")
        s_ht = sm("h_transposed")
        s_hto = sm("h_t_out")
        s_lg = sm("logits")
        s_r = sm("router_steps")
        s_exp = sm("router_exp")
        s_rank = sm("ranks_and_counts")
        s_slot = sm("slots_ready")
        s_table = sm("table_ready")
        s_sc = sm("rows_scattered")
        s_x = [sm("x_loaded_even"), sm("x_loaded_odd")]
        s_xt = sm("x_transposed")
        s_xto = sm("x_t_out")
        s_up = sm("up_products")
        s_si = sm("silu")
        s_g = sm("gated")
        s_gt = sm("gated_transposed")
        s_gto = sm("gated_t_out")
        s_dn = sm("down_products")
        s_y = sm("y_out")
        s_yd = [sm("y_stored_even"), sm("y_stored_odd")]
        s_got = [sm(f"results_gathered_{i}") for i in range(4)]
        s_t = sm("tokens_updated")
        s_ft = sm("final_transposed")
        s_fo = sm("final_out")
        s_st = sm("output_stored")

        X_BANK, Y_BANK, G_BANK = 7, 6, 4
        block = ctx.enter_context(nc.Block())
        PAIRS = (MAXBLK - 1) // 2
        assert MAXBLK % 2 == 1

        @block.sync
        def _(sp):
            for dst, src in ((gate_w, w["gate"]), (iota_e, k.dram["iota_e"]), (iota_b, k.dram["iota_b"]), (steps, k.dram["steps"]),
                             (earlier, k.dram["earlier"])):
                sp.dma_start(dst[:], src).then_inc(s_w, 16)
            load_experts(sp, k, w["experts"], chunks, range(preloaded, RING_EXPERTS), s_loaded)
            sp.wait_ge(s_table, 1)
            for e in range(RING_EXPERTS, E):
                done = sp.value_load(free_at[0:1, e - RING_EXPERTS:e - RING_EXPERTS + 1], min_val=1, max_val=MAXBLK)
                sp.wait_ge(s_loaded, 16 * e)
                sp.wait_ge(s_y, done)
                load_experts(sp, k, w["experts"], chunks, (e,), s_loaded)
            if finish is not None:
                for i in range(TT // 2):
                    sp.wait_ge(s_fo, i + 1)
                    sp.dma_start(finish[i], k.x1[:, :, i, :]).then_inc(s_st, 16)
                sp.wait_ge(s_st, 16 * TT // 2)

        @block.gpsimd
        def _(pool):
            pool.wait_ge(s_slot, 1)
            pool.wait_ge(k.s_cleared, 16)
            for T in range(TT):
                for c in range(2):
                    pool.indirect_dma_start(out=k.rows_in, out_offset=bass.IndirectOffsetOnAxis(ap=slot_at[:, c, T:T + 1], axis=0),
                                            in_=normed[:, T, :], in_offset=None).then_inc(s_sc, 16)
            pool.wait_ge(s_sc, 16 * 2 * TT)

            def load_x(j, odd, turned=None):
                if turned is not None:
                    pool.wait_ge(s_xt, turned)
                pool.dma_start(xs[:, odd, :], k.rows_in[bass.ds(j * P, P), :]).then_inc(s_x[odd], 16)

            def store_y(j, odd):
                pool.wait_ge(s_y, j + 1)
                pool.dma_start(k.rows_out[bass.ds(j * P, P), :], y[:, odd, :]).then_inc(s_yd[odd], 16)

            load_x(0, 0)
            load_x(1, 1)
            for j in (2, 3):
                load_x(j, j % 2, j - 1)

            def turn(i, more=True):
                for odd in (1, 0):
                    j = 2 * i + (1 if odd else 2)
                    if more:
                        load_x(j + 3, 1 - odd, j + 2)
                    store_y(j - 1, 1 - odd)

            turn(0)
            with pool.Fori(1, PAIRS - 1) as i:
                turn(i)
            turn(PAIRS - 1, more=False)
            store_y(MAXBLK - 1, 0)
            pool.wait_ge(s_y, MAXBLK)
            pool.wait_ge(s_yd[0], 16 * (MAXBLK + 1) // 2)
            pool.wait_ge(s_yd[1], 16 * (MAXBLK // 2))
            for T in range(TT):
                if T >= 4:
                    pool.wait_ge(s_t, 2 * (T - 3))
                for c in range(2):
                    pool.indirect_dma_start(out=got[:, T % 4, c, :], out_offset=None, in_=k.rows_out,
                                            in_offset=bass.IndirectOffsetOnAxis(ap=slot_at[:, c, T:T + 1], axis=0)).then_inc(s_got[T % 4], 16)

        @block.vector
        def _(dve):
            ln.statistics(dve, k.t)
            ln.normalise(dve, k.t, normed)
            for i in range(1, TT // 2, 2):
                dve.wait_ge(s_ht, i + 1)
                dve.tensor_copy(h_t[:, :, N * i:N * i + N], psum[:, i, :].rearrange("p (t n) -> p t n", t=CT)).then_inc(s_hto, 1)
            n = 0

            def step(ins):
                nonlocal n
                n += 1
                ins.then_inc(s_r, 1)
                dve.wait_ge(s_r, n)

            dve.wait_ge(s_lg, 1)
            step(dve.tensor_copy(logits[:].rearrange("p t e -> p (t e)"), psum[:, 4, 0:TT * E]))
            for T in range(TT):
                last = dve.max(top[:, T, :], logits[:, T, :])
            step(last)
            for T in range(TT):
                last = dve.max_index(top_at[:, T, :], top[:, T, :], logits[:, T, :])
            step(last)
            step(dve.tensor_tensor(share[:, 0, :], top[:, :, 1], top[:, :, 0], ALU.subtract))
            step(dve.tensor_copy(choice[:], top_at[:, :, 0:2]))
            every = [P, TT, E]
            for c in range(2):
                step(dve.tensor_tensor(chosen[:, c], iota_e[:].unsqueeze(1).broadcast_to(every),
                                       choice[:, :, c].unsqueeze(2).broadcast_to(every), ALU.is_equal))
            step(dve.tensor_tensor(either[:], chosen[:, 0], chosen[:, 1], ALU.add))
            dve.wait_ge(s_exp, 1)
            step(dve.tensor_scalar(share[:, 1, :], share[:, 0, :], 1.0, None, ALU.add))
            step(dve.reciprocal(share[:, 2, :], share[:, 1, :]))
            step(dve.tensor_tensor(share[:, 3, :], share[:, 0, :], share[:, 2, :], ALU.mult))
            dve.wait_ge(s_rank, 1)
            step(dve.tensor_copy(count[:], psum[:, 6, 0:E]))
            wide = [P, E, TT]
            step(dve.tensor_tensor(over[:], count[:].unsqueeze(2).broadcast_to(wide),
                                   steps[:].unsqueeze(1).broadcast_to(wide), ALU.is_gt))
            step(dve.tensor_reduce(blocks[:], over[:], AX_X, ALU.add))
            step(dve.tensor_scalar(blocks[:], blocks[:], 1.0, None, ALU.max))
            step(dve.memset(unit[:], 1.0))
            step(dve.tensor_tensor_scan(block_end[:], unit[:], blocks[:], 0.0, ALU.mult, ALU.add))
            step(dve.tensor_tensor(base[:], block_end[:], blocks[:], ALU.subtract))
            step(dve.tensor_scalar(base[:], base[:], float(P), None, ALU.mult))
            step(dve.tensor_tensor(place[:], psum[:, 5, 0:TT * E].rearrange("p (t e) -> p t e", t=TT),
                                   base[:].unsqueeze(1).broadcast_to(every), ALU.add))
            for c in range(2):
                step(dve.tensor_tensor(taken[:, c], place[:], chosen[:, c], ALU.mult))
            step(dve.tensor_reduce(slot[:].rearrange("p c t -> p (c t)"), taken[:].rearrange("p c t e -> p (c t) e"),
                                   AX_X, ALU.add))
            dve.tensor_copy(slot_at[:], slot[:]).then_inc(s_slot, 1)
            wide = [P, PAIRED, E]
            step(dve.tensor_tensor(past[:], block_end[:].unsqueeze(1).broadcast_to(wide),
                                   iota_b[:].unsqueeze(2).broadcast_to(wide), ALU.is_le))
            step(dve.tensor_reduce(expert[:, 0, :], past[:], AX_X, ALU.add))
            step(dve.tensor_scalar(expert[:, 0, :], expert[:, 0, :], float(E - 1), None, ALU.min))
            step(dve.tensor_scalar(expert[:, 1, :], expert[:, 0, :], float(RING_EXPERTS), float(-RING_EXPERTS),
                                   ALU.is_ge, ALU.mult))
            step(dve.tensor_tensor(expert[:, 1, :], expert[:, 0, :], expert[:, 1, :], ALU.add))
            for turn in range(2, (E - 1) // RING_EXPERTS + 1):
                step(dve.tensor_scalar(expert[:, 2, :], expert[:, 0, :], float(turn * RING_EXPERTS),
                                       float(-RING_EXPERTS), ALU.is_ge, ALU.mult))
                step(dve.tensor_tensor(expert[:, 1, :], expert[:, 1, :], expert[:, 2, :], ALU.add))
            step(dve.tensor_scalar(table[:, 0, :], expert[:, 1, :], float(chunks * CHUNK_COLS), None, ALU.mult))
            step(dve.tensor_scalar(expert[:, 2, :], expert[:, 0, :], 1.0, float(RING_EXPERTS), ALU.add, ALU.max))
            step(dve.tensor_scalar(table[:, 1, :], expert[:, 2, :], 16.0, None, ALU.mult))
            dve.tensor_copy(free_at[:], block_end[:]).then_inc(s_table, 1)

            def gate(q, b):
                dve.wait_ge(s_up, 2 * q + 2)
                dve.wait_ge(s_si, q + 1)
                dve.tensor_tensor(gated[:, b, :], silu[:, b, :], psum[:, 2 * b + 1, :], ALU.mult).then_inc(s_g, 1)

            def take_x(j, b):
                loads = dve.value_load(table[0:1, 1, bass.ds(j, 1)], min_val=16, max_val=16 * E)
                dve.wait_ge(s_loaded, loads)
                dve.wait_ge(s_xt, j + 1)
                dve.tensor_copy(x_t[:, b].rearrange("p t n -> p (t n)"), psum[:, X_BANK, 0:C]).then_inc(s_xto, 1)

            def take_y(j, b, stored):
                dve.wait_ge(s_dn, chunks * (j + 1))
                if above_zero(stored):
                    dve.wait_ge(s_yd[b], stored)
                dve.tensor_copy(y[:, b, :], psum[:, Y_BANK, 0:C]).then_inc(s_y, 1)

            dve.wait_ge(s_table, 1)
            take_x(0, 0)
            if chunks == 2:
                gate(0, 0)
            gate(chunks - 1, chunks - 1)
            take_x(1, 1)
            def turn(i):
                for odd in (1, 0):
                    j = 2 * i + (1 if odd else 2)
                    if chunks == 2:
                        gate(2 * j, 0)
                        take_y(j - 1, 1 - odd, 16 * i)
                        gate(2 * j + 1, 1)
                        take_x(j + 1, 1 - odd)
                    else:
                        gate(j, odd)
                        take_x(j + 1, 1 - odd)
                        take_y(j - 1, 1 - odd, 16 * i)

            turn(0)
            with dve.Fori(1, PAIRS) as i:
                turn(i)
            take_y(MAXBLK - 1, 0, 16 * PAIRS)
            for T in range(TT):
                for c in range(2):
                    dve.wait_ge(s_got[T % 4], 32 * (T // 4 + 1))
                    if c:
                        dve.wait_ge(s_t, 2 * T + 1)
                    dve.scalar_tensor_tensor(k.t[:, T, :], got[:, T % 4, c, :], share[:, 2 + c, T:T + 1], k.t[:, T, :],
                                             ALU.mult, ALU.add).then_inc(s_t, 1)

        @block.scalar
        def _(act):
            ln.deviation(act)
            for i in range(0, TT // 2, 2):
                act.wait_ge(s_ht, i + 1)
                act.activation(h_t[:, :, N * i:N * i + N], psum[:, i, :].rearrange("p (t n) -> p t n", t=CT),
                               ACT.Copy).then_inc(s_hto, 1)
            act.wait_ge(s_r, 4)
            act.activation(share[:, 0, :], share[:, 0, :], ACT.Exp).then_inc(s_exp, 1)

            def silu_of(q, b):
                act.wait_ge(s_up, 2 * q + 1)
                act.activation(silu[:, b, :], psum[:, 2 * b, :], ACT.Silu).then_inc(s_si, 1)

            def take_gated(q, b):
                act.wait_ge(s_gt, q + 1)
                act.activation(gated_t[:, b, :], psum[:, G_BANK + b, :], ACT.Copy).then_inc(s_gto, 1)

            silu_of(0, 0)
            if chunks == 2:
                take_gated(0, 0)
                silu_of(1, 1)
            def turn(i):
                for odd in (1, 0):
                    j = 2 * i + (1 if odd else 2)
                    for c in range(chunks):
                        b = c if chunks == 2 else odd
                        take_gated(chunks * j + c - 1, 1 - b)
                        silu_of(chunks * j + c, b)

            turn(0)
            with act.Fori(1, PAIRS) as i:
                turn(i)
            take_gated(chunks * MAXBLK - 1, chunks - 1)
            if finish is not None:
                for i in range(TT // 2):
                    act.wait_ge(s_ft, i + 1)
                    act.activation(k.x1[:, :, i, :], psum[:, i, :].rearrange("p (t n) -> p t n", t=CT), ACT.Copy).then_inc(s_fo, 1)

        @block.tensor
        def _(pe):
            for i in range(TT // 2):
                pe.wait_ge(ln.s_out, 2 * i + 2)
                for t in range(CT):
                    for a in range(2):
                        last = pe.transpose(psum[:, i, N * t + P * a:N * t + P * a + P],
                                            normed[:, 2 * i + a, P * t:P * t + P], k.ident_sb[:])
                last.then_inc(s_ht, 1)
            pe.wait_ge(s_w, 16 * 5)
            pe.wait_ge(s_hto, TT // 2)
            for T in range(TT):
                for t in range(CT):
                    last = pe.matmul(psum[:, 4, E * T:E * T + E], h_t[:, t, P * T:P * T + P], gate_w[:, t, :],
                                     start=(t == 0), stop=(t == CT - 1))
            last.then_inc(s_lg, 1)
            pe.wait_ge(s_r, 8)
            ranks = psum[:, 5, 0:TT * E]
            pe.matmul(ranks, earlier[:, 0, :], either[:].rearrange("p t e -> p (t e)"), start=True, stop=False)
            for T in range(TT - 1):
                pe.matmul(ranks[:, E * (T + 1):].rearrange("p (t e) -> p t e", e=E), earlier[:, 1, :],
                          either[:, T:T + 1, :].broadcast_to([P, TT - 1 - T, E]), start=False, stop=(T == TT - 2))
            for T in range(TT):
                last = pe.matmul(psum[:, 6, 0:E], earlier[:, 1, :], either[:, T, :], start=(T == 0), stop=(T == TT - 1))
            last.then_inc(s_rank, 1)
            pe.wait_ge(s_table, 1)

            def turn_x(j, b, loads):
                pe.wait_ge(s_x[b], loads)
                if above_zero(j):
                    pe.wait_ge(s_xto, j)
                for t in range(CT):
                    last = pe.transpose(psum[:, X_BANK, P * t:P * t + P], xs[:, b, P * t:P * t + P], k.ident_sb[:])
                last.then_inc(s_xt, 1)

            def up(q, xb, b, at, c):
                for side in range(2):
                    for t in range(CT):
                        start = CHUNK_COLS * c + CHUNK * (CT * side + t)
                        last = pe.matmul(psum[:, 2 * b + side, :], x_t[:, xb, t, :],
                                         k.ring[:, bass.ds(at + start, CHUNK)], start=(t == 0), stop=(t == CT - 1))
                    last.then_inc(s_up, 1)

            def turn_gated(q, b):
                pe.wait_ge(s_g, q + 1)
                for a in range(CHUNK // P):
                    last = pe.transpose(psum[:, G_BANK + b, P * a:P * a + P], gated[:, b, P * a:P * a + P], k.ident_sb[:])
                last.then_inc(s_gt, 1)

            def down(q, b, at, c):
                pe.wait_ge(s_gto, q + 1)
                for a in range(CHUNK // P):
                    start = CHUNK_COLS * c + 2 * CT * CHUNK + C * a
                    last = pe.matmul(psum[:, Y_BANK, 0:C], gated_t[:, b, P * a:P * a + P],
                                     k.ring[:, bass.ds(at + start, C)], start=(c == 0 and a == 0),
                                     stop=(c == chunks - 1 and a == CHUNK // P - 1))
                last.then_inc(s_dn, 1)

            def ring_column(j):
                return pe.value_load(table[0:1, 0, bass.ds(j, 1)], min_val=0,
                                     max_val=(RING_EXPERTS - 1) * chunks * CHUNK_COLS)

            pe.wait_ge(s_slot, 1)
            at = ring_column(0)
            turn_x(0, 0, 16)
            pe.wait_ge(s_xto, 1)
            up(0, 0, 0, at, 0)
            if chunks == 2:
                turn_gated(0, 0)
                up(1, 0, 1, at, 1)
            turn_x(1, 1, 16)
            if chunks == 2:
                down(0, 0, at, 0)

            def turn(i):
                at = ring_column(2 * i)
                for odd in (1, 0):
                    j = 2 * i + (1 if odd else 2)
                    at_before, at = at, ring_column(j)
                    for c in range(chunks):
                        b = c if chunks == 2 else odd
                        q = chunks * j + c
                        turn_gated(q - 1, 1 - b)
                        if c == 0:
                            pe.wait_ge(s_xto, j + 1)
                        up(q, odd, b, at, c)
                        if c == chunks - 1:
                            turn_x(j + 1, 1 - odd, 16 * (i + 2))
                            before = j if chunks == 2 else j - 1
                            if above_zero(before):
                                pe.wait_ge(s_y, before)
                        if c == 0:
                            down(q - 1, 1 - b, at_before, chunks - 1)
                        else:
                            down(q - 1, 1 - b, at, c - 1)

            turn(0)
            with pe.Fori(1, PAIRS) as i:
                turn(i)
            at = ring_column(MAXBLK - 1)
            turn_gated(chunks * MAXBLK - 1, chunks - 1)
            pe.wait_ge(s_y, MAXBLK - 1)
            down(chunks * MAXBLK - 1, chunks - 1, at, chunks - 1)
            if finish is not None:
                for i in range(TT // 2):
                    pe.wait_ge(s_t, 4 * (i + 1))
                    for t in range(CT):
                        for a in range(2):
                            last = pe.transpose(psum[:, i, N * t + P * a:N * t + P * a + P],
                                                k.t[:, 2 * i + a, P * t:P * t + P], k.ident_sb[:])
                    last.then_inc(s_ft, 1)



class Shared:
    pass


def _host_arrays(inputs):
    bf16 = mybir.dt.np(BF16)
    f = {n: np.asarray(a) for n, a in inputs.items()}
    a = {}

    def tiles(m, rows=P):
        return np.ascontiguousarray(m.reshape((m.shape[0] // rows, rows) + m.shape[1:]).swapaxes(0, 1))

    def per_image(v):
        return np.repeat(v[..., None], B, axis=-1)

    a["x"] = np.ascontiguousarray(f["x"].reshape(B, CT, P, N).transpose(2, 1, 0, 3))
    a["w1"] = tiles(f["L0_conv_w1"].reshape(CB, C).T)
    a["w_off"] = f["L0_conv_w_off"].reshape(27, CB, TAPS).transpose(1, 2, 0)
    a["b_off"] = f["L0_conv_b_off"].reshape(1, 27)
    a["w2"] = f["L0_conv_w2"].reshape(CB, CB, TAPS).transpose(1, 2, 0).reshape(CB, TAPS * CB)
    a["w3"] = f["L0_conv_w3"].reshape(C, CB).T
    a["gn64"] = per_image(np.stack([f["L0_conv_" + n] for n in ("gn1_scale", "gn1_bias", "gn2_scale", "gn2_bias")], 1))
    a["gn256"] = np.stack([per_image(tiles(f["L0_conv_" + n])).reshape(P, CT * B) for n in ("gn3_scale", "gn3_bias")], 1)
    a["ident"] = np.eye(P, dtype=np.float32)
    a["pair"] = np.kron(np.eye(CB // 2), np.full((2, 2), 0.5)).astype(np.float32)
    a["avg8"] = np.kron(np.eye(P // 8), np.full((8, 8), 0.125)).astype(np.float32)
    n = np.arange(N).reshape(NT, P)
    taps = np.arange(TAPS)
    gx = (n % HW)[:, :, None] + taps % 3 - 1
    gy = (n // HW)[:, :, None] + taps // 3 - 1
    grid = np.concatenate([gx, gy], -1).transpose(1, 0, 2)
    a["grid"] = np.tile(grid, (1, B, 1)).astype(np.float32)
    a["iota"] = np.tile(np.arange(HW, dtype=np.float32), (P, 1))
    a["ones"] = np.ones((1, P), np.float32)

    l1 = {n[8:]: m for n, m in f.items() if n.startswith("L1_conv_")}
    a["w_in"] = tiles(l1["in_proj_w"].T)
    a["b_in"] = tiles(l1["in_proj_b"])
    a["dw"] = tiles(np.concatenate([l1["dw_w"].reshape(C, 3), l1["dw_b"].reshape(C, 1)], 1))
    a["w_dbc"] = tiles(l1["dbc_w"].T)
    a["b_dbc"] = l1["dbc_b"].reshape(1, -1)
    for name, key in (("a_log", "A_log"), ("d_skip", "Dparam")):
        a[name] = np.tile(l1[key].reshape(1, -1), (P, 1))
    a["mobius"] = np.tile(l1["mobius"].reshape(1, HEADS, 4), (P, 1, 1))
    a["w_out"] = tiles(l1["out_proj_w"].T)
    a["b_out"] = l1["out_proj_b"].reshape(1, C)
    side = np.linspace(-1.0, 1.0, HW, dtype=np.float32)
    points = np.stack([np.tile(side, HW), np.repeat(side, HW)])
    own = points.reshape(2, NT, P).transpose(2, 0, 1)
    a["z"] = np.concatenate([np.tile(points, (P, 1, 1)), own], -1)
    a["before"] = (np.arange(N) < n.T[:, :, None]).astype(np.float32)
    a["iota_n"] = np.tile(np.arange(N, dtype=np.float32), (P, 1))
    order = np.arange(P)
    forbid = np.float32(-1e30)
    above = np.where(order[None, :] > order[:, None], forbid, 0.0)
    a["bans"] = np.stack([above, above.T, np.full((P, P), forbid)], 1).astype(bf16)
    a["ident16"] = np.eye(P).astype(bf16)

    def padded_heads(m):
        return tiles(np.concatenate([m.reshape(AH, HD, C), np.zeros((AH, HD, C), np.float32)], 1).reshape(2 * C, C))

    a["a2_wqkv"] = tiles(f["L2_attn_w_qkv"])
    a["a2_w_proj"] = padded_heads(f["L2_attn_w_proj"])
    a["a2_b_proj"] = f["L2_attn_b_proj"].reshape(1, C)
    a["a3_wqkv"] = tiles(np.concatenate([f["L3_attn_" + n] for n in ("Wq", "Wk", "Wv")], 1))
    a["a3_w_proj"] = padded_heads(f["L3_attn_Wo"])
    a["a3_b_proj"] = f["L3_attn_bo"].reshape(1, C)

    def experts(first, second, last):
        def cols(m, c, part):
            m = m[:, :, CHUNK * c:CHUNK * c + CHUNK] if part < 2 else m[:, CHUNK * c:CHUNK * c + CHUNK, :]
            return m.reshape(E, m.shape[1] // P, P, m.shape[2]).transpose(0, 2, 1, 3).reshape(E, P, -1)

        chunks = first.shape[2] // CHUNK
        return np.concatenate([cols(m, c, part) for c in range(chunks) for part, m in enumerate((first, second, last))], -1)

    a["f2_gate"] = tiles(f["L2_ffn_gate_w"].T)
    a["f2_experts"] = experts(*(f["L2_ffn_" + n].transpose(0, 2, 1) for n in ("w1", "w3", "w2")))
    a["f3_gate"] = tiles(f["L3_ffn_Wg"])
    a["f3_experts"] = experts(*(f["L3_ffn_" + n] for n in ("W1", "W2", "W3")))
    a["iota_e"] = np.tile(np.arange(E, dtype=np.float32), (P, 1))
    a["iota_b"] = np.tile(np.arange(PAIRED, dtype=np.float32), (P, 1))
    a["steps"] = np.tile(np.arange(0, TOK, P, dtype=np.float32), (P, 1))
    a["earlier"] = np.stack([order[:, None] < order[None, :], np.ones((P, P))], 1).astype(bf16)
    rows = np.arange(96)[:, None]
    a["select"] = np.repeat((rows % 32 == np.arange(3 * S))[:, :, None], P, 2).astype(bf16)
    return {n: np.ascontiguousarray(m) for n, m in a.items()}


def build(nc, k, out):
    with ExitStack() as ctx:
        def sem(name):
            return ctx.enter_context(nc.semaphore(name))

        def sb(name, shape, dt=F32):
            return ctx.enter_context(nc.sbuf_tensor(name, shape, dt))

        psum = ctx.enter_context(nc.psum_tensor("psum", [P, 8, BANK], F32))
        k.ident_sb = sb("ident_sb", [P, P])
        k.avg8_sb = sb("avg8_sb", [P, P])
        k.x1 = sb("x1", [P, CT, B, N])
        k.h = sb("h", [P, CT, B, N])
        k.t = sb("t", [P, TT, C])
        k.ring = sb("ring", [P, RING_CHUNKS * CHUNK_COLS])
        k.ring_late = k.ring[:, RING_CHUNKS // 2 * CHUNK_COLS:]
        k.parts_dram = nc.dram_tensor("parts_dram", (2, 3, C, TOK), BF16, kind="Internal").ap()
        k.rows_in = nc.dram_tensor("rows_in", (PAIRED * P, C), F32, kind="Internal").ap()
        k.rows_out = nc.dram_tensor("rows_out", (SLOTS, C), F32, kind="Internal").ap()
        k.s_cleared = sem("rows_in_cleared")
        k.s_ring2 = sem("layer_2_experts_loaded")
        k.s_ring3 = sem("layer_3_experts_loaded")
        a2 = dict(wqkv=k.dram["a2_wqkv"], w_proj=k.dram["a2_w_proj"], b_proj=k.dram["a2_b_proj"])
        a3 = dict(wqkv=k.dram["a3_wqkv"], w_proj=k.dram["a3_w_proj"], b_proj=k.dram["a3_b_proj"])
        f2 = dict(gate=k.dram["f2_gate"], experts=k.dram["f2_experts"])
        f3 = dict(gate=k.dram["f3_gate"], experts=k.dram["f3_experts"])
        stores = [out[b].rearrange("(t p) y x -> p t (y x)", p=P) for b in range(B)]

        def own(name):
            return nc.alloc_semaphore(name=name)

        with nc.cleanup_on_exit():
            deformable_conv(nc, own, sb, psum, k)
        with nc.cleanup_on_exit():
            selective_scan(nc, own, sb, psum, k)
        with nc.cleanup_on_exit():
            attention(nc, own, sb, psum, k, a2, False, "a2",
                      lambda sp: load_experts(sp, k, k.dram["f2_experts"], 1, range(RING_CHUNKS // 2, RING_CHUNKS), k.s_ring2))
        with nc.cleanup_on_exit():
            experts_ffn(nc, own, sb, psum, k, f2, 1, RING_CHUNKS, k.s_ring2, "f2")
        with nc.cleanup_on_exit():
            attention(nc, own, sb, psum, k, a3, True, "a3",
                      lambda sp: load_experts(sp, k, k.dram["f3_experts"], 2, range(RING_CHUNKS // 2), k.s_ring3))
        with nc.cleanup_on_exit():
            experts_ffn(nc, own, sb, psum, k, f3, 2, RING_CHUNKS // 2, k.s_ring3, "f3", stores)


def _prepare(inputs):
    arrays = _host_arrays(inputs)
    return {f"in_{n}": m for n, m in arrays.items()}


def _declare(nc, arrays):
    k = Shared()
    k.dram = {n[3:]: nc.dram_tensor(n, m.shape, mybir.dt.from_np(m.dtype), kind="ExternalInput").ap()
              for n, m in arrays.items()}
    return k


def kernel(**inputs):
    import concourse.bacc as bacc
    from concourse.bass_utils import run_bass_kernel_spmd

    nc = bacc.Bacc("TRN2", target_bir_lowering=False, num_devices=1)
    arrays = _prepare(inputs)
    k = _declare(nc, arrays)
    out = nc.dram_tensor("out", (B, C, HW, HW), F32, kind="ExternalOutput").ap()
    build(nc, k, out)
    result = run_bass_kernel_spmd(nc, [arrays], core_ids=[0])
    return result.results[0]["out"]
```

```python
from contextlib import ExitStack

import numpy as np

import concourse.bass as bass
from concourse import mybir

F32 = mybir.dt.float32
BF16 = mybir.dt.bfloat16
I32 = mybir.dt.int32
U32 = mybir.dt.uint32
ACT = mybir.ActivationFunctionType
ALU = mybir.AluOpType
AX_X = mybir.AxisListType.X

P = 128
B, C, HW = 4, 256, 16
N = HW * HW
TOK = B * N
CT = C // P
NT = N // P
TT = TOK // P
CB = 64
TAPS = 9
S = 8
HEADS = 2
AH, HD = 16, 16
E = 8
MAXBLK = (2 * TOK + E * (P - 1)) // P
BANK = 512


class GroupNorm:

    def __init__(self, name, sb, sem, parts, cols, eps):
        self.parts, self.cols, self.eps = parts, cols, eps
        self.raw = sb(f"{name}_raw", [parts, cols, 6])
        self.moments = sb(f"{name}_moments", [parts, cols, 2])
        self.square = sb(f"{name}_square", [parts, cols])
        self.group = sb(f"{name}_group", [parts, cols, 2])
        self.var = sb(f"{name}_var", [parts, cols])
        self.sd = sb(f"{name}_sd", [parts, cols])
        self.scale = sb(f"{name}_scale", [parts, cols])
        self.shift = sb(f"{name}_shift", [parts, cols])
        self.s_stats = sem(f"{name}_stats")
        self.s_moments = sem(f"{name}_moments")
        self.s_grouped = sem(f"{name}_grouped")
        self.s_var = sem(f"{name}_var")
        self.s_sd = sem(f"{name}_sd")
        self.s_affine = sem(f"{name}_affine")

    def stats(self, dve, column, source):
        dve.bn_stats(self.raw[:, column, :], source).then_inc(self.s_stats, 1)

    def partition_moments(self, dve):
        dve.wait_ge(self.s_stats, self.cols)
        for c in range(self.cols):
            last = dve.bn_aggr(self.moments[:, c, :], self.raw[:, c, :])
        last.then_inc(self.s_moments, 1)
        dve.wait_ge(self.s_moments, 1)
        dve.tensor_tensor(self.square[:], self.moments[:, :, 0], self.moments[:, :, 0],
                          ALU.mult).then_inc(self.s_moments, 1)
        dve.wait_ge(self.s_moments, 2)
        dve.tensor_tensor(self.moments[:, :, 1], self.moments[:, :, 1], self.square[:],
                          ALU.add).then_inc(self.s_moments, 1)

    def group_mean(self, pe, psum, averaging):
        pe.wait_ge(self.s_moments, 3)
        pe.matmul(psum, averaging, self.moments[:].rearrange("p c k -> p (c k)"),
                  start=True, stop=True).then_inc(self.s_grouped, 1)

    def variance(self, dve, psum):
        dve.wait_ge(self.s_grouped, 1)
        dve.tensor_copy(self.group[:].rearrange("p c k -> p (c k)"), psum).then_inc(self.s_var, 1)
        dve.wait_ge(self.s_var, 1)
        dve.tensor_tensor(self.square[:], self.group[:, :, 0], self.group[:, :, 0],
                          ALU.mult).then_inc(self.s_var, 1)
        dve.wait_ge(self.s_var, 2)
        dve.scalar_tensor_tensor(self.var[:], self.group[:, :, 1], self.eps, self.square[:],
                                 ALU.add, ALU.subtract).then_inc(self.s_var, 1)

    def deviation(self, act):
        act.wait_ge(self.s_var, 3)
        act.activation(self.sd[:], self.var[:], ACT.Sqrt).then_inc(self.s_sd, 1)

    def affine(self, dve, gamma=None, beta=None):
        dve.wait_ge(self.s_sd, 1)
        dve.reciprocal(self.scale[:], self.sd[:]).then_inc(self.s_affine, 1)
        if gamma is not None:
            dve.wait_ge(self.s_affine, 1)
            dve.tensor_tensor(self.scale[:], self.scale[:], gamma, ALU.mult).then_inc(self.s_affine, 1)
        else:
            dve.engine_nop().then_inc(self.s_affine, 1)
        dve.wait_ge(self.s_affine, 2)
        dve.tensor_tensor(self.shift[:], self.group[:, :, 0], self.scale[:], ALU.mult).then_inc(self.s_affine, 1)
        dve.wait_ge(self.s_affine, 3)
        if beta is not None:
            dve.tensor_tensor(self.shift[:], beta, self.shift[:], ALU.subtract).then_inc(self.s_affine, 1)
        else:
            dve.tensor_scalar(self.shift[:], self.shift[:], -1.0, None, ALU.mult).then_inc(self.s_affine, 1)

    READY = 4


def deformable_conv(nc, sem, sbuf, psum, k):
    with ExitStack() as ctx:
        def sb(name, shape, dt=F32):
            return ctx.enter_context(nc.sbuf_tensor(name, shape, dt))

        x = sb("x_in", [P, CT, B, N])
        w1 = sb("w1", [P, CT, P])
        image = sb("image", [P, 3, B, HW + 2, HW])
        w_off = sb("w_off", [P, 2, 3, 27])
        b_off = sb("b_off", [P, 27])
        w2 = sb("w2", [P, TAPS * CB])
        w3 = sb("w3", [P, 2, C])
        gn64 = sb("gn64", [P, 4, B])
        gn256 = sb("gn256", [P, 2, CT * B])
        pair = sb("pair", [P, P])
        grid = sb("grid", [P, TT, 2 * TAPS])
        iota = sb("iota", [P, HW])
        om = sb("om", [P, TT, 3 * TAPS])
        pos = sb("pos", [P, TT, 2 * TAPS])
        deformed = sb("deformed", [P, B // 2, N])
        mask = sb("mask", [P, TT, TAPS])
        hat = sb("hat", [P, TT, 2 * TAPS, HW])
        weights = sb("weights", [P, 2, NT, TAPS, N])
        weights_t = k.ring[:, 0:B * NT * TAPS * N].rearrange("p (b k n) -> p b k n", b=B, n=N)
        mixed = sb("mixed", [P, B, NT, TAPS, CB])
        r2 = sb("r2", [P, B // 2, N])
        pre = k.h[:].rearrange("p t b n -> p (t b) n")

        g1 = GroupNorm("gn1", sb, sem, P, B, 1e-5)
        g2 = GroupNorm("gn2", sb, sem, P, B // 2, 1e-5)
        g3 = GroupNorm("gn3", sb, sem, P, CT * B, 1e-5)
        g4 = GroupNorm("gn4", sb, sem, P, CT * B, 1e-5)

        s_x = sem("x_loaded")
        s_w1 = sem("w1_loaded")
        s_w = sem("l0_weights_loaded")
        s_c1 = sem("conv1")
        s_pad = sem("padding_zeroed")
        s_img = sem("image_ready")
        s_moved = sem("moved_images_ready")
        s_om = sem("offsets")
        s_oms = sem("offsets_on_sbuf")
        s_yo = sem("deformed_out")
        s_pos = sem("positions")
        s_mask = sem("mask_ready")
        s_dist = sem("distances")
        s_abs = sem("distances_absolute")
        s_tent = sem("hats_unmasked")
        s_hat = sem("hats_ready")
        s_wd = sem("weights_dve")
        s_wp = sem("weights_pool")
        s_tr = sem("weights_transposed")
        s_ea = sem("transpose_out_act")
        s_ed = sem("transpose_out_dve")
        s_mix = sem("mixed_product")
        s_mo = sem("mixed_out")
        s_y = sem("deformed")
        s_r2 = sem("r2_ready")
        s_c3 = sem("conv3")
        s_pre = sem("pre_residual")
        s_x1 = sem("x1_ready")
        s_h1 = sem("h1_ready")

        GROUP = 2
        BANKS = NT * TAPS // GROUP
        MIX_BEFORE = (0, 5)
        y_banks = 6
        block = ctx.enter_context(nc.Block())

        @block.sync
        def _(sp):
            sp.dma_start(w1[:], k.dram["w1"]).then_inc(s_w1, 16)
            sp.dma_start(x[:], k.dram["x"]).then_inc(s_x, 16)
            for dst, src in ((pair, k.dram["pair"]), (gn64, k.dram["gn64"]), (w_off, k.dram["w_off"]), (b_off, k.dram["b_off"]),
                             (grid, k.dram["grid"]), (iota, k.dram["iota"]), (w2, k.dram["w2"]), (k.ident_sb, k.dram["ident"]),
                             (k.avg8_sb, k.dram["avg8"]), (w3, k.dram["w3"]), (gn256, k.dram["gn256"])):
                sp.dma_start(dst[:], src).then_inc(s_w, 16)

        LOADED = 16 * 11

        @block.gpsimd
        def _(pool):
            pool.memset(image[:], 0.0).then_inc(s_pad, 1)
            for b in range(B):
                T = NT * b + 1
                pool.wait_ge(s_hat, b + 1)
                if b >= 2:
                    pool.wait_ge(s_tr, BANKS * (b - 1))
                pool.tensor_tensor(weights[:, b % 2, 1, :, :].rearrange("p k (y x) -> p k y x", y=HW),
                                   hat[:, T, TAPS:, :].unsqueeze(3).broadcast_to([P, TAPS, HW, HW]),
                                   hat[:, T, :TAPS, :].unsqueeze(2).broadcast_to([P, TAPS, HW, HW]),
                                   ALU.mult).then_inc(s_wp, 1)

        @block.vector
        def _(dve):
            for b in range(B):
                dve.wait_ge(s_c1, b // 2 + 1)
                g1.stats(dve, b, psum[:, y_banks + b // 2, (b % 2) * N:(b % 2) * N + N])
            g1.partition_moments(dve)
            g1.variance(dve, psum[:, 4, 0:2 * B])
            dve.wait_ge(s_w, LOADED)
            g1.affine(dve, gn64[:, 0, :], gn64[:, 1, :])
            dve.wait_ge(s_img, 2 * B)
            dve.tensor_copy(image[:, 2, :, :, 0:HW - 1], image[:, 1, :, :, 1:HW]).then_inc(s_moved, 1)
            dve.wait_ge(s_om, 1)
            dve.tensor_tensor(om[:], psum[:, 5, 0:TT * 3 * TAPS].rearrange("p (t o) -> p t o", t=TT),
                              b_off[:].unsqueeze(1).broadcast_to([P, TT, 3 * TAPS]), ALU.add).then_inc(s_oms, 1)
            dve.wait_ge(s_oms, 1)
            dve.tensor_tensor(pos[:], om[:, :, 0:2 * TAPS], grid[:], ALU.add).then_inc(s_pos, 1)
            dve.wait_ge(s_pos, 1)
            for b in range(B):
                shape = [P, NT * 2 * TAPS, HW]
                tiles = slice(NT * b, NT * b + NT)
                dve.tensor_tensor(hat[:, tiles].rearrange("p t k i -> p (t k) i"),
                                  pos[:, tiles].rearrange("p t k -> p (t k)").unsqueeze(2).broadcast_to(shape),
                                  iota[:].unsqueeze(1).broadcast_to(shape), ALU.subtract).then_inc(s_dist, 1)

            def sampling(b):
                tiles = slice(NT * b, NT * b + NT)
                dve.wait_ge(s_tent, b + 1)
                dve.tensor_tensor(hat[:, tiles, TAPS:, :], hat[:, tiles, TAPS:, :],
                                  mask[:, tiles].unsqueeze(3).broadcast_to([P, NT, TAPS, HW]), ALU.mult).then_inc(s_hat, 1)
                dve.wait_ge(s_hat, b + 1)
                if b >= 2:
                    dve.wait_ge(s_tr, BANKS * (b - 1))
                T = NT * b
                dve.tensor_tensor(weights[:, b % 2, 0, :, :].rearrange("p k (y x) -> p k y x", y=HW),
                                  hat[:, T, TAPS:, :].unsqueeze(3).broadcast_to([P, TAPS, HW, HW]),
                                  hat[:, T, :TAPS, :].unsqueeze(2).broadcast_to([P, TAPS, HW, HW]),
                                  ALU.mult).then_inc(s_wd, 1)

            def take(i):
                dve.wait_ge(s_y, i + 1)
                dve.tensor_copy(deformed[:, i, :], psum[:, y_banks + i, 0:N]).then_inc(s_yo, 1)
                dve.wait_ge(s_yo, i + 1)
                g2.stats(dve, i, deformed[:, i, :])

            sampling(0)
            for b in range(B):
                if b + 1 < B:
                    sampling(b + 1)
                for j in range(BANKS):
                    J = BANKS * b + j
                    if J % 2 == 1:
                        dve.wait_ge(s_tr, J + 1)
                        dve.tensor_copy(weights_t[:, b, GROUP * j:GROUP * j + GROUP, :].rearrange("p a n -> p (a n)"),
                                        psum[:, J % 4, :]).then_inc(s_ed, 1)
                if b == B - 1:
                    take(0)
            take(1)
            g2.partition_moments(dve)
            g2.variance(dve, psum[:, 4, 0:B])
            g2.affine(dve, gn64[:, 2, 0:B // 2], gn64[:, 3, 0:B // 2])
            for i in range(CT * B):
                if i % 2 == 0:
                    dve.wait_ge(s_c3, i // 2 + 1)
                g3.stats(dve, i, psum[:, i // 2, (i % 2) * N:(i % 2) * N + N])
            g3.partition_moments(dve)
            g3.variance(dve, psum[:, 4, 0:2 * CT * B])
            g3.affine(dve, gn256[:, 0, :], gn256[:, 1, :])
            dve.wait_ge(g3.s_affine, g3.READY)
            xs = x[:].rearrange("p t b n -> p (t b) n")
            for i in range(CT * B):
                dve.scalar_tensor_tensor(pre[:, i, :], psum[:, i // 2, (i % 2) * N:(i % 2) * N + N],
                                         g3.scale[:, i:i + 1], xs[:, i, :], ALU.mult, ALU.add).then_inc(s_pre, 1)
            for i in range(CT * B):
                dve.wait_ge(s_x1, i + 1)
                g4.stats(dve, i, k.x1[:].rearrange("p t b n -> p (t b) n")[:, i, :])
            g4.partition_moments(dve)
            g4.variance(dve, psum[:, 5, 0:2 * CT * B])
            g4.affine(dve)
            dve.wait_ge(g4.s_affine, g4.READY)
            for i in range(CT * B):
                dve.tensor_scalar(k.h[:].rearrange("p t b n -> p (t b) n")[:, i, :],
                                  k.x1[:].rearrange("p t b n -> p (t b) n")[:, i, :],
                                  g4.scale[:, i:i + 1], g4.shift[:, i:i + 1], ALU.mult, ALU.add).then_inc(s_h1, 1)

        @block.scalar
        def _(act):
            g1.deviation(act)
            act.wait_ge(g1.s_affine, g1.READY)
            act.wait_ge(s_pad, 1)
            for b in range(B):
                for half in range(2):
                    channels = slice(CB * half, CB * half + CB)
                    act.activation(image[channels, 1, b, 1 - half:HW + 1 - half, :],
                                   psum[channels, y_banks + b // 2, (b % 2) * N:(b % 2) * N + N].rearrange("p (y x) -> p y x", y=HW),
                                   ACT.Relu, bias=g1.shift[channels, b:b + 1], scale=g1.scale[channels, b:b + 1]).then_inc(s_img, 1)
            act.wait_ge(s_img, 2 * B)
            act.activation(image[:, 0, :, :, 1:HW], image[:, 1, :, :, 0:HW - 1], ACT.Copy).then_inc(s_moved, 1)
            act.wait_ge(s_oms, 1)
            act.activation(mask[:], om[:, :, 2 * TAPS:], ACT.Sigmoid).then_inc(s_mask, 1)
            for b in range(B):
                hats = hat[:, NT * b:NT * b + NT].rearrange("p t k i -> p (t k i)")
                act.wait_ge(s_dist, b + 1)
                act.activation(hats, hats, ACT.Abs).then_inc(s_abs, 1)
                act.wait_ge(s_abs, b + 1)
                act.activation(hats, hats, ACT.Relu, bias=1.0, scale=-1.0).then_inc(s_tent, 1)

            def take_mixed(i):
                b, s = i // NT, i % NT
                act.wait_ge(s_mix, i + 1)
                act.activation(mixed[:, b, s, :, :].rearrange("p k o -> p (k o)").rearrange("p (a n) -> p a n", a=2),
                               psum[:, 4:6, 0:TAPS * CB // 2], ACT.Copy).then_inc(s_mo, 1)

            for b in range(B):
                for j in range(BANKS):
                    if j in MIX_BEFORE:
                        take_mixed(NT * b + MIX_BEFORE.index(j))
                    J = BANKS * b + j
                    if J % 2 == 0:
                        act.wait_ge(s_tr, J + 1)
                        act.activation(weights_t[:, b, GROUP * j:GROUP * j + GROUP, :].rearrange("p a n -> p (a n)"),
                                       psum[:, J % 4, :], ACT.Copy).then_inc(s_ea, 1)
            g2.deviation(act)
            act.wait_ge(g2.s_affine, g2.READY)
            for i in range(B // 2):
                act.activation(r2[:, i, :], deformed[:, i, :], ACT.Relu,
                               bias=g2.shift[:, i:i + 1], scale=g2.scale[:, i:i + 1]).then_inc(s_r2, 1)
            g3.deviation(act)
            act.wait_ge(g3.s_affine, g3.READY)
            for i in range(CT * B):
                act.wait_ge(s_pre, i + 1)
                act.activation(k.x1[:].rearrange("p t b n -> p (t b) n")[:, i, :], pre[:, i, :], ACT.Relu,
                               bias=g3.shift[:, i:i + 1]).then_inc(s_x1, 1)
            g4.deviation(act)

        @block.tensor
        def _(pe):
            pe.wait_ge(s_w1, 16)
            pe.wait_ge(s_x, 16)
            for half in range(2):
                for t in range(CT):
                    last = pe.matmul(psum[:, y_banks + half, :], w1[:, t, :],
                                     x[:, t, 2 * half:2 * half + 2, :].rearrange("p b n -> p (b n)"),
                                     start=(t == 0), stop=(t == CT - 1))
                last.then_inc(s_c1, 1)
            pe.wait_ge(s_w, LOADED)
            g1.group_mean(pe, psum[:, 4, 0:2 * B], pair[:])
            pe.wait_ge(s_moved, 2)

            def rows(dx, b, y):
                return image[:, dx, b, y:y + HW // NT, :].rearrange("p y x -> p (y x)")

            for T in range(TT):
                b, y0 = T // NT, (T % NT) * HW // NT
                for both in range(2):
                    for dx in range(3):
                        last = pe.matmul(psum[:, 5, 27 * T:27 * T + 27], rows(dx, b, y0 + 2 * both), w_off[:, both, dx, :],
                                         start=(both == 0 and dx == 0), stop=(both == 1 and dx == 2))
            last.then_inc(s_om, 1)

            def mix(i):
                b, s = i // NT, i % NT
                if i >= 1:
                    pe.wait_ge(s_mo, i)
                else:
                    pe.wait_ge(s_oms, 1)
                for a in range(2):
                    last = pe.matmul(psum[:, 4 + a, 0:TAPS * CB // 2], rows(1, b, 1 + s * HW // NT),
                                     w2[:, a * TAPS * CB // 2:(a + 1) * TAPS * CB // 2], start=True, stop=True)
                last.then_inc(s_mix, 1)

            def sample(i):
                pe.wait_ge(s_mo, NT * (2 * i + 2))
                pe.wait_ge(s_ea, (BANKS * (2 * i + 2) + 1) // 2)
                pe.wait_ge(s_ed, BANKS * (2 * i + 2) // 2)
                for tap in range(NT * TAPS):
                    for half in range(2):
                        b = 2 * i + half
                        last = pe.matmul(psum[CB * half:CB * half + CB, y_banks + i, 0:N],
                                         mixed[:, b, tap // TAPS, tap % TAPS, :], weights_t[:, b, tap, :],
                                         start=(tap == 0), stop=(tap == NT * TAPS - 1))
                last.then_inc(s_y, 1)

            for b in range(B):
                for j in range(BANKS):
                    if j in MIX_BEFORE:
                        mix(NT * b + MIX_BEFORE.index(j))
                    if j == 0:
                        pe.wait_ge(s_wd, b + 1)
                        pe.wait_ge(s_wp, b + 1)
                    J = BANKS * b + j
                    if J >= 4:
                        pe.wait_ge(s_ea if J % 2 == 0 else s_ed, (J - 4) // 2 + 1)
                    for a in range(GROUP):
                        s, tap = (GROUP * j + a) // TAPS, (GROUP * j + a) % TAPS
                        for t in range(NT):
                            last = pe.transpose(psum[:, J % 4, a * N + P * t:a * N + P * t + P],
                                                weights[:, b % 2, t, tap, P * s:P * s + P], k.ident_sb[:])
                    last.then_inc(s_tr, 1)
                if b == B - 2:
                    sample(0)
            sample(1)
            g2.group_mean(pe, psum[:, 4, 0:B], pair[:])
            pe.wait_ge(s_r2, B // 2)
            for t in range(CT):
                for b in range(B):
                    last = pe.matmul(psum[:, 2 * t + b // 2, (b % 2) * N:(b % 2) * N + N], w3[:, b % 2, P * t:P * t + P],
                                     r2[:, b // 2, :], start=True, stop=True)
                    if b % 2:
                        last.then_inc(s_c3, 1)
            g3.group_mean(pe, psum[:, 4, 0:2 * CT * B], k.avg8_sb[:])
            g4.group_mean(pe, psum[:, 5, 0:2 * CT * B], k.avg8_sb[:])


def selective_scan(nc, sem, sbuf, psum, k):
    QROWS = 32
    DEEP = 3
    ROWS = 3 * S
    with ExitStack() as ctx:
        def sb(name, shape, dt=F32):
            return ctx.enter_context(nc.sbuf_tensor(name, shape, dt))

        w_in = sb("w_in", [P, CT, 3 * C])
        b_in = sb("b_in", [P, 3 * CT])
        dw = sb("dw", [P, CT, 4])
        w_dbc = sb("w_dbc", [P, CT, 2 * (2 * S + 1)])
        b_dbc = sb("b_dbc", [1, 2 * (2 * S + 1)])
        a_log = sb("a_log", [P, HEADS * S])
        d_skip = sb("d_skip", [P, HEADS])
        mobius = sb("mobius", [P, HEADS, 4])
        w_out = sb("w_out", [P, CT, C])
        b_out = sb("b_out", [1, C])
        z = sb("z", [P, 2, N + NT])
        before = sb("before", [P, NT, N])
        iota = sb("iota_n", [P, N])
        ones = sb("ones_row1", [1, P])
        select = sb("select", [3 * QROWS, ROWS, P], BF16)

        xs = sb("xs", [P, CT, B, N + 2])
        res, gate, x_perm, y_scan = (k.ring_late[:, i * CT * TOK:(i + 1) * CT * TOK].rearrange("p (t n) -> p t n", t=CT)
                                     for i in range(4))
        conv = y_scan.rearrange("p t (b n) -> p t b n", b=B)
        xf = sb("xf", [P, CT, TOK])
        xf_t = sb("xf_t", [P, TT, C])
        mob = sb("mob", [P, HEADS, 4])
        det = sb("det", [P, 3, HEADS])
        cplx = sb("cplx", [P, 6, N + NT])
        score = sb("score", [P, HEADS, N + NT])
        less = sb("less", [P, HEADS, NT, N])
        rank = sb("rank", [P, HEADS, NT])
        order = sb("order", [P, HEADS, NT, N])
        order_t = sb("order_t", [P, HEADS, NT, N])
        tie = order_t
        dbc = sb("dbc", [P, TT, HEADS, 2 * S + 1])
        soft = sb("soft", [P, 6, TT, HEADS])
        a_neg = sb("a_neg", [P, HEADS * S])
        rows = sb("rows", [P, TT, HEADS, 3, QROWS])
        parts = sb("parts", [3 * QROWS, HEADS, TOK], BF16)
        rest = sb("rest", [3 * QROWS, TOK])
        middle = sb("middle", [3 * QROWS, TOK], BF16)
        dtb = sb("dtb", [P, DEEP, BANK])
        u = sb("u", [P, DEEP, BANK])
        state = sb("state", [P, DEEP, BANK])
        prod = sb("prod", [P, DEEP, BANK])
        y_t = xf_t
        y = x_perm
        silu_out = u

        s_w = sem("l1_weights_loaded")
        s_zero = sem("l1_zeroed")
        s_in = sem("in_proj")
        s_silu = sem("in_proj_silu")
        s_gate = sem("gate_silu")
        s_cv = sem("depthwise_steps")
        s_xf = sem("xf_ready")
        s_xt = sem("xf_transposed")
        s_xto = sem("xf_t_out")
        s_mob = sem("mobius_steps")
        s_det = sem("mobius_root")
        s_rank = sem("rank_steps")
        s_ord = sem("order_ready")
        s_ot = sem("order_transposed")
        s_oto = sem("order_t_out")
        s_dbc = sem("dbc_product")
        s_so = sem("softplus_dve")
        s_sa = sem("softplus_act")
        s_rows = sem("rows_ready")
        s_rp = sem("rows_permuted")
        s_hi = sem("high_part")
        s_rest = sem("rest_of_parts")
        s_mid = sem("middle_part")
        s_parts = sem("parts_ready")
        s_xp = sem("x_permuted")
        s_xpo = sem("x_perm_out")
        s_bdt = sem("dt_b_spread")
        s_bda = sem("decay_spread")
        s_bc = sem("c_spread")
        s_dtb = sem("dtb_out")
        s_u = sem("scan_input")
        s_scan = sem("scanned")
        s_cm = sem("times_c")
        s_acc = sem("summed_over_states")
        s_ys = sem("y_scan_out")
        s_yt = sem("y_transposed")
        s_yto = sem("y_t_out")
        s_un = sem("y_unpermuted")
        s_y = sem("gating_steps")
        s_op = sem("out_proj")
        s_so2 = sem("out_proj_silu")
        s_t = sem("tokens_ready")

        PAIRS = HEADS * B // 2
        STEPS = PAIRS * S
        block = ctx.enter_context(nc.Block())
        DT, AB, EX, U1, LN, TMP = range(6)

        @block.sync
        def _(sp):
            for dst, src in ((w_in, k.dram["w_in"]), (b_in, k.dram["b_in"]), (mobius, k.dram["mobius"]), (z, k.dram["z"]), (before, k.dram["before"]),
                             (iota, k.dram["iota_n"]), (dw, k.dram["dw"]), (w_dbc, k.dram["w_dbc"]), (b_dbc, k.dram["b_dbc"]), (a_log, k.dram["a_log"]),
                             (d_skip, k.dram["d_skip"]), (w_out, k.dram["w_out"]), (b_out, k.dram["b_out"]), (ones, k.dram["ones"]),
                             (select, k.dram["select"])):
                sp.dma_start(dst[:], src).then_inc(s_w, 16)
            for n in range(RING_CHUNKS // 2):
                load_chunk(sp, k, k.dram["f2_experts"], 1, n, k.s_ring2)

        LOADED = 16 * 15

        @block.gpsimd
        def _(pool):
            pool.memset(xs[:, :, :, 0:1], 0.0).then_inc(s_zero, 1)
            pool.memset(xs[:, :, :, N + 1:N + 2], 0.0).then_inc(s_zero, 1)
            pool.memset(rows[:], 0.0).then_inc(s_zero, 1)
            for h in range(HEADS):
                pool.wait_ge(s_parts, h + 1)
                pool.wait_ge(s_mid, 2 * (h + 1))
                for q in range(3):
                    last = pool.memset(parts[QROWS * q:QROWS * q + S, h, :].rearrange("p (b n) -> p b n", b=B)[:, :, 0:1], 0.0)
                last.then_inc(s_zero, 1)
            for i in range(STEPS):
                h, half = i // S // 2, i // S % 2
                if i % (2 * S) == 0:
                    pool.wait_ge(s_xpo, h + 1)
                pool.wait_ge(s_dtb, i + 1)
                if i >= DEEP:
                    pool.wait_ge(s_scan, i - DEEP + 1)
                pool.tensor_tensor(u[:, i % DEEP, :], dtb[:, i % DEEP, :], x_perm[:, h, BANK * half:BANK * half + BANK],
                                   ALU.mult).then_inc(s_u, 1)

        @block.vector
        def _(dve):
            dve.wait_ge(s_w, LOADED)
            n = 0

            def step(ins):
                nonlocal n
                n += 1
                ins.then_inc(s_mob, 1)
                dve.wait_ge(s_mob, n)

            step(dve.tensor_tensor(det[:, 0, :], mobius[:, :, 0], mobius[:, :, 3], ALU.mult))
            step(dve.tensor_tensor(det[:, 1, :], mobius[:, :, 1], mobius[:, :, 2], ALU.mult))
            step(dve.tensor_tensor(det[:, 2, :], det[:, 0, :], det[:, 1, :], ALU.subtract))
            dve.wait_ge(s_det, 1)
            step(dve.tensor_scalar(det[:, 0, :], det[:, 0, :], 0.001, None, ALU.max))
            dve.wait_ge(s_det, 2)
            step(dve.reciprocal(det[:, 2, :], det[:, 1, :]))
            step(dve.tensor_tensor(mob[:], mobius[:], det[:, 2, :].unsqueeze(2).broadcast_to([P, HEADS, 4]), ALU.mult))
            step(dve.tensor_scalar(det[:, 0, :], mob[:, :, 3], 1e-6, None, ALU.add))
            for h in range(HEADS):
                a, bb, c, dd = mob[:, h, 0:1], mob[:, h, 1:2], mob[:, h, 2:3], det[:, 0, h:h + 1]
                NR, NI, DR, DI, RE, IM = (cplx[:, i, :] for i in range(6))
                step(dve.tensor_scalar(NR, z[:, 0, :], a, bb, ALU.mult, ALU.add))
                step(dve.tensor_scalar(NI, z[:, 1, :], a, None, ALU.mult))
                step(dve.tensor_scalar(DR, z[:, 0, :], c, dd, ALU.mult, ALU.add))
                step(dve.tensor_scalar(DI, z[:, 1, :], c, None, ALU.mult))
                step(dve.tensor_tensor(RE, NR, DR, ALU.mult))
                step(dve.tensor_tensor(IM, NI, DI, ALU.mult))
                step(dve.tensor_tensor(RE, RE, IM, ALU.add))
                step(dve.tensor_tensor(NI, NI, DR, ALU.mult))
                step(dve.tensor_tensor(NR, NR, DI, ALU.mult))
                step(dve.tensor_tensor(IM, NI, NR, ALU.subtract))
                step(dve.scalar_tensor_tensor(RE, IM, 1.3, RE, ALU.mult, ALU.add))
                step(dve.tensor_tensor(DR, DR, DR, ALU.mult))
                step(dve.tensor_tensor(DI, DI, DI, ALU.mult))
                step(dve.tensor_tensor(DR, DR, DI, ALU.add))
                step(dve.reciprocal(DI, DR))
                step(dve.tensor_tensor(score[:, h, :], RE, DI, ALU.mult))
            for h in range(HEADS):
                for t in range(NT):
                    own = score[:, h, N + t:N + t + 1]
                    dve.tensor_scalar(less[:, h, t, :], score[:, h, 0:N], own, None, ALU.is_lt).then_inc(s_rank, 1)
                    dve.scalar_tensor_tensor(tie[:, h, t, :], score[:, h, 0:N], own, before[:, t, :],
                                             ALU.is_equal, ALU.mult).then_inc(s_rank, 1)
            dve.wait_ge(s_rank, 2 * HEADS * NT)
            flat = "p h t n -> p (h t) n"
            dve.tensor_tensor(less[:].rearrange(flat), less[:].rearrange(flat), tie[:].rearrange(flat),
                              ALU.add).then_inc(s_rank, 1)
            dve.wait_ge(s_rank, 2 * HEADS * NT + 1)
            dve.tensor_reduce(rank[:].rearrange("p h t -> p (h t)"), less[:].rearrange(flat), AX_X, ALU.add).then_inc(s_rank, 1)
            dve.wait_ge(s_rank, 2 * HEADS * NT + 2)
            for h in range(HEADS):
                for t in range(NT):
                    dve.tensor_scalar(order[:, h, t, :], iota[:], rank[:, h, t:t + 1], None,
                                      ALU.is_equal).then_inc(s_ord, 1)
            for t in range(CT):
                dve.wait_ge(s_silu, t + 1)
                dve.wait_ge(s_zero, 2)
                dve.tensor_scalar(conv[:, t], xs[:, t, :, 0:N], dw[:, t, 0:1], dw[:, t, 3:4], ALU.mult, ALU.add).then_inc(s_cv, 1)
                dve.wait_ge(s_cv, 3 * t + 1)
                dve.scalar_tensor_tensor(conv[:, t], xs[:, t, :, 1:N + 1], dw[:, t, 1:2], conv[:, t],
                                         ALU.mult, ALU.add).then_inc(s_cv, 1)
                dve.wait_ge(s_cv, 3 * t + 2)
                dve.scalar_tensor_tensor(conv[:, t], xs[:, t, :, 2:N + 2], dw[:, t, 2:3], conv[:, t],
                                         ALU.mult, ALU.add).then_inc(s_cv, 1)
            for h in range(HEADS):
                dve.wait_ge(s_ot, h + 1)
                dve.tensor_copy(order_t[:, h].rearrange("p t n -> p (t n)"), psum[:, 4 + h, :]).then_inc(s_oto, 1)
            dve.wait_ge(s_dbc, 1)
            flat_dbc = dbc[:].rearrange("p t h j -> p (t h j)")
            dve.tensor_copy(flat_dbc, psum[:, 6, 0:TT * HEADS * (2 * S + 1)]).then_inc(s_so, 1)
            dve.wait_ge(s_so, 1)
            dve.wait_ge(s_sa, 2)
            dve.tensor_scalar(soft[:, U1], soft[:, EX], 1.0, None, ALU.add).then_inc(s_so, 1)
            dve.wait_ge(s_sa, 3)
            dve.tensor_scalar(soft[:, U1], soft[:, U1], 1.0, None, ALU.subtract).then_inc(s_so, 1)
            dve.tensor_tensor(soft[:, LN], soft[:, LN], soft[:, EX], ALU.mult).then_inc(s_so, 1)
            dve.wait_ge(s_so, 4)
            dve.tensor_scalar(soft[:, AB], soft[:, U1], 1e-30, None, ALU.max).then_inc(s_so, 1)
            dve.wait_ge(s_so, 5)
            dve.reciprocal(soft[:, TMP], soft[:, AB]).then_inc(s_so, 1)
            dve.wait_ge(s_so, 6)
            dve.tensor_tensor(soft[:, LN], soft[:, LN], soft[:, TMP], ALU.mult).then_inc(s_so, 1)
            dve.scalar_tensor_tensor(soft[:, EX], soft[:, U1], 0.0, soft[:, EX], ALU.is_equal, ALU.mult).then_inc(s_so, 1)
            dve.wait_ge(s_so, 8)
            dve.tensor_tensor(soft[:, LN], soft[:, LN], soft[:, EX], ALU.add).then_inc(s_so, 1)
            dve.wait_ge(s_so, 9)
            dve.scalar_tensor_tensor(soft[:, DT], dbc[:, :, :, 0], 0.0, soft[:, LN], ALU.max, ALU.add).then_inc(s_so, 1)
            dve.wait_ge(s_so, 10)
            dve.wait_ge(s_sa, 4)
            dve.wait_ge(s_zero, 3)
            dt_wide = soft[:, DT].unsqueeze(3).broadcast_to([P, TT, HEADS, S])
            dve.tensor_tensor(rows[:, :, :, 0, 0:S], dt_wide,
                              a_neg[:].rearrange("p (h s) -> p h s", h=HEADS).unsqueeze(1).broadcast_to([P, TT, HEADS, S]),
                              ALU.mult).then_inc(s_rows, 1)
            dve.tensor_tensor(rows[:, :, :, 0, S:2 * S], dt_wide, dbc[:, :, :, 1:1 + S], ALU.mult).then_inc(s_rows, 1)
            dve.tensor_copy(rows[:, :, :, 0, 2 * S:3 * S], dbc[:, :, :, 1 + S:]).then_inc(s_rows, 1)
            dve.wait_ge(s_sa, 5)
            dve.wait_ge(s_rows, 3)
            for q in (1, 2):
                for h in range(HEADS):
                    dve.tensor_copy(rows[:, :, h, q, 0:ROWS], rows[:, :, h, 0, 0:ROWS]).then_inc(s_rows, 1)
            for h in range(HEADS):
                dve.wait_ge(s_hi, h + 1)
                if h:
                    dve.wait_ge(s_mid, 2)
                    dve.wait_ge(s_parts, 1)
                permuted = psum[0:3 * QROWS, 2 * h:2 * h + 2, :].rearrange("p a n -> p (a n)")
                dve.tensor_tensor(rest[:], permuted, parts[:, h, :], ALU.subtract).then_inc(s_rest, 1)
                dve.wait_ge(s_mid, 2 * h + 2)
                dve.tensor_tensor(parts[2 * QROWS:3 * QROWS, h, :], rest[2 * QROWS:3 * QROWS], middle[2 * QROWS:3 * QROWS],
                                  ALU.subtract).then_inc(s_parts, 1)
            def times_c(i):
                dve.wait_ge(s_scan, i + 1)
                dve.wait_ge(s_bc, i + 1)
                if i >= DEEP:
                    dve.wait_ge(s_acc, i - DEEP + 1)
                dve.tensor_tensor(prod[:, i % DEEP, :], state[:, i % DEEP, :], psum[:, 4 + i % 2, :], ALU.mult).then_inc(s_cm, 1)

            for i in range(STEPS):
                dve.wait_ge(s_bda, i + 1)
                dve.wait_ge(s_u, i + 1)
                if i >= DEEP:
                    dve.wait_ge(s_cm, i - DEEP + 1)
                dve.tensor_tensor_scan(state[:, i % DEEP, :], psum[:, i % 2, :], u[:, i % DEEP, :], 0.0,
                                       ALU.mult, ALU.add).then_inc(s_scan, 1)
                if i >= 1:
                    times_c(i - 1)
            times_c(STEPS - 1)
            dve.wait_ge(s_silu, 3 * CT)
            dve.wait_ge(s_gate, CT)
            for h in range(HEADS):
                for half in range(2):
                    i = 2 * h + half
                    cols = slice(BANK * half, BANK * half + BANK)
                    dve.wait_ge(s_un, i + 1)
                    dve.scalar_tensor_tensor(y[:, h, cols], xf[:, h, cols], d_skip[:, h:h + 1], psum[:, 4 + i, :],
                                             ALU.mult, ALU.add).then_inc(s_y, 1)
                    dve.wait_ge(s_y, 3 * i + 1)
                    dve.tensor_tensor(y[:, h, cols], y[:, h, cols], gate[:, h, cols], ALU.mult).then_inc(s_y, 1)
                    dve.wait_ge(s_y, 3 * i + 2)
                    dve.tensor_tensor(y[:, h, cols], y[:, h, cols], res[:, h, cols], ALU.add).then_inc(s_y, 1)
            for i in range(TT // 2):
                dve.wait_ge(s_so2, i + 1)
                dve.tensor_tensor(k.t[:, 2 * i:2 * i + 2, :].rearrange("p a n -> p (a n)"), silu_out[:, i % 2, :],
                                  psum[:, 2 + i % 2, :], ALU.add).then_inc(s_t, 1)

        def scanned(act, pair):
            h, half = pair // 2, pair % 2
            act.wait_ge(s_acc, S * (pair + 1))
            act.activation(y_scan[:, h, BANK * half:BANK * half + BANK], psum[:, 6 + pair % 2, :],
                           ACT.Copy).then_inc(s_ys, 1)

        @block.scalar
        def _(act):
            act.wait_ge(s_w, LOADED)
            act.wait_ge(s_mob, 3)
            act.activation(det[:, 0, :], det[:, 2, :], ACT.Abs).then_inc(s_det, 1)
            act.wait_ge(s_mob, 4)
            act.activation(det[:, 1, :], det[:, 0, :], ACT.Sqrt).then_inc(s_det, 1)
            for i in range(3 * CT):
                act.wait_ge(s_in, i + 1)
                source = psum[:, 2 * (i % 2):2 * (i % 2) + 2, :].rearrange("p a n -> p (a n)")
                if i < CT:
                    target = xs[:, i, :, 1:N + 1]
                    source = source.rearrange("p (b n) -> p b n", b=B)
                    act.wait_ge(s_zero, 2)
                else:
                    target = (res if i < 2 * CT else gate)[:, i % CT, :]
                act.activation(target, source, ACT.Silu, bias=b_in[:, i:i + 1]).then_inc(s_silu, 1)
                if CT <= i < 2 * CT:
                    act.wait_ge(s_cv, 3 * (i - CT + 1))
                    act.activation(xf[:, i - CT, :], conv[:, i - CT].rearrange("p b n -> p (b n)"), ACT.Silu).then_inc(s_xf, 1)
            act.wait_ge(s_silu, 3 * CT)
            for i in range(CT):
                act.activation(gate[:, i, :], gate[:, i, :], ACT.Silu).then_inc(s_gate, 1)
            for i in range(TT // 2):
                act.wait_ge(s_xt, i + 1)
                act.activation(xf_t[:, 2 * i:2 * i + 2, :].rearrange("p a n -> p (a n)"), psum[:, i, :], ACT.Copy).then_inc(s_xto, 1)
            act.wait_ge(s_so, 1)
            act.activation(soft[:, AB], dbc[:, :, :, 0], ACT.Abs).then_inc(s_sa, 1)
            act.wait_ge(s_sa, 1)
            act.activation(soft[:, EX], soft[:, AB], ACT.Exp, scale=-1.0).then_inc(s_sa, 1)
            act.wait_ge(s_so, 2)
            act.activation(soft[:, LN], soft[:, U1], ACT.Ln).then_inc(s_sa, 1)
            act.activation(a_neg[:], a_log[:], ACT.Exp).then_inc(s_sa, 1)
            act.wait_ge(s_rows, 1)
            act.activation(rows[:, :, :, 0, 0:S], rows[:, :, :, 0, 0:S], ACT.Exp, scale=-1.0).then_inc(s_sa, 1)
            for h in range(HEADS):
                act.wait_ge(s_rp, h + 1)
                act.activation(parts[:, h, :], psum[0:3 * QROWS, 2 * h:2 * h + 2, :].rearrange("p a n -> p (a n)"),
                               ACT.Copy).then_inc(s_hi, 1)
                act.wait_ge(s_rest, h + 1)
                act.activation(parts[QROWS:2 * QROWS, h, :], rest[QROWS:2 * QROWS], ACT.Copy).then_inc(s_mid, 1)
                act.activation(middle[2 * QROWS:3 * QROWS], rest[2 * QROWS:3 * QROWS], ACT.Copy).then_inc(s_mid, 1)
                act.wait_ge(s_xp, h + 1)
                act.activation(x_perm[:, h, :], psum[:, 4 + 2 * h:6 + 2 * h, :].rearrange("p a n -> p (a n)"),
                               ACT.Copy).then_inc(s_xpo, 1)
            for i in range(STEPS):
                act.wait_ge(s_bdt, i + 1)
                if i >= DEEP:
                    act.wait_ge(s_u, i - DEEP + 1)
                act.activation(dtb[:, i % DEEP, :], psum[:, 2 + i % 2, :], ACT.Copy).then_inc(s_dtb, 1)
                if i % S == 4 and i > S:
                    scanned(act, i // S - 1)
            scanned(act, PAIRS - 1)
            for i in range(TT // 2):
                act.wait_ge(s_yt, i + 1)
                act.activation(y_t[:, 2 * i:2 * i + 2, :].rearrange("p a n -> p (a n)"), psum[:, i, :], ACT.Copy).then_inc(s_yto, 1)
            for i in range(TT // 2):
                act.wait_ge(s_op, i + 1)
                if i >= 2:
                    act.wait_ge(s_t, i - 1)
                act.activation(silu_out[:, i % 2, :], psum[:, i % 2, :], ACT.Silu).then_inc(s_so2, 1)

        @block.tensor
        def _(pe):
            pe.wait_ge(s_w, LOADED)
            for i in range(3 * CT):
                if i >= 2:
                    pe.wait_ge(s_silu, i - 1)
                for half in range(2):
                    for t in range(CT):
                        last = pe.matmul(psum[:, 2 * (i % 2) + half, :], w_in[:, t, P * i:P * i + P],
                                         k.h[:, t, 2 * half:2 * half + 2, :].rearrange("p b n -> p (b n)"),
                                         start=(t == 0), stop=(t == CT - 1))
                last.then_inc(s_in, 1)
            pe.wait_ge(s_ord, HEADS * NT)
            for h in range(HEADS):
                for r in range(NT):
                    for t in range(NT):
                        last = pe.transpose(psum[:, 4 + h, N * r + P * t:N * r + P * t + P],
                                            order[:, h, t, P * r:P * r + P], k.ident_sb[:])
                last.then_inc(s_ot, 1)
            pe.wait_ge(s_xf, CT)
            W = HEADS * (2 * S + 1)
            for T in range(TT):
                out = psum[:, 6, W * T:W * T + W]
                for t in range(CT):
                    pe.matmul(out, xf[:, t, P * T:P * T + P], w_dbc[:, t, :], start=(t == 0), stop=False)
                last = pe.matmul(out, ones[:], b_dbc[:], start=False, stop=True)
            last.then_inc(s_dbc, 1)
            pe.wait_ge(s_silu, 3 * CT)
            for i in range(TT // 2):
                for a in range(2):
                    for t in range(CT):
                        last = pe.transpose(psum[:, i, C * a + P * t:C * a + P * t + P],
                                            xf[:, t, P * (2 * i + a):P * (2 * i + a) + P], k.ident_sb[:])
                last.then_inc(s_xt, 1)
            pe.wait_ge(s_rows, 3 + 2 * HEADS)
            pe.wait_ge(s_xto, TT // 2)
            pe.wait_ge(s_oto, HEADS)
            pe.wait_ge(s_so, 1)
            for h in range(HEADS):
                for b in range(B):
                    for t in range(NT):
                        last = pe.matmul(psum[0:3 * QROWS, 2 * h + b // 2, N * (b % 2):N * (b % 2) + N],
                                         rows[:, NT * b + t, h].rearrange("p q j -> p (q j)"), order[:, h, t, :],
                                         start=(t == 0), stop=(t == NT - 1))
                last.then_inc(s_rp, 1)
                for b in range(B):
                    for t in range(NT):
                        last = pe.matmul(psum[:, 4 + 2 * h + b // 2, N * (b % 2):N * (b % 2) + N],
                                         xf_t[:, NT * b + t, P * h:P * h + P], order[:, h, t, :],
                                         start=(t == 0), stop=(t == NT - 1))
                last.then_inc(s_xp, 1)
            pe.wait_ge(s_zero, 3 + HEADS)
            pe.wait_ge(s_xpo, HEADS)
            pe.wait_ge(s_parts, HEADS)

            def sum_states(i):
                pair, s = i // S, i % S
                pe.wait_ge(s_cm, i + 1)
                if pair >= 2 and s == 0:
                    pe.wait_ge(s_ys, pair - 1)
                pe.matmul(psum[:, 6 + pair % 2, :], k.ident_sb[:], prod[:, i % DEEP, :],
                          start=(s == 0), stop=(s == S - 1)).then_inc(s_acc, 1)

            def spread(i, row, bank, done):
                h, half = i // S // 2, i // S % 2
                pe.matmul(psum[:, bank + i % 2, :], select[:, row * S + i % S, :],
                          parts[:, h, BANK * half:BANK * half + BANK], start=True, stop=True).then_inc(done, 1)

            spread(0, 1, 2, s_bdt)
            spread(1, 1, 2, s_bdt)
            spread(0, 0, 0, s_bda)
            for i in range(STEPS):
                if i + 2 < STEPS:
                    pe.wait_ge(s_dtb, i + 1)
                    spread(i + 2, 1, 2, s_bdt)
                if i + 1 < STEPS:
                    if i >= 1:
                        pe.wait_ge(s_scan, i)
                    spread(i + 1, 0, 0, s_bda)
                if i >= 2:
                    pe.wait_ge(s_cm, i - 1)
                spread(i, 2, 4, s_bc)
                if i >= 2:
                    sum_states(i - 2)
            sum_states(STEPS - 2)
            sum_states(STEPS - 1)
            pe.wait_ge(s_ys, PAIRS)
            for i in range(TT // 2):
                for a in range(2):
                    for h in range(HEADS):
                        last = pe.transpose(psum[:, i, C * a + P * h:C * a + P * h + P],
                                            y_scan[:, h, P * (2 * i + a):P * (2 * i + a) + P], k.ident_sb[:])
                last.then_inc(s_yt, 1)
            pe.wait_ge(s_yto, TT // 2)
            for h in range(HEADS):
                for half in range(2):
                    for b in range(2 * half, 2 * half + 2):
                        for t in range(NT):
                            last = pe.matmul(psum[:, 4 + 2 * h + half, N * (b % 2):N * (b % 2) + N],
                                             y_t[:, NT * b + t, P * h:P * h + P], order_t[:, h, t, :],
                                             start=(t == 0), stop=(t == NT - 1))
                    last.then_inc(s_un, 1)
            for i in range(TT // 2):
                pe.wait_ge(s_y, 3 * 2 * HEADS)
                if i >= 2:
                    pe.wait_ge(s_so2, i - 1)
                    pe.wait_ge(s_t, i - 1)
                for a in range(2):
                    T = 2 * i + a
                    for t in range(CT):
                        pe.matmul(psum[:, i % 2, C * a:C * a + C], y[:, t, P * T:P * T + P], w_out[:, t, :],
                                  start=(t == 0), stop=False)
                    pe.matmul(psum[:, i % 2, C * a:C * a + C], ones[:], b_out[:], start=False, stop=True)
                    for t in range(CT):
                        last = pe.transpose(psum[:, 2 + i % 2, C * a + P * t:C * a + P * t + P],
                                            k.x1[:, t].rearrange("p b n -> p (b n)")[:, P * T:P * T + P], k.ident_sb[:])
                last.then_inc(s_op, 1)


class LayerNorm:

    def __init__(self, name, sb, sem, eps):
        self.eps = eps
        self.raw = sb(f"{name}_raw", [P, TT, 6])
        self.moments = sb(f"{name}_moments", [P, TT, 2])
        self.var = sb(f"{name}_var", [P, TT])
        self.sd = sb(f"{name}_sd", [P, TT])
        self.rstd = sb(f"{name}_rstd", [P, TT])
        self.s_raw = sem(f"{name}_raw")
        self.s_moments = sem(f"{name}_moments")
        self.s_sd = sem(f"{name}_sd")
        self.s_rstd = sem(f"{name}_rstd")
        self.s_out = sem(f"{name}_out")

    def statistics(self, dve, t):
        for T in range(TT):
            dve.bn_stats(self.raw[:, T, :], t[:, T, :]).then_inc(self.s_raw, 1)
        for T in range(TT):
            dve.wait_ge(self.s_raw, T + 1)
            last = dve.bn_aggr(self.moments[:, T, :], self.raw[:, T, :])
        last.then_inc(self.s_moments, 1)
        dve.wait_ge(self.s_moments, 1)
        dve.tensor_scalar(self.var[:], self.moments[:, :, 1], self.eps, None, ALU.add).then_inc(self.s_moments, 1)

    def deviation(self, act):
        act.wait_ge(self.s_moments, 2)
        act.activation(self.sd[:], self.var[:], ACT.Sqrt).then_inc(self.s_sd, 1)

    def normalise(self, dve, t, out):
        dve.wait_ge(self.s_sd, 1)
        dve.reciprocal(self.rstd[:], self.sd[:]).then_inc(self.s_rstd, 1)
        dve.wait_ge(self.s_rstd, 1)
        for T in range(TT):
            dve.tensor_scalar(out[:, T, :], t[:, T, :], self.moments[:, T, 0:1], self.rstd[:, T:T + 1],
                              ALU.subtract, ALU.mult).then_inc(self.s_out, 1)


COMBOS = ((0, 0), (0, 1), (0, 2), (1, 0), (1, 1), (2, 0))
STACK = len(COMBOS) * HD
MAXROWS = 2
GROUP = 8
GROUPS = B * AH // GROUP
SLOTS_G = 4


def image_and_half(g):
    return 2 * (g // 4) + g % 2, g // 2 % 2


def attention(nc, sem, sbuf, psum, k, w, causal, tag, prefetch):
    with ExitStack() as ctx:
        def sb(name, shape, dt=F32):
            return ctx.enter_context(nc.sbuf_tensor(f"{tag}_{name}", shape, dt))

        def sm(name):
            return sem(f"{tag}_{name}")

        wqkv = sb("wqkv", [P, CT, 3 * C])
        w_proj = sb("w_proj", [P, CT, C])
        b_proj = sb("b_proj", [1, C])
        ones = sb("ones_row", [1, P])
        ident16 = sb("ident16", [P, P], BF16)
        bans = sb("bans", [P, 3, P], BF16)
        h_t = k.x1[:].rearrange("p t b n -> p t (b n)")
        normed = k.h[:].rearrange("p t b n -> p (t b n)").rearrange("p (t c) -> p t c", c=C)
        rest = sb("rest", [P, 2, TOK])
        parts = sb("parts", [P, CT, 2, 3, TOK], BF16)
        stack_q = sb("stack_q", [STACK + MAXROWS, SLOTS_G, GROUP, N], BF16)
        stack_k = sb("stack_k", [STACK + MAXROWS, SLOTS_G, GROUP, N], BF16)
        values = sb("values", [P, TT, AH, 2 * HD])
        maxima = sb("maxima", [P, GROUPS, NT, GROUP])
        negated = sb("negated", [GROUP, SLOTS_G, MAXROWS, N], BF16)
        expo = sb("expo", [P, 2, 2, BANK])
        ctxn = rest[:, 0, :].rearrange("p (b t n) -> p b t n", b=2, t=CT)
        raw = rest[:, 1, :].rearrange("p (g n) -> p g n", g=2)
        inverse = sb("inverse", [P, 2, NT, GROUP])
        ctx_t = sb("ctx_t", [P, 2, NT, P])
        ln = LayerNorm(f"{tag}_ln", sb, sem, 1e-5)

        s_w = sm("weights_loaded")
        s_ones = sm("constants_set")
        s_ht = sm("h_transposed")
        s_hto = sm("h_t_out")
        s_qk = sm("qk_projected")
        s_hi = sm("high_part")
        s_r = sm("remainder")
        s_mid = sm("middle_part")
        s_lo = sm("low_part")
        s_v = sm("v_projected")
        s_vo = sm("v_out")
        s_pd = sm("parts_in_dram")
        s_st = [sm(f"stack_loaded_{i}") for i in range(SLOTS_G)]
        s_sc = sm("scores_for_max")
        s_mx = sm("maxima")
        s_mt = sm("maxima_transposed")
        s_nh = sm("negated_high")
        s_nl = sm("negated_low")
        s_mr = [sm("max_rows_even"), sm("max_rows_odd")]
        s_s2 = sm("scores_less_max")
        s_ex = sm("exponentials")
        s_av = sm("values_weighted")
        s_raw = sm("contexts_out")
        s_ct = sm("contexts_transposed")
        s_inv = sm("denominators_inverted")
        s_div = sm("contexts_divided")
        s_cb = sm("contexts_turned_back")
        s_cn = sm("contexts_ready")
        s_pj = sm("projected")
        s_res = sm("residual_added")

        UNITS = GROUP // 2
        n1 = P if causal else 0
        WIDTH = 2 * N - n1
        block = ctx.enter_context(nc.Block())

        @block.sync
        def _(sp):
            for dst, src in ((wqkv, w["wqkv"]), (w_proj, w["w_proj"]), (b_proj, w["b_proj"]), (ones, k.dram["ones"]),
                             (ident16, k.dram["ident16"]), (bans, k.dram["bans"])):
                sp.dma_start(dst[:], src).then_inc(s_w, 16)

            def load_stacks(g):
                b, half = image_and_half(g)
                for which, stack in enumerate((stack_q, stack_k)):
                    sp.dma_start(stack[0:STACK, g % SLOTS_G],
                                 k.stacks_dram[which, :, GROUP * half:GROUP * half + GROUP, N * b:N * b + N]
                                 ).then_inc(s_st[g % SLOTS_G], 16)

            for i in range(2 * CT):
                t, which = i // 2, i % 2
                for part, done in enumerate((s_hi, s_mid, s_lo)):
                    sp.wait_ge(done, i + 1)
                    for c, combo in enumerate(COMBOS):
                        if combo[which] == part:
                            sp.dma_start(k.stacks_dram[which, HD * c:HD * c + HD, GROUP * t:GROUP * t + GROUP].rearrange("d h n -> h d n"),
                                         parts[:, t, which, part]).then_inc(s_pd, 16)
                if which:
                    sp.wait_ge(s_pd, 16 * len(COMBOS) * (i + 1))
                    for g in range(2 * t, 2 * t + 2):
                        load_stacks(g)

            def max_rows(g):
                sp.wait_ge(s_nl, g + 1)
                sp.wait_ge(s_nh, g + 1)
                for q in range(MAXROWS):
                    sp.dma_start(stack_q[STACK + q:STACK + q + 1, g % SLOTS_G], negated[:, g % SLOTS_G, q, :]
                                 ).then_inc(s_mr[g % 2], 16)

            max_rows(0)
            for g in range(GROUPS - 1):
                max_rows(g + 1)
                prefetch(sp, g)
                if g >= 1 and g + 3 < GROUPS:
                    sp.wait_ge(s_s2, UNITS * g)
                    load_stacks(g + 3)

        @block.gpsimd
        def _(pool):
            pool.memset(values[:, :, :, HD:], 1.0).then_inc(s_ones, 1)
            pool.wait_ge(s_ones, 1)
            pool.memset(stack_k[STACK:, :, :, :], 1.0).then_inc(s_ones, 1)

        @block.vector
        def _(dve):
            ln.statistics(dve, k.t)
            ln.normalise(dve, k.t, normed)
            for i in range(TT // 2):
                dve.wait_ge(s_ht, i + 1)
                if i % 2:
                    dve.tensor_copy(h_t[:, :, N * i:N * i + N], psum[:, i, :].rearrange("p (t n) -> p t n", t=CT)).then_inc(s_hto, 1)
            for i in range(2 * CT):
                source = psum[:, 2 * (i % 2):2 * (i % 2) + 2, :].rearrange("p a n -> p (a n)")
                t, which = i // 2, i % 2
                dve.wait_ge(s_hi, i + 1)
                dve.tensor_tensor(rest[:, i % 2, :], source, parts[:, t, which, 0, :], ALU.subtract).then_inc(s_r, 1)
                dve.wait_ge(s_mid, i + 1)
                dve.tensor_tensor(parts[:, t, which, 2, :], rest[:, i % 2, :], parts[:, t, which, 1, :],
                                  ALU.subtract).then_inc(s_lo, 1)
            for i in range(TT // 2):
                dve.wait_ge(s_v, i + 1)
                dve.tensor_copy(values[:, 2 * i:2 * i + 2, :, 0:HD],
                                psum[:, 4 + i % 2, :].rearrange("p (a h d) -> p a h d", a=2, h=AH)).then_inc(s_vo, 1)

            def take_max(i):
                g, h = i // GROUP, i % GROUP
                dve.wait_ge(s_sc, i + 1)
                dve.tensor_reduce(maxima[:, g, :, h], psum[:, i % 2, :].rearrange("p (t m) -> p t m", t=NT),
                                  AX_X, ALU.max).then_inc(s_mx, 1)

            def negate(g):
                dve.wait_ge(s_nh, g + 1)
                dve.scalar_tensor_tensor(negated[:, g % SLOTS_G, 1, :], psum[0:GROUP, 0, 0:N], -1.0,
                                         negated[:, g % SLOTS_G, 0, :], ALU.mult, ALU.subtract).then_inc(s_nl, 1)

            def divide(g):
                turned = psum[:, 6 + g % 2, :].rearrange("p (a h d) -> p a h d", a=NT, h=GROUP)
                dve.wait_ge(s_ct, g + 1)
                dve.reciprocal(inverse[:, g % 2], turned[:, :, :, HD]).then_inc(s_inv, 1)
                dve.wait_ge(s_inv, g + 1)
                dve.tensor_tensor(ctx_t[:, g % 2].rearrange("p a (h d) -> p a h d", d=HD), turned[:, :, :, 0:HD],
                                  inverse[:, g % 2].unsqueeze(3).broadcast_to([P, NT, GROUP, HD]), ALU.mult).then_inc(s_div, 1)

            def add_residual(g):
                b, _ = image_and_half(g)
                dve.wait_ge(s_pj, b + 1)
                tile = k.t[:, NT * b:NT * b + NT, :].rearrange("p a n -> p (a n)")
                dve.tensor_tensor(tile, tile, psum[:, 6 + g % 2, :], ALU.add).then_inc(s_res, 1)

            for g in range(2):
                for h in range(GROUP):
                    take_max(GROUP * g + h)
                negate(g)
            for g in range(GROUPS):
                for unit in range(UNITS):
                    if unit == 0 and 1 <= g < GROUPS - 1:
                        negate(g + 1)
                    if unit == 0 and g >= 2 and image_and_half(g - 2)[1]:
                        add_residual(g - 2)
                    if unit == 1 and g >= 1:
                        divide(g - 1)
                    if g + 2 < GROUPS:
                        take_max(GROUP * (g + 2) + 2 * unit)
                        take_max(GROUP * (g + 2) + 2 * unit + 1)
            add_residual(GROUPS - 2)
            divide(GROUPS - 1)
            add_residual(GROUPS - 1)

        @block.scalar
        def _(act):
            ln.deviation(act)
            for i in range(0, TT // 2, 2):
                act.wait_ge(s_ht, i + 1)
                act.activation(h_t[:, :, N * i:N * i + N], psum[:, i, :].rearrange("p (t n) -> p t n", t=CT),
                               ACT.Copy).then_inc(s_hto, 1)
            for i in range(2 * CT):
                source = psum[:, 2 * (i % 2):2 * (i % 2) + 2, :].rearrange("p a n -> p (a n)")
                t, which = i // 2, i % 2
                act.wait_ge(s_qk, i + 1)
                act.activation(parts[:, t, which, 0, :], source, ACT.Copy).then_inc(s_hi, 1)
                act.wait_ge(s_r, i + 1)
                act.activation(parts[:, t, which, 1, :], rest[:, i % 2, :], ACT.Copy).then_inc(s_mid, 1)

            def negate(g):
                act.wait_ge(s_mt, g + 1)
                act.activation(negated[:, g % SLOTS_G, 0, :], psum[0:GROUP, 0, 0:N], ACT.Copy, scale=-1.0).then_inc(s_nh, 1)

            def take_contexts(g):
                act.wait_ge(s_av, UNITS * (g + 1))
                act.activation(raw[:, g % 2, :], psum[:, 6 + g % 2, :], ACT.Copy).then_inc(s_raw, 1)

            def take_back(g):
                b, half = image_and_half(g)
                act.wait_ge(s_cb, g + 1)
                act.activation(ctxn[:, b % 2, half, :], psum[:, 6 + g % 2, 0:N], ACT.Copy).then_inc(s_cn, 1)

            negate(0)
            negate(1)
            for g in range(GROUPS):
                for unit in range(UNITS):
                    i = UNITS * g + unit
                    if unit == 0 and 1 <= g < GROUPS - 1:
                        negate(g + 1)
                    act.wait_ge(s_s2, i + 1)
                    if i >= 2:
                        act.wait_ge(s_av, i - 1)
                    act.activation(expo[:, i % 2, :, 0:WIDTH], psum[:, 2 + 2 * (i % 2):4 + 2 * (i % 2), 0:WIDTH],
                                   ACT.Exp, scale=HD ** -0.5).then_inc(s_ex, 1)
                    if unit == 0 and g >= 1:
                        take_contexts(g - 1)
                    if unit == 2 and g >= 1:
                        take_back(g - 1)
            take_contexts(GROUPS - 1)
            take_back(GROUPS - 1)

        @block.tensor
        def _(pe):
            for i in range(TT // 2):
                pe.wait_ge(ln.s_out, 2 * i + 2)
                for t in range(CT):
                    for a in range(2):
                        last = pe.transpose(psum[:, i, N * t + P * a:N * t + P * a + P],
                                            normed[:, 2 * i + a, P * t:P * t + P], k.ident_sb[:])
                last.then_inc(s_ht, 1)
            pe.wait_ge(s_w, 16 * 6)
            pe.wait_ge(s_hto, TT // 2)
            for i in range(2 * CT):
                t_out, which = i // 2, i % 2
                column = C * which + P * t_out
                if i >= 2:
                    pe.wait_ge(s_r, i - 1)
                for half in range(2):
                    for t in range(CT):
                        last = pe.matmul(psum[:, 2 * (i % 2) + half, :], wqkv[:, t, column:column + P],
                                         h_t[:, t, BANK * half:BANK * half + BANK], start=(t == 0), stop=(t == CT - 1))
                last.then_inc(s_qk, 1)
            for i in range(TT // 2):
                if i >= 2:
                    pe.wait_ge(s_vo, i - 1)
                for a in range(2):
                    T = 2 * i + a
                    for t in range(CT):
                        last = pe.matmul(psum[:, 4 + i % 2, C * a:C * a + C], h_t[:, t, P * T:P * T + P],
                                         wqkv[:, t, 2 * C:], start=(t == 0), stop=(t == CT - 1))
                last.then_inc(s_v, 1)
            pe.wait_ge(s_ones, 2)
            pe.wait_ge(s_vo, TT // 2)

            def scores_for_max(i):
                g, h = i // GROUP, i % GROUP
                slot = g % SLOTS_G
                if h == 0:
                    pe.wait_ge(s_st[slot], 16 * 2 * (g // SLOTS_G + 1))
                if i >= 2:
                    pe.wait_ge(s_mx, i - 1)
                if h == 0 and g >= 1:
                    pe.wait_ge(s_nl, g)
                for t in range(NT):
                    keys = P if causal and t == 0 else N
                    out = psum[:, i % 2, N * t:N * t + keys]
                    last = pe.matmul(out, stack_q[0:STACK, slot, h, P * t:P * t + P],
                                     stack_k[0:STACK, slot, h, 0:keys], start=True, stop=not causal)
                    if causal:
                        last = pe.matmul(psum[:, i % 2, N * t + P * t:N * t + P * t + P], ident16[:], bans[:, 0, :],
                                         start=False, stop=True)
                        if t == 0:
                            pe.matmul(psum[:, i % 2, P:N], ident16[:], bans[:, 2, :], start=True, stop=True)
                last.then_inc(s_sc, 1)

            def turn_maxima(g):
                pe.wait_ge(s_mx, GROUP * (g + 1))
                for t in range(NT):
                    last = pe.transpose(psum[0:GROUP, 0, P * t:P * t + P], maxima[:, g, t, :], k.ident_sb[:])
                last.then_inc(s_mt, 1)

            def scores_less_max(i):
                g, unit = i // UNITS, i % UNITS
                slot = g % SLOTS_G
                if unit == 0:
                    pe.wait_ge(s_mr[g % 2], 16 * MAXROWS * (g // 2 + 1))
                if i >= 2:
                    pe.wait_ge(s_ex, i - 1)
                for j in range(2):
                    h, bank = 2 * unit + j, 2 + 2 * (i % 2) + j
                    for m in range(NT):
                        first = n1 if m else 0
                        col = N * m
                        last = pe.matmul(psum[:, bank, col:col + N - first],
                                         stack_k[:, slot, h, P * m:P * m + P], stack_q[:, slot, h, first:N],
                                         start=True, stop=not causal)
                        if causal:
                            last = pe.matmul(psum[:, bank, col:col + P], ident16[:], bans[:, 1, :], start=False, stop=True)
                last.then_inc(s_s2, 1)

            def weigh_values(i):
                g, unit = i // UNITS, i % UNITS
                b, half = image_and_half(g)
                pe.wait_ge(s_ex, i + 1)
                if unit == 0 and g >= 2:
                    pe.wait_ge(s_cn, g - 1)
                    image, projected = image_and_half(g - 2)
                    if projected:
                        pe.wait_ge(s_res, image + 1)
                for j in range(2):
                    h = 2 * unit + j
                    q, col = 32 * (h % 4), N * (h // 4)
                    for m in range(NT):
                        first = n1 if m else 0
                        last = pe.matmul(psum[q:q + 32, 6 + g % 2, col + first:col + N],
                                         values[:, NT * b + m, GROUP * half + h, :], expo[:, i % 2, j, N * m:N * m + N - first],
                                         start=(m == 0), stop=(m == NT - 1))
                last.then_inc(s_av, 1)

            def turn_contexts(g):
                pe.wait_ge(s_raw, g + 1)
                for a in range(NT):
                    for j in range(NT):
                        last = pe.transpose(psum[:, 6 + g % 2, N * a + P * j:N * a + P * j + P],
                                            raw[:, g % 2, N * j + P * a:N * j + P * a + P], k.ident_sb[:])
                last.then_inc(s_ct, 1)

            def turn_back(g):
                pe.wait_ge(s_div, g + 1)
                for a in range(NT):
                    last = pe.transpose(psum[:, 6 + g % 2, P * a:P * a + P], ctx_t[:, g % 2, a, :], k.ident_sb[:])
                last.then_inc(s_cb, 1)

            def project(g):
                b, _ = image_and_half(g)
                pe.wait_ge(s_cn, g + 1)
                for a in range(NT):
                    out = psum[:, 6 + g % 2, C * a:C * a + C]
                    for t in range(CT):
                        pe.matmul(out, ctxn[:, b % 2, t, P * a:P * a + P], w_proj[:, t, :], start=(t == 0), stop=False)
                    last = pe.matmul(out, ones[:], b_proj[:], start=False, stop=True)
                last.then_inc(s_pj, 1)

            for g in range(2):
                for h in range(GROUP):
                    scores_for_max(GROUP * g + h)
                turn_maxima(g)
            for g in range(GROUPS):
                for unit in range(UNITS):
                    i = UNITS * g + unit
                    scores_less_max(i)
                    if unit == 0 and 1 <= g < GROUPS - 1:
                        turn_maxima(g + 1)
                    if i:
                        weigh_values(i - 1)
                    if unit == 1 and g >= 1:
                        turn_contexts(g - 1)
                    if unit == 2 and g >= 1:
                        turn_back(g - 1)
                    if unit == 3 and g >= 1 and image_and_half(g - 1)[1]:
                        project(g - 1)
                    if g + 2 < GROUPS:
                        scores_for_max(GROUP * (g + 2) + 2 * unit)
                        scores_for_max(GROUP * (g + 2) + 2 * unit + 1)
            weigh_values(UNITS * GROUPS - 1)
            turn_contexts(GROUPS - 1)
            turn_back(GROUPS - 1)
            project(GROUPS - 1)


CHUNK = 512
CHUNK_COLS = 2 * CT * CHUNK + CHUNK // P * C
RING_CHUNKS = 6
PAIRED = (MAXBLK + 1) // 2 * 2


def above_zero(count):
    return not isinstance(count, int) or count > 0


def load_chunk(sp, k, weights, chunks, n, loaded):
    place = CHUNK_COLS * (n % RING_CHUNKS)
    column = CHUNK_COLS * (n % chunks)
    sp.dma_start(k.ring[:, place:place + CHUNK_COLS], weights[n // chunks, :, column:column + CHUNK_COLS]).then_inc(loaded, 16)


def experts_ffn(nc, sem, sbuf, psum, k, w, chunks, s_loaded, tag, finish=None):
    RING_EXPERTS = RING_CHUNKS // chunks
    with ExitStack() as ctx:
        def sb(name, shape, dt=F32):
            return ctx.enter_context(nc.sbuf_tensor(f"{tag}_{name}", shape, dt))

        def sm(name):
            return sem(f"{tag}_{name}")

        gate_w = sb("gate_w", [P, CT, E])
        iota_e = sb("iota_e", [P, E])
        iota_b = sb("iota_b", [P, PAIRED])
        steps = sb("steps", [P, TT])
        earlier = sb("earlier", [P, 2, P], BF16)
        h_t = k.x1[:].rearrange("p t b n -> p t (b n)")
        normed = k.h[:].rearrange("p t b n -> p (t b n)").rearrange("p (t c) -> p t c", c=C)
        logits = sb("logits", [P, TT, E])
        top = sb("top", [P, TT, E])
        top_at = sb("top_at", [P, TT, E], U32)
        choice = sb("choice", [P, TT, 2])
        chosen = sb("chosen", [P, 2, TT, E])
        either = sb("either", [P, TT, E], BF16)
        share = sb("share", [P, 4, TT])
        count = sb("count", [P, E])
        over = sb("over", [P, E, TT])
        blocks = sb("blocks", [P, E])
        block_end = sb("block_end", [P, E])
        unit = sb("unit", [P, E])
        base = sb("base", [P, E])
        place = sb("place", [P, TT, E])
        taken = sb("taken", [P, 2, TT, E])
        slot = sb("slot", [P, 2, TT])
        edges = sb("edges", [P, PAIRED + 1])
        iota_p = sb("iota_p", [P, P])
        labels = sb("labels", [P, 2, TT, 2])
        behind = sb("behind", [P, 2, TT, PAIRED + 1])
        in_block = sb("in_block", [P, 2, TT, PAIRED])
        at_row = sb("at_row", [P, 2, TT])
        row_hot = sb("row_hot", [P, 2, TT, P], BF16)
        label_hot = sb("label_hot", [P, 2, TT, 2, PAIRED], BF16)
        unused = sb("unused", [P, PAIRED])
        number = sb("number", [P, PAIRED])
        own_slot = sb("own_slot", [P, PAIRED])
        from_row = sb("from_row", [P, PAIRED], U32)
        to_row = sb("to_row", [P, PAIRED], U32)
        past = sb("past", [P, PAIRED, E])
        expert = sb("expert", [P, 3, PAIRED])
        table = sb("table", [P, 2, PAIRED], I32)
        free_at = sb("free_at", [P, E], I32)
        from_now = sb("from_now", [P, 2], U32)
        to_now = sb("to_now", [P, 2], U32)
        xs = sb("xs", [P, 2, C])
        x_t = sb("x_t", [P, 2, CT, P])
        silu = sb("silu", [P, 2, CHUNK])
        gated = sb("gated", [P, 2, CHUNK])
        gated_t = sb("gated_t", [P, 2, CHUNK])
        y = sb("y", [P, 2, C])
        got = k.ring[:, 0:2 * TT * C].rearrange("p (t k c) -> p t k c", t=TT, k=2)
        ln = LayerNorm(f"{tag}_ln", sb, sem, 1e-5)

        s_w = sm("weights_loaded")
        s_ht = sm("h_transposed")
        s_hto = sm("h_t_out")
        s_lg = sm("logits")
        s_r = sm("router_steps")
        s_exp = sm("router_exp")
        s_rank = sm("ranks_and_counts")
        s_hot = sm("one_hot_rows")
        s_turn = sm("slots_turned_around")
        s_slot = sm("slots_ready")
        s_table = sm("table_ready")
        s_nd = sm("rows_in_dram")
        s_fn = sm("from_now_set")
        s_tn = sm("to_now_set")
        s_x = [sm("x_loaded_even"), sm("x_loaded_odd")]
        s_xt = sm("x_transposed")
        s_xto = sm("x_t_out")
        s_up = sm("up_products")
        s_si = sm("silu")
        s_g = sm("gated")
        s_gt = sm("gated_transposed")
        s_gto = sm("gated_t_out")
        s_dn = sm("down_products")
        s_y = sm("y_out")
        s_yd = [sm("y_stored_even"), sm("y_stored_odd")]
        s_got = [sm(f"results_gathered_{i}") for i in range(4)]
        s_t = sm("tokens_updated")
        s_ft = sm("final_transposed")
        s_fo = sm("final_out")
        s_st = sm("output_stored")

        X_BANK, Y_BANK, G_BANK = 7, 6, 4
        block = ctx.enter_context(nc.Block())
        PAIRS = (MAXBLK - 1) // 2
        assert MAXBLK % 2 == 1

        @block.sync
        def _(sp):
            for dst, src in ((gate_w, w["gate"]), (iota_e, k.dram["iota_e"]), (iota_b, k.dram["iota_b"]), (steps, k.dram["steps"]),
                             (earlier, k.dram["earlier"]), (edges, k.dram["edges"]), (iota_p, k.dram["iota_p"]),
                             (labels, k.dram["labels"]), (own_slot, k.dram["own_slot"])):
                sp.dma_start(dst[:], src).then_inc(s_w, 16)
            sp.wait_ge(ln.s_out, TT)
            for c in range(2):
                sp.dma_start(k.rows_in[0:2 * TOK].rearrange("(t k p) c -> k p t c", k=2, p=P)[c], normed).then_inc(s_nd, 16)
            sp.wait_ge(s_table, 1)
            for e in range(RING_EXPERTS, E):
                done = sp.value_load(free_at[0:1, e - RING_EXPERTS:e - RING_EXPERTS + 1], min_val=1, max_val=MAXBLK)
                sp.wait_ge(s_loaded, 16 * chunks * e)
                sp.wait_ge(s_y, done)
                for n in range(chunks * e, chunks * e + chunks):
                    load_chunk(sp, k, w["experts"], chunks, n, s_loaded)
            sp.wait_ge(s_yd[0], 16 * (MAXBLK + 1) // 2)
            sp.wait_ge(s_yd[1], 16 * (MAXBLK // 2))
            for i in range(TT // 2):
                sp.dma_start(got[:, 2 * i:2 * i + 2],
                             k.rows_out[4 * P * i:4 * P * i + 4 * P].rearrange("(t k p) c -> p t k c", k=2, p=P)).then_inc(s_got[i], 16)
            if finish is not None:
                for i in range(TT // 2):
                    sp.wait_ge(s_fo, i + 1)
                    sp.dma_start(finish[i], k.x1[:, :, i, :]).then_inc(s_st, 16)
                sp.wait_ge(s_st, 16 * TT // 2)

        @block.gpsimd
        def _(pool):
            pool.wait_ge(s_slot, 1)
            pool.wait_ge(s_nd, 32)

            def load_x(j, odd, turned=None):
                if turned is not None:
                    pool.wait_ge(s_xt, turned)
                pool.tensor_copy(from_now[:, odd:odd + 1], from_row[:, bass.ds(j, 1)]).then_inc(s_fn, 1)
                pool.wait_ge(s_fn, j + 1)
                pool.nop(nofuse=True)
                pool.indirect_dma_start(out=xs[:, odd, :], out_offset=None, in_=k.rows_in,
                                        in_offset=bass.IndirectOffsetOnAxis(ap=from_now[:, odd:odd + 1], axis=0)
                                        ).then_inc(s_x[odd], 16)

            def store_y(j, odd):
                pool.wait_ge(s_y, j + 1)
                pool.tensor_copy(to_now[:, odd:odd + 1], to_row[:, bass.ds(j, 1)]).then_inc(s_tn, 1)
                pool.wait_ge(s_tn, j + 1)
                pool.nop(nofuse=True)
                pool.indirect_dma_start(out=k.rows_out, out_offset=bass.IndirectOffsetOnAxis(ap=to_now[:, odd:odd + 1], axis=0),
                                        in_=y[:, odd, :], in_offset=None).then_inc(s_yd[odd], 16)

            load_x(0, 0)
            load_x(1, 1)
            for j in (2, 3):
                load_x(j, j % 2, j - 1)

            def turn(i, more=True):
                for odd in (1, 0):
                    j = 2 * i + (1 if odd else 2)
                    if more:
                        load_x(j + 3, 1 - odd, j + 2)
                    store_y(j - 1, 1 - odd)

            turn(0)
            with pool.Fori(1, PAIRS - 1) as i:
                turn(i)
            turn(PAIRS - 1, more=False)
            store_y(MAXBLK - 1, 0)

        @block.vector
        def _(dve):
            ln.statistics(dve, k.t)
            ln.normalise(dve, k.t, normed)
            for i in range(1, TT // 2, 2):
                dve.wait_ge(s_ht, i + 1)
                dve.tensor_copy(h_t[:, :, N * i:N * i + N], psum[:, i, :].rearrange("p (t n) -> p t n", t=CT)).then_inc(s_hto, 1)
            n = 0

            def step(ins):
                nonlocal n
                n += 1
                ins.then_inc(s_r, 1)
                dve.wait_ge(s_r, n)

            dve.wait_ge(s_lg, 1)
            step(dve.tensor_copy(logits[:].rearrange("p t e -> p (t e)"), psum[:, 4, 0:TT * E]))
            for T in range(TT):
                last = dve.max(top[:, T, :], logits[:, T, :])
            step(last)
            for T in range(TT):
                last = dve.max_index(top_at[:, T, :], top[:, T, :], logits[:, T, :])
            step(last)
            step(dve.tensor_tensor(share[:, 0, :], top[:, :, 1], top[:, :, 0], ALU.subtract))
            step(dve.tensor_copy(choice[:], top_at[:, :, 0:2]))
            every = [P, TT, E]
            for c in range(2):
                step(dve.tensor_tensor(chosen[:, c], iota_e[:].unsqueeze(1).broadcast_to(every),
                                       choice[:, :, c].unsqueeze(2).broadcast_to(every), ALU.is_equal))
            step(dve.tensor_tensor(either[:], chosen[:, 0], chosen[:, 1], ALU.add))
            dve.wait_ge(s_exp, 1)
            step(dve.tensor_scalar(share[:, 1, :], share[:, 0, :], 1.0, None, ALU.add))
            step(dve.reciprocal(share[:, 2, :], share[:, 1, :]))
            step(dve.tensor_tensor(share[:, 3, :], share[:, 0, :], share[:, 2, :], ALU.mult))
            dve.wait_ge(s_rank, 1)
            step(dve.tensor_copy(count[:], psum[:, 6, 0:E]))
            wide = [P, E, TT]
            step(dve.tensor_tensor(over[:], count[:].unsqueeze(2).broadcast_to(wide),
                                   steps[:].unsqueeze(1).broadcast_to(wide), ALU.is_gt))
            step(dve.tensor_reduce(blocks[:], over[:], AX_X, ALU.add))
            step(dve.tensor_scalar(blocks[:], blocks[:], 1.0, None, ALU.max))
            step(dve.memset(unit[:], 1.0))
            step(dve.tensor_tensor_scan(block_end[:], unit[:], blocks[:], 0.0, ALU.mult, ALU.add))
            step(dve.tensor_tensor(base[:], block_end[:], blocks[:], ALU.subtract))
            step(dve.tensor_scalar(base[:], base[:], float(P), None, ALU.mult))
            step(dve.tensor_tensor(place[:], psum[:, 5, 0:TT * E].rearrange("p (t e) -> p t e", t=TT),
                                   base[:].unsqueeze(1).broadcast_to(every), ALU.add))
            for c in range(2):
                step(dve.tensor_tensor(taken[:, c], place[:], chosen[:, c], ALU.mult))
            step(dve.tensor_reduce(slot[:].rearrange("p c t -> p (c t)"), taken[:].rearrange("p c t e -> p (c t) e"),
                                   AX_X, ALU.add))
            dve.wait_ge(s_w, 16 * 9)
            flat = "p c t b -> p (c t) b"
            many = slot[:].rearrange("p c t -> p (c t)").unsqueeze(2)
            step(dve.tensor_tensor(behind[:].rearrange(flat), many.broadcast_to([P, 2 * TT, PAIRED + 1]),
                                   edges[:].unsqueeze(1).broadcast_to([P, 2 * TT, PAIRED + 1]), ALU.is_ge))
            step(dve.tensor_tensor(in_block[:], behind[:, :, :, 0:PAIRED], behind[:, :, :, 1:], ALU.subtract))
            step(dve.tensor_reduce(at_row[:].rearrange("p c t -> p (c t)"), behind[:, :, :, 1:].rearrange(flat), AX_X, ALU.add))
            step(dve.scalar_tensor_tensor(at_row[:], at_row[:], float(-P), slot[:], ALU.mult, ALU.add))
            for c in range(2):
                for value in range(2):
                    dve.tensor_tensor(label_hot[:, c, :, value, :], in_block[:, c],
                                      labels[:, c, :, value].unsqueeze(2).broadcast_to([P, TT, PAIRED]), ALU.mult).then_inc(s_hot, 1)
            for c in range(2):
                dve.tensor_tensor(row_hot[:, c], iota_p[:].unsqueeze(1).broadcast_to([P, TT, P]),
                                  at_row[:, c].unsqueeze(2).broadcast_to([P, TT, P]), ALU.is_equal).then_inc(s_hot, 1)
            dve.wait_ge(s_turn, 1)
            tile_of, token_of = psum[:, 7, 0:PAIRED], psum[:, 7, PAIRED:2 * PAIRED]
            step(dve.tensor_copy(number[:], token_of))
            step(dve.scalar_tensor_tensor(unused[:], tile_of, 1.0, own_slot[:], ALU.is_lt, ALU.mult))
            step(dve.scalar_tensor_tensor(number[:], tile_of, float(P), number[:], ALU.mult, ALU.add))
            step(dve.tensor_scalar(from_row[:], number[:], float(-P), 0.0, ALU.add, ALU.max))
            dve.scalar_tensor_tensor(to_row[:], number[:], float(-P), unused[:], ALU.add, ALU.add).then_inc(s_slot, 1)
            wide = [P, PAIRED, E]
            step(dve.tensor_tensor(past[:], block_end[:].unsqueeze(1).broadcast_to(wide),
                                   iota_b[:].unsqueeze(2).broadcast_to(wide), ALU.is_le))
            step(dve.tensor_reduce(expert[:, 0, :], past[:], AX_X, ALU.add))
            step(dve.tensor_scalar(expert[:, 0, :], expert[:, 0, :], float(E - 1), None, ALU.min))
            step(dve.tensor_scalar(expert[:, 1, :], expert[:, 0, :], float(RING_EXPERTS), float(-RING_EXPERTS),
                                   ALU.is_ge, ALU.mult))
            step(dve.tensor_tensor(expert[:, 1, :], expert[:, 0, :], expert[:, 1, :], ALU.add))
            for turn in range(2, (E - 1) // RING_EXPERTS + 1):
                step(dve.tensor_scalar(expert[:, 2, :], expert[:, 0, :], float(turn * RING_EXPERTS),
                                       float(-RING_EXPERTS), ALU.is_ge, ALU.mult))
                step(dve.tensor_tensor(expert[:, 1, :], expert[:, 1, :], expert[:, 2, :], ALU.add))
            step(dve.tensor_scalar(table[:, 0, :], expert[:, 1, :], float(chunks * CHUNK_COLS), None, ALU.mult))
            step(dve.tensor_scalar(expert[:, 2, :], expert[:, 0, :], 1.0, float(RING_EXPERTS), ALU.add, ALU.max))
            step(dve.tensor_scalar(table[:, 1, :], expert[:, 2, :], 16.0 * chunks, None, ALU.mult))
            dve.tensor_copy(free_at[:], block_end[:]).then_inc(s_table, 1)

            def gate(q, b):
                dve.wait_ge(s_up, 2 * q + 2)
                dve.wait_ge(s_si, q + 1)
                dve.tensor_tensor(gated[:, b, :], silu[:, b, :], psum[:, 2 * b + 1, :], ALU.mult).then_inc(s_g, 1)

            def take_x(j, b):
                loads = dve.value_load(table[0:1, 1, bass.ds(j, 1)], min_val=16 * chunks, max_val=16 * chunks * E)
                dve.wait_ge(s_loaded, loads)
                dve.wait_ge(s_xt, j + 1)
                dve.tensor_copy(x_t[:, b].rearrange("p t n -> p (t n)"), psum[:, X_BANK, 0:C]).then_inc(s_xto, 1)

            def take_y(j, b, stored):
                dve.wait_ge(s_dn, chunks * (j + 1))
                if above_zero(stored):
                    dve.wait_ge(s_yd[b], stored)
                dve.tensor_copy(y[:, b, :], psum[:, Y_BANK, 0:C]).then_inc(s_y, 1)

            dve.wait_ge(s_table, 1)
            take_x(0, 0)
            if chunks == 2:
                gate(0, 0)
            gate(chunks - 1, chunks - 1)
            take_x(1, 1)
            def turn(i):
                for odd in (1, 0):
                    j = 2 * i + (1 if odd else 2)
                    if chunks == 2:
                        gate(2 * j, 0)
                        take_y(j - 1, 1 - odd, 16 * i)
                        gate(2 * j + 1, 1)
                        take_x(j + 1, 1 - odd)
                    else:
                        gate(j, odd)
                        take_x(j + 1, 1 - odd)
                        take_y(j - 1, 1 - odd, 16 * i)

            turn(0)
            with dve.Fori(1, PAIRS) as i:
                turn(i)
            take_y(MAXBLK - 1, 0, 16 * PAIRS)
            for T in range(TT):
                for c in range(2):
                    dve.wait_ge(s_got[T // 2], 16)
                    if c:
                        dve.wait_ge(s_t, 2 * T + 1)
                    dve.scalar_tensor_tensor(k.t[:, T, :], got[:, T, c, :], share[:, 2 + c, T:T + 1], k.t[:, T, :],
                                             ALU.mult, ALU.add).then_inc(s_t, 1)

        @block.scalar
        def _(act):
            ln.deviation(act)
            for i in range(0, TT // 2, 2):
                act.wait_ge(s_ht, i + 1)
                act.activation(h_t[:, :, N * i:N * i + N], psum[:, i, :].rearrange("p (t n) -> p t n", t=CT),
                               ACT.Copy).then_inc(s_hto, 1)
            act.wait_ge(s_r, 4)
            act.activation(share[:, 0, :], share[:, 0, :], ACT.Exp).then_inc(s_exp, 1)

            def silu_of(q, b):
                act.wait_ge(s_up, 2 * q + 1)
                act.activation(silu[:, b, :], psum[:, 2 * b, :], ACT.Silu).then_inc(s_si, 1)

            def take_gated(q, b):
                act.wait_ge(s_gt, q + 1)
                act.activation(gated_t[:, b, :], psum[:, G_BANK + b, :], ACT.Copy).then_inc(s_gto, 1)

            silu_of(0, 0)
            if chunks == 2:
                take_gated(0, 0)
                silu_of(1, 1)
            def turn(i):
                for odd in (1, 0):
                    j = 2 * i + (1 if odd else 2)
                    for c in range(chunks):
                        b = c if chunks == 2 else odd
                        take_gated(chunks * j + c - 1, 1 - b)
                        silu_of(chunks * j + c, b)

            turn(0)
            with act.Fori(1, PAIRS) as i:
                turn(i)
            take_gated(chunks * MAXBLK - 1, chunks - 1)
            if finish is not None:
                for i in range(TT // 2):
                    act.wait_ge(s_ft, i + 1)
                    act.activation(k.x1[:, :, i, :], psum[:, i, :].rearrange("p (t n) -> p t n", t=CT), ACT.Copy).then_inc(s_fo, 1)

        @block.tensor
        def _(pe):
            for i in range(TT // 2):
                pe.wait_ge(ln.s_out, 2 * i + 2)
                for t in range(CT):
                    for a in range(2):
                        last = pe.transpose(psum[:, i, N * t + P * a:N * t + P * a + P],
                                            normed[:, 2 * i + a, P * t:P * t + P], k.ident_sb[:])
                last.then_inc(s_ht, 1)
            pe.wait_ge(s_w, 16 * 9)
            pe.wait_ge(s_hto, TT // 2)
            for T in range(TT):
                for t in range(CT):
                    last = pe.matmul(psum[:, 4, E * T:E * T + E], h_t[:, t, P * T:P * T + P], gate_w[:, t, :],
                                     start=(t == 0), stop=(t == CT - 1))
            last.then_inc(s_lg, 1)
            pe.wait_ge(s_r, 8)
            ranks = psum[:, 5, 0:TT * E]
            pe.matmul(ranks, earlier[:, 0, :], either[:].rearrange("p t e -> p (t e)"), start=True, stop=False)
            for T in range(TT - 1):
                pe.matmul(ranks[:, E * (T + 1):].rearrange("p (t e) -> p t e", e=E), earlier[:, 1, :],
                          either[:, T:T + 1, :].broadcast_to([P, TT - 1 - T, E]), start=False, stop=(T == TT - 2))
            for T in range(TT):
                last = pe.matmul(psum[:, 6, 0:E], earlier[:, 1, :], either[:, T, :], start=(T == 0), stop=(T == TT - 1))
            last.then_inc(s_rank, 1)
            for c in range(2):
                pe.wait_ge(s_hot, 5 + c)
                for T in range(TT):
                    last = pe.matmul(psum[:, 7, 0:2 * PAIRED], row_hot[:, c, T, :], label_hot[:, c, T].rearrange("p l b -> p (l b)"),
                                     start=(c == 0 and T == 0), stop=(c == 1 and T == TT - 1))
            last.then_inc(s_turn, 1)
            pe.wait_ge(s_table, 1)

            def turn_x(j, b, loads):
                pe.wait_ge(s_x[b], loads)
                if above_zero(j):
                    pe.wait_ge(s_xto, j)
                for t in range(CT):
                    last = pe.transpose(psum[:, X_BANK, P * t:P * t + P], xs[:, b, P * t:P * t + P], k.ident_sb[:])
                last.then_inc(s_xt, 1)

            def up(q, xb, b, at, c):
                for side in range(2):
                    for t in range(CT):
                        start = CHUNK_COLS * c + CHUNK * (CT * side + t)
                        last = pe.matmul(psum[:, 2 * b + side, :], x_t[:, xb, t, :],
                                         k.ring[:, bass.ds(at + start, CHUNK)], start=(t == 0), stop=(t == CT - 1))
                    last.then_inc(s_up, 1)

            def turn_gated(q, b):
                pe.wait_ge(s_g, q + 1)
                for a in range(CHUNK // P):
                    last = pe.transpose(psum[:, G_BANK + b, P * a:P * a + P], gated[:, b, P * a:P * a + P], k.ident_sb[:])
                last.then_inc(s_gt, 1)

            def down(q, b, at, c):
                pe.wait_ge(s_gto, q + 1)
                for a in range(CHUNK // P):
                    start = CHUNK_COLS * c + 2 * CT * CHUNK + C * a
                    last = pe.matmul(psum[:, Y_BANK, 0:C], gated_t[:, b, P * a:P * a + P],
                                     k.ring[:, bass.ds(at + start, C)], start=(c == 0 and a == 0),
                                     stop=(c == chunks - 1 and a == CHUNK // P - 1))
                last.then_inc(s_dn, 1)

            def ring_column(j):
                return pe.value_load(table[0:1, 0, bass.ds(j, 1)], min_val=0,
                                     max_val=(RING_EXPERTS - 1) * chunks * CHUNK_COLS)

            pe.wait_ge(s_slot, 1)
            at = ring_column(0)
            turn_x(0, 0, 16)
            pe.wait_ge(s_xto, 1)
            up(0, 0, 0, at, 0)
            if chunks == 2:
                turn_gated(0, 0)
                up(1, 0, 1, at, 1)
            turn_x(1, 1, 16)
            if chunks == 2:
                down(0, 0, at, 0)

            def turn(i):
                at = ring_column(2 * i)
                for odd in (1, 0):
                    j = 2 * i + (1 if odd else 2)
                    at_before, at = at, ring_column(j)
                    for c in range(chunks):
                        b = c if chunks == 2 else odd
                        q = chunks * j + c
                        turn_gated(q - 1, 1 - b)
                        if c == 0:
                            pe.wait_ge(s_xto, j + 1)
                        up(q, odd, b, at, c)
                        if c == chunks - 1:
                            turn_x(j + 1, 1 - odd, 16 * (i + 2))
                            before = j if chunks == 2 else j - 1
                            if above_zero(before):
                                pe.wait_ge(s_y, before)
                        if c == 0:
                            down(q - 1, 1 - b, at_before, chunks - 1)
                        else:
                            down(q - 1, 1 - b, at, c - 1)

            turn(0)
            with pe.Fori(1, PAIRS) as i:
                turn(i)
            at = ring_column(MAXBLK - 1)
            turn_gated(chunks * MAXBLK - 1, chunks - 1)
            pe.wait_ge(s_y, MAXBLK - 1)
            down(chunks * MAXBLK - 1, chunks - 1, at, chunks - 1)
            if finish is not None:
                for i in range(TT // 2):
                    pe.wait_ge(s_t, 4 * (i + 1))
                    for t in range(CT):
                        for a in range(2):
                            last = pe.transpose(psum[:, i, N * t + P * a:N * t + P * a + P],
                                                k.t[:, 2 * i + a, P * t:P * t + P], k.ident_sb[:])
                    last.then_inc(s_ft, 1)



class Shared:
    pass


def _host_arrays(inputs):
    bf16 = mybir.dt.np(BF16)
    f = {n: np.asarray(a) for n, a in inputs.items()}
    a = {}

    def tiles(m, rows=P):
        return np.ascontiguousarray(m.reshape((m.shape[0] // rows, rows) + m.shape[1:]).swapaxes(0, 1))

    def per_image(v):
        return np.repeat(v[..., None], B, axis=-1)

    a["x"] = np.ascontiguousarray(f["x"].reshape(B, CT, P, N).transpose(2, 1, 0, 3))
    a["w1"] = np.tile(tiles(f["L0_conv_w1"].reshape(CB, C).T), (1, 1, 2))
    w_off = f["L0_conv_w_off"].reshape(27, CB, 3, 3).transpose(2, 1, 3, 0)
    a["w_off"] = np.stack([np.concatenate([w_off[0], w_off[1]]), np.concatenate([w_off[2], np.zeros_like(w_off[2])])], 1)
    a["b_off"] = np.tile(f["L0_conv_b_off"].reshape(1, 27), (P, 1))
    w2 = f["L0_conv_w2"].reshape(CB, CB, TAPS).transpose(1, 2, 0).reshape(CB, TAPS * CB)
    a["w2"] = np.concatenate([w2, np.zeros_like(w2)])
    w3 = f["L0_conv_w3"].reshape(C, CB).T
    a["w3"] = np.stack([np.concatenate([w3, np.zeros_like(w3)]), np.concatenate([np.zeros_like(w3), w3])], 1)
    gn64 = per_image(np.stack([f["L0_conv_" + n] for n in ("gn1_scale", "gn1_bias", "gn2_scale", "gn2_bias")], 1))
    a["gn64"] = np.concatenate([gn64, gn64])
    a["gn256"] = np.stack([per_image(tiles(f["L0_conv_" + n])).reshape(P, CT * B) for n in ("gn3_scale", "gn3_bias")], 1)
    a["ident"] = np.eye(P, dtype=np.float32)
    a["pair"] = np.kron(np.eye(P // 2), np.full((2, 2), 0.5)).astype(np.float32)
    a["avg8"] = np.kron(np.eye(P // 8), np.full((8, 8), 0.125)).astype(np.float32)
    n = np.arange(N).reshape(NT, P)
    taps = np.arange(TAPS)
    gx = (n % HW)[:, :, None] + taps % 3 - 1
    gy = (n // HW)[:, :, None] + taps // 3 - 1
    grid = np.concatenate([gx, gy], -1).transpose(1, 0, 2)
    a["grid"] = np.tile(grid, (1, B, 1)).astype(np.float32)
    a["iota"] = np.tile(np.arange(HW, dtype=np.float32), (P, 1))
    a["ones"] = np.ones((1, P), np.float32)

    l1 = {n[8:]: m for n, m in f.items() if n.startswith("L1_conv_")}
    a["w_in"] = tiles(l1["in_proj_w"].T)
    a["b_in"] = tiles(l1["in_proj_b"])
    a["dw"] = tiles(np.concatenate([l1["dw_w"].reshape(C, 3), l1["dw_b"].reshape(C, 1)], 1))
    a["w_dbc"] = tiles(l1["dbc_w"].T)
    a["b_dbc"] = l1["dbc_b"].reshape(1, -1)
    for name, key in (("a_log", "A_log"), ("d_skip", "Dparam")):
        a[name] = np.tile(l1[key].reshape(1, -1), (P, 1))
    a["mobius"] = np.tile(l1["mobius"].reshape(1, HEADS, 4), (P, 1, 1))
    a["w_out"] = tiles(l1["out_proj_w"].T)
    a["b_out"] = l1["out_proj_b"].reshape(1, C)
    side = np.linspace(-1.0, 1.0, HW, dtype=np.float32)
    points = np.stack([np.tile(side, HW), np.repeat(side, HW)])
    own = points.reshape(2, NT, P).transpose(2, 0, 1)
    a["z"] = np.concatenate([np.tile(points, (P, 1, 1)), own], -1)
    a["before"] = (np.arange(N) < n.T[:, :, None]).astype(np.float32)
    a["iota_n"] = np.tile(np.arange(N, dtype=np.float32), (P, 1))
    order = np.arange(P)
    forbid = np.float32(-1e30)
    above = np.where(order[None, :] > order[:, None], forbid, 0.0)
    a["bans"] = np.stack([above, above.T, np.full((P, P), forbid)], 1).astype(bf16)
    a["ident16"] = np.eye(P).astype(bf16)

    a["a2_wqkv"] = tiles(f["L2_attn_w_qkv"])
    a["a2_w_proj"] = tiles(f["L2_attn_w_proj"])
    a["a2_b_proj"] = f["L2_attn_b_proj"].reshape(1, C)
    a["a3_wqkv"] = tiles(np.concatenate([f["L3_attn_" + n] for n in ("Wq", "Wk", "Wv")], 1))
    a["a3_w_proj"] = tiles(f["L3_attn_Wo"])
    a["a3_b_proj"] = f["L3_attn_bo"].reshape(1, C)

    def experts(first, second, last):
        def cols(m, c, part):
            m = m[:, :, CHUNK * c:CHUNK * c + CHUNK] if part < 2 else m[:, CHUNK * c:CHUNK * c + CHUNK, :]
            return m.reshape(E, m.shape[1] // P, P, m.shape[2]).transpose(0, 2, 1, 3).reshape(E, P, -1)

        chunks = first.shape[2] // CHUNK
        return np.concatenate([cols(m, c, part) for c in range(chunks) for part, m in enumerate((first, second, last))], -1)

    a["f2_gate"] = tiles(f["L2_ffn_gate_w"].T)
    a["f2_experts"] = experts(*(f["L2_ffn_" + n].transpose(0, 2, 1) for n in ("w1", "w3", "w2")))
    a["f3_gate"] = tiles(f["L3_ffn_Wg"])
    a["f3_experts"] = experts(*(f["L3_ffn_" + n] for n in ("W1", "W2", "W3")))
    a["iota_e"] = np.tile(np.arange(E, dtype=np.float32), (P, 1))
    a["iota_b"] = np.tile(np.arange(PAIRED, dtype=np.float32), (P, 1))
    a["edges"] = np.tile(np.arange(0, (PAIRED + 1) * P, P, dtype=np.float32), (P, 1))
    a["iota_p"] = np.tile(np.arange(P, dtype=np.float32), (P, 1))
    tile_and_choice = 1 + 2 * np.arange(TT)[None, :] + np.arange(2)[:, None]
    a["labels"] = np.stack([np.tile(tile_and_choice, (P, 1, 1)), np.tile(np.arange(P)[:, None, None], (1, 2, TT))],
                           -1).astype(np.float32)
    a["own_slot"] = (2 * TOK + P + np.arange(PAIRED * P).reshape(PAIRED, P).T).astype(np.float32)
    a["steps"] = np.tile(np.arange(0, TOK, P, dtype=np.float32), (P, 1))
    a["earlier"] = np.stack([order[:, None] < order[None, :], np.ones((P, P))], 1).astype(bf16)
    rows = np.arange(96)[:, None]
    a["select"] = np.repeat((rows % 32 == np.arange(3 * S))[:, :, None], P, 2).astype(bf16)
    return {n: np.ascontiguousarray(m) for n, m in a.items()}


def build(nc, k, out):
    with ExitStack() as ctx:
        def sem(name):
            return ctx.enter_context(nc.semaphore(name))

        def sb(name, shape, dt=F32):
            return ctx.enter_context(nc.sbuf_tensor(name, shape, dt))

        psum = ctx.enter_context(nc.psum_tensor("psum", [P, 8, BANK], F32))
        k.ident_sb = sb("ident_sb", [P, P])
        k.avg8_sb = sb("avg8_sb", [P, P])
        k.x1 = sb("x1", [P, CT, B, N])
        k.h = sb("h", [P, CT, B, N])
        k.t = sb("t", [P, TT, C])
        k.ring = sb("ring", [P, RING_CHUNKS * CHUNK_COLS])
        k.ring_late = k.ring[:, RING_CHUNKS // 2 * CHUNK_COLS:]
        k.stacks_dram = nc.dram_tensor("stacks_dram", (2, STACK, AH, TOK), BF16, kind="Internal").ap()
        k.rows_in = nc.dram_tensor("rows_in", (2 * TOK, C), F32, kind="Internal").ap()
        k.rows_out = nc.dram_tensor("rows_out", (2 * TOK + PAIRED * P, C), F32, kind="Internal").ap()
        k.s_ring2 = sem("layer_2_experts_loaded")
        k.s_ring3 = sem("layer_3_experts_loaded")
        a2 = dict(wqkv=k.dram["a2_wqkv"], w_proj=k.dram["a2_w_proj"], b_proj=k.dram["a2_b_proj"])
        a3 = dict(wqkv=k.dram["a3_wqkv"], w_proj=k.dram["a3_w_proj"], b_proj=k.dram["a3_b_proj"])
        f2 = dict(gate=k.dram["f2_gate"], experts=k.dram["f2_experts"])
        f3 = dict(gate=k.dram["f3_gate"], experts=k.dram["f3_experts"])
        stores = [out[b].rearrange("(t p) y x -> p t (y x)", p=P) for b in range(B)]

        def own(name):
            return nc.alloc_semaphore(name=name)

        def prefetcher(name, chunks, wanted, loaded):
            def prefetch(sp, i):
                if i < len(wanted):
                    load_chunk(sp, k, k.dram[name], chunks, wanted[i], loaded)
            return prefetch

        with nc.cleanup_on_exit():
            deformable_conv(nc, own, sb, psum, k)
        with nc.cleanup_on_exit():
            selective_scan(nc, own, sb, psum, k)
        with nc.cleanup_on_exit():
            attention(nc, own, sb, psum, k, a2, False, "a2",
                      prefetcher("f2_experts", 1, range(RING_CHUNKS // 2, RING_CHUNKS), k.s_ring2))
        with nc.cleanup_on_exit():
            experts_ffn(nc, own, sb, psum, k, f2, 1, k.s_ring2, "f2")
        with nc.cleanup_on_exit():
            attention(nc, own, sb, psum, k, a3, True, "a3",
                      prefetcher("f3_experts", 2, range(RING_CHUNKS), k.s_ring3))
        with nc.cleanup_on_exit():
            experts_ffn(nc, own, sb, psum, k, f3, 2, k.s_ring3, "f3", stores)


def _prepare(inputs):
    arrays = _host_arrays(inputs)
    return {f"in_{n}": m for n, m in arrays.items()}


def _declare(nc, arrays):
    k = Shared()
    k.dram = {n[3:]: nc.dram_tensor(n, m.shape, mybir.dt.from_np(m.dtype), kind="ExternalInput").ap()
              for n, m in arrays.items()}
    return k


def kernel(**inputs):
    import concourse.bacc as bacc
    from concourse.bass_utils import run_bass_kernel_spmd

    nc = bacc.Bacc("TRN2", target_bir_lowering=False, num_devices=1)
    arrays = _prepare(inputs)
    k = _declare(nc, arrays)
    out = nc.dram_tensor("out", (B, C, HW, HW), F32, kind="ExternalOutput").ap()
    build(nc, k, out)
    result = run_bass_kernel_spmd(nc, [arrays], core_ids=[0])
    return result.results[0]["out"]
```

```python
from contextlib import ExitStack

import numpy as np

import concourse.bass as bass
from concourse import mybir

F32 = mybir.dt.float32
BF16 = mybir.dt.bfloat16
I32 = mybir.dt.int32
U32 = mybir.dt.uint32
ACT = mybir.ActivationFunctionType
ALU = mybir.AluOpType
AX_X = mybir.AxisListType.X

P = 128
B, C, HW = 4, 256, 16
N = HW * HW
TOK = B * N
CT = C // P
NT = N // P
TT = TOK // P
CB = 64
TAPS = 9
S = 8
HEADS = 2
AH, HD = 16, 16
E = 8
MAXBLK = (2 * TOK + E * (P - 1)) // P
BANK = 512


class GroupNorm:

    def __init__(self, name, sb, sem, parts, cols, eps):
        self.parts, self.cols, self.eps = parts, cols, eps
        self.raw = sb(f"{name}_raw", [parts, cols, 6])
        self.moments = sb(f"{name}_moments", [parts, cols, 2])
        self.square = sb(f"{name}_square", [parts, cols])
        self.group = sb(f"{name}_group", [parts, cols, 2])
        self.var = sb(f"{name}_var", [parts, cols])
        self.sd = sb(f"{name}_sd", [parts, cols])
        self.scale = sb(f"{name}_scale", [parts, cols])
        self.shift = sb(f"{name}_shift", [parts, cols])
        self.s_stats = sem(f"{name}_stats")
        self.s_moments = sem(f"{name}_moments")
        self.s_grouped = sem(f"{name}_grouped")
        self.s_var = sem(f"{name}_var")
        self.s_sd = sem(f"{name}_sd")
        self.s_affine = sem(f"{name}_affine")

    def stats(self, dve, column, source):
        dve.bn_stats(self.raw[:, column, :], source).then_inc(self.s_stats, 1)

    def partition_moments(self, dve):
        dve.wait_ge(self.s_stats, self.cols)
        for c in range(self.cols):
            last = dve.bn_aggr(self.moments[:, c, :], self.raw[:, c, :])
        last.then_inc(self.s_moments, 1)
        dve.wait_ge(self.s_moments, 1)
        dve.tensor_tensor(self.square[:], self.moments[:, :, 0], self.moments[:, :, 0],
                          ALU.mult).then_inc(self.s_moments, 1)
        dve.wait_ge(self.s_moments, 2)
        dve.tensor_tensor(self.moments[:, :, 1], self.moments[:, :, 1], self.square[:],
                          ALU.add).then_inc(self.s_moments, 1)

    def group_mean(self, pe, psum, averaging):
        pe.wait_ge(self.s_moments, 3)
        pe.matmul(psum, averaging, self.moments[:].rearrange("p c k -> p (c k)"),
                  start=True, stop=True).then_inc(self.s_grouped, 1)

    def variance(self, dve, psum):
        dve.wait_ge(self.s_grouped, 1)
        dve.tensor_copy(self.group[:].rearrange("p c k -> p (c k)"), psum).then_inc(self.s_var, 1)
        dve.wait_ge(self.s_var, 1)
        dve.tensor_tensor(self.square[:], self.group[:, :, 0], self.group[:, :, 0],
                          ALU.mult).then_inc(self.s_var, 1)
        dve.wait_ge(self.s_var, 2)
        dve.scalar_tensor_tensor(self.var[:], self.group[:, :, 1], self.eps, self.square[:],
                                 ALU.add, ALU.subtract).then_inc(self.s_var, 1)

    def deviation(self, act):
        act.wait_ge(self.s_var, 3)
        act.activation(self.sd[:], self.var[:], ACT.Sqrt).then_inc(self.s_sd, 1)

    def affine(self, dve, gamma=None, beta=None):
        dve.wait_ge(self.s_sd, 1)
        dve.reciprocal(self.scale[:], self.sd[:]).then_inc(self.s_affine, 1)
        if gamma is not None:
            dve.wait_ge(self.s_affine, 1)
            dve.tensor_tensor(self.scale[:], self.scale[:], gamma, ALU.mult).then_inc(self.s_affine, 1)
        else:
            dve.engine_nop().then_inc(self.s_affine, 1)
        dve.wait_ge(self.s_affine, 2)
        dve.tensor_tensor(self.shift[:], self.group[:, :, 0], self.scale[:], ALU.mult).then_inc(self.s_affine, 1)
        dve.wait_ge(self.s_affine, 3)
        if beta is not None:
            dve.tensor_tensor(self.shift[:], beta, self.shift[:], ALU.subtract).then_inc(self.s_affine, 1)
        else:
            dve.tensor_scalar(self.shift[:], self.shift[:], -1.0, None, ALU.mult).then_inc(self.s_affine, 1)

    READY = 4


class PixelOrder:

    def __init__(self, sb, sem, k, room):
        used = 0

        def take(*shape):
            nonlocal used
            size = 1
            for d in shape:
                size *= d
            view = room[:, used:used + size]
            used += size
            names = "abc"[:len(shape)]
            return view if len(shape) == 1 else view.rearrange(f"p ({' '.join(names)}) -> p {' '.join(names)}",
                                                               **dict(zip(names[1:], shape[1:])))

        self.mobius = sb("mobius", [P, HEADS, 4])
        self.mob = sb("mob", [P, HEADS, 4])
        self.det = sb("det", [P, 3, HEADS])
        self.rank_of = sb("rank", [P, HEADS, NT])
        self.z = take(2, N + NT)
        self.before = take(NT, N)
        self.iota = take(N)
        self.cplx = take(6, N + NT)
        self.value = take(HEADS, N + NT)
        self.less = take(HEADS * NT, N)
        self.tie = take(HEADS * NT, N)
        self.order = k.order
        self.s_in = sem("mobius_loaded")
        self.s_mob = sem("mobius_steps")
        self.s_det = sem("mobius_root")
        self.s_rank = sem("rank_steps")
        self.s_order = sem("order_ready")
        self.steps = 0

    def load(self, sp, k):
        for dst, name in ((self.mobius[:], "mobius"), (self.z, "z"), (self.before, "before"), (self.iota, "iota_n")):
            sp.dma_start(dst, k.dram[name]).then_inc(self.s_in, 16)

    def root(self, act):
        act.wait_ge(self.s_mob, 3)
        act.activation(self.det[:, 0, :], self.det[:, 2, :], ACT.Abs).then_inc(self.s_det, 1)
        act.wait_ge(self.s_mob, 4)
        act.activation(self.det[:, 1, :], self.det[:, 0, :], ACT.Sqrt).then_inc(self.s_det, 1)

    def step(self, dve, ins):
        self.steps += 1
        ins.then_inc(self.s_mob, 1)
        dve.wait_ge(self.s_mob, self.steps)

    def coefficients(self, dve):
        mobius, mob, det = self.mobius, self.mob, self.det
        dve.wait_ge(self.s_in, 16 * 4)
        self.step(dve, dve.tensor_tensor(det[:, 0, :], mobius[:, :, 0], mobius[:, :, 3], ALU.mult))
        self.step(dve, dve.tensor_tensor(det[:, 1, :], mobius[:, :, 1], mobius[:, :, 2], ALU.mult))
        self.step(dve, dve.tensor_tensor(det[:, 2, :], det[:, 0, :], det[:, 1, :], ALU.subtract))
        dve.wait_ge(self.s_det, 1)
        self.step(dve, dve.tensor_scalar(det[:, 0, :], det[:, 0, :], 0.001, None, ALU.max))
        dve.wait_ge(self.s_det, 2)
        self.step(dve, dve.reciprocal(det[:, 2, :], det[:, 1, :]))
        self.step(dve, dve.tensor_tensor(mob[:], mobius[:], det[:, 2, :].unsqueeze(2).broadcast_to([P, HEADS, 4]), ALU.mult))
        self.step(dve, dve.tensor_scalar(det[:, 0, :], mob[:, :, 3], 1e-6, None, ALU.add))

    def products(self, dve, h):
        a, bb, c, dd = self.mob[:, h, 0:1], self.mob[:, h, 1:2], self.mob[:, h, 2:3], self.det[:, 0, h:h + 1]
        NR, NI, DR, DI, RE, IM = (self.cplx[:, i, :] for i in range(6))
        z = self.z
        self.step(dve, dve.tensor_scalar(NR, z[:, 0, :], a, bb, ALU.mult, ALU.add))
        self.step(dve, dve.tensor_scalar(NI, z[:, 1, :], a, None, ALU.mult))
        self.step(dve, dve.tensor_scalar(DR, z[:, 0, :], c, dd, ALU.mult, ALU.add))
        self.step(dve, dve.tensor_scalar(DI, z[:, 1, :], c, None, ALU.mult))
        self.step(dve, dve.tensor_tensor(RE, NR, DR, ALU.mult))
        self.step(dve, dve.tensor_tensor(IM, NI, DI, ALU.mult))
        self.step(dve, dve.tensor_tensor(RE, RE, IM, ALU.add))

    def quotient(self, dve, h):
        NR, NI, DR, DI, RE, IM = (self.cplx[:, i, :] for i in range(6))
        self.step(dve, dve.tensor_tensor(NI, NI, DR, ALU.mult))
        self.step(dve, dve.tensor_tensor(NR, NR, DI, ALU.mult))
        self.step(dve, dve.tensor_tensor(IM, NI, NR, ALU.subtract))
        self.step(dve, dve.scalar_tensor_tensor(RE, IM, 1.3, RE, ALU.mult, ALU.add))
        self.step(dve, dve.tensor_tensor(DR, DR, DR, ALU.mult))
        self.step(dve, dve.tensor_tensor(DI, DI, DI, ALU.mult))
        self.step(dve, dve.tensor_tensor(DR, DR, DI, ALU.add))
        self.step(dve, dve.reciprocal(DI, DR))
        self.step(dve, dve.tensor_tensor(self.value[:, h, :], RE, DI, ALU.mult))

    def rank(self, dve):
        for h in range(HEADS):
            for t in range(NT):
                own, i = self.value[:, h, N + t:N + t + 1], NT * h + t
                dve.tensor_scalar(self.less[:, i, :], self.value[:, h, 0:N], own, None, ALU.is_lt).then_inc(self.s_rank, 1)
                dve.scalar_tensor_tensor(self.tie[:, i, :], self.value[:, h, 0:N], own, self.before[:, t, :],
                                         ALU.is_equal, ALU.mult).then_inc(self.s_rank, 1)
        ties = 2 * HEADS * NT
        dve.wait_ge(self.s_rank, ties)
        dve.tensor_tensor(self.less, self.less, self.tie, ALU.add).then_inc(self.s_rank, 1)
        dve.wait_ge(self.s_rank, ties + 1)
        dve.tensor_reduce(self.rank_of[:].rearrange("p h t -> p (h t)"), self.less, AX_X, ALU.add).then_inc(self.s_rank, 1)
        dve.wait_ge(self.s_rank, ties + 2)
        for h in range(HEADS):
            for t in range(NT):
                last = dve.tensor_scalar(self.order[:, h, t, :], self.iota, self.rank_of[:, h, t:t + 1], None, ALU.is_equal)
        last.then_inc(self.s_order, 1)
        dve.wait_ge(self.s_order, 1)


def deformable_conv(nc, sem, sbuf, psum, k):
    with ExitStack() as ctx:
        def sb(name, shape, dt=F32):
            return ctx.enter_context(nc.sbuf_tensor(name, shape, dt))

        x = sb("x_in", [P, CT, B, N])
        w1 = sb("w1", [P, CT, P])
        image = sb("image", [P, 3, B, HW + 2, HW])
        w_off = sb("w_off", [P, 2, 3, 27])
        b_off = sb("b_off", [P, 27])
        w2 = sb("w2", [P, TAPS * CB])
        w3 = sb("w3", [P, 2, C])
        gn64 = sb("gn64", [P, 4, B])
        gn256 = sb("gn256", [P, 2, CT * B])
        pair = sb("pair", [P, P])
        grid = sb("grid", [P, TT, 2 * TAPS])
        iota = sb("iota", [P, HW])
        om = sb("om", [P, TT, 3 * TAPS])
        pos = sb("pos", [P, TT, 2 * TAPS])
        deformed = sb("deformed", [P, B // 2, N])
        mask = sb("mask", [P, TT, TAPS])
        hat = sb("hat", [P, TT, 2 * TAPS, HW])
        weights = sb("weights", [P, 2, NT, TAPS, N])
        weights_t = k.ring[:, 0:B * NT * TAPS * N].rearrange("p (b k n) -> p b k n", b=B, n=N)
        mixed = sb("mixed", [P, B, NT, TAPS, CB])
        r2 = sb("r2", [P, B // 2, N])
        pre = k.h[:].rearrange("p t b n -> p (t b) n")

        order = PixelOrder(sb, sem, k, weights[:].rearrange("p b s k n -> p (b s k n)"))

        g1 = GroupNorm("gn1", sb, sem, P, B, 1e-5)
        g2 = GroupNorm("gn2", sb, sem, P, B // 2, 1e-5)
        g3 = GroupNorm("gn3", sb, sem, P, CT * B, 1e-5)
        g4 = GroupNorm("gn4", sb, sem, P, CT * B, 1e-5)

        s_x = sem("x_loaded")
        s_w1 = sem("w1_loaded")
        s_w = sem("l0_weights_loaded")
        s_c1 = sem("conv1")
        s_pad = sem("padding_zeroed")
        s_img = sem("image_ready")
        s_moved = sem("moved_images_ready")
        s_om = sem("offsets")
        s_oms = sem("offsets_on_sbuf")
        s_yo = sem("deformed_out")
        s_pos = sem("positions")
        s_mask = sem("mask_ready")
        s_dist = sem("distances")
        s_abs = sem("distances_absolute")
        s_tent = sem("hats_unmasked")
        s_hat = sem("hats_ready")
        s_wd = sem("weights_dve")
        s_wp = sem("weights_pool")
        s_tr = sem("weights_transposed")
        s_ea = sem("transpose_out_act")
        s_ed = sem("transpose_out_dve")
        s_mix = sem("mixed_product")
        s_mo = sem("mixed_out")
        s_y = sem("deformed")
        s_r2 = sem("r2_ready")
        s_c3 = sem("conv3")
        s_pre = sem("pre_residual")
        s_x1 = sem("x1_ready")
        s_h1 = sem("h1_ready")

        GROUP = 2
        BANKS = NT * TAPS // GROUP
        MIX_BEFORE = (0, 5)
        y_banks = 6
        block = ctx.enter_context(nc.Block())

        @block.sync
        def _(sp):
            sp.dma_start(w1[:], k.dram["w1"]).then_inc(s_w1, 16)
            sp.dma_start(x[:], k.dram["x"]).then_inc(s_x, 16)
            order.load(sp, k)
            for dst, src in ((pair, k.dram["pair"]), (gn64, k.dram["gn64"]), (w_off, k.dram["w_off"]), (b_off, k.dram["b_off"]),
                             (grid, k.dram["grid"]), (iota, k.dram["iota"]), (w2, k.dram["w2"]), (k.ident_sb, k.dram["ident"]),
                             (k.avg8_sb, k.dram["avg8"]), (w3, k.dram["w3"]), (gn256, k.dram["gn256"])):
                sp.dma_start(dst[:], src).then_inc(s_w, 16)

        LOADED = 16 * 11

        @block.gpsimd
        def _(pool):
            pool.memset(image[:], 0.0).then_inc(s_pad, 1)
            for b in range(B):
                T = NT * b + 1
                pool.wait_ge(s_hat, b + 1)
                if b >= 2:
                    pool.wait_ge(s_tr, BANKS * (b - 1))
                pool.tensor_tensor(weights[:, b % 2, 1, :, :].rearrange("p k (y x) -> p k y x", y=HW),
                                   hat[:, T, TAPS:, :].unsqueeze(3).broadcast_to([P, TAPS, HW, HW]),
                                   hat[:, T, :TAPS, :].unsqueeze(2).broadcast_to([P, TAPS, HW, HW]),
                                   ALU.mult).then_inc(s_wp, 1)

        @block.vector
        def _(dve):
            order.coefficients(dve)
            for b in range(B):
                dve.wait_ge(s_c1, b // 2 + 1)
                g1.stats(dve, b, psum[:, y_banks + b // 2, (b % 2) * N:(b % 2) * N + N])
            g1.partition_moments(dve)
            g1.variance(dve, psum[:, 4, 0:2 * B])
            dve.wait_ge(s_w, LOADED)
            g1.affine(dve, gn64[:, 0, :], gn64[:, 1, :])
            order.products(dve, 0)
            dve.wait_ge(s_img, 2 * B)
            dve.tensor_copy(image[:, 2, :, :, 0:HW - 1], image[:, 1, :, :, 1:HW]).then_inc(s_moved, 1)
            order.quotient(dve, 0)
            order.products(dve, 1)
            order.quotient(dve, 1)
            order.rank(dve)
            dve.wait_ge(s_om, 1)
            dve.tensor_tensor(om[:], psum[:, 5, 0:TT * 3 * TAPS].rearrange("p (t o) -> p t o", t=TT),
                              b_off[:].unsqueeze(1).broadcast_to([P, TT, 3 * TAPS]), ALU.add).then_inc(s_oms, 1)
            dve.wait_ge(s_oms, 1)
            dve.tensor_tensor(pos[:], om[:, :, 0:2 * TAPS], grid[:], ALU.add).then_inc(s_pos, 1)
            dve.wait_ge(s_pos, 1)
            for b in range(B):
                shape = [P, NT * 2 * TAPS, HW]
                tiles = slice(NT * b, NT * b + NT)
                dve.tensor_tensor(hat[:, tiles].rearrange("p t k i -> p (t k) i"),
                                  pos[:, tiles].rearrange("p t k -> p (t k)").unsqueeze(2).broadcast_to(shape),
                                  iota[:].unsqueeze(1).broadcast_to(shape), ALU.subtract).then_inc(s_dist, 1)

            def mask_hats(b):
                tiles = slice(NT * b, NT * b + NT)
                dve.wait_ge(s_tent, b + 1)
                dve.tensor_tensor(hat[:, tiles, TAPS:, :], hat[:, tiles, TAPS:, :],
                                  mask[:, tiles].unsqueeze(3).broadcast_to([P, NT, TAPS, HW]), ALU.mult).then_inc(s_hat, 1)

            def sampling(b):
                dve.wait_ge(s_hat, b + 1)
                if b >= 2:
                    dve.wait_ge(s_tr, BANKS * (b - 1))
                T = NT * b
                dve.tensor_tensor(weights[:, b % 2, 0, :, :].rearrange("p k (y x) -> p k y x", y=HW),
                                  hat[:, T, TAPS:, :].unsqueeze(3).broadcast_to([P, TAPS, HW, HW]),
                                  hat[:, T, :TAPS, :].unsqueeze(2).broadcast_to([P, TAPS, HW, HW]),
                                  ALU.mult).then_inc(s_wd, 1)

            def take(i):
                dve.wait_ge(s_y, i + 1)
                dve.tensor_copy(deformed[:, i, :], psum[:, y_banks + i, 0:N]).then_inc(s_yo, 1)
                dve.wait_ge(s_yo, i + 1)
                g2.stats(dve, i, deformed[:, i, :])

            mask_hats(0)
            sampling(0)
            mask_hats(1)
            for b in range(B):
                for j in range(BANKS):
                    J = BANKS * b + j
                    if j == 4 and b == 0:
                        sampling(1)
                        mask_hats(2)
                        mask_hats(3)
                    if J % 2 == 1:
                        dve.wait_ge(s_tr, J + 1)
                        dve.tensor_copy(weights_t[:, b, GROUP * j:GROUP * j + GROUP, :].rearrange("p a n -> p (a n)"),
                                        psum[:, J % 4, :]).then_inc(s_ed, 1)
                if b + 2 < B:
                    sampling(b + 2)
                if b == B // 2:
                    take(0)
            take(1)
            g2.partition_moments(dve)
            g2.variance(dve, psum[:, 4, 0:B])
            g2.affine(dve, gn64[:, 2, 0:B // 2], gn64[:, 3, 0:B // 2])
            for i in range(CT * B):
                if i % 2 == 0:
                    dve.wait_ge(s_c3, i // 2 + 1)
                g3.stats(dve, i, psum[:, i // 2, (i % 2) * N:(i % 2) * N + N])
            g3.partition_moments(dve)
            g3.variance(dve, psum[:, 4, 0:2 * CT * B])
            g3.affine(dve, gn256[:, 0, :], gn256[:, 1, :])
            dve.wait_ge(g3.s_affine, g3.READY)
            xs = x[:].rearrange("p t b n -> p (t b) n")
            for i in range(CT * B):
                dve.scalar_tensor_tensor(pre[:, i, :], psum[:, i // 2, (i % 2) * N:(i % 2) * N + N],
                                         g3.scale[:, i:i + 1], xs[:, i, :], ALU.mult, ALU.add).then_inc(s_pre, 1)
            for i in range(CT * B):
                dve.wait_ge(s_x1, i + 1)
                g4.stats(dve, i, k.x1[:].rearrange("p t b n -> p (t b) n")[:, i, :])
            g4.partition_moments(dve)
            g4.variance(dve, psum[:, 5, 0:2 * CT * B])
            g4.affine(dve)
            dve.wait_ge(g4.s_affine, g4.READY)
            for i in range(0, CT * B, 2):
                dve.tensor_scalar(k.h[:].rearrange("p t b n -> p (t b) n")[:, i, :],
                                  k.x1[:].rearrange("p t b n -> p (t b) n")[:, i, :],
                                  g4.scale[:, i:i + 1], g4.shift[:, i:i + 1], ALU.mult, ALU.add).then_inc(s_h1, 1)

        @block.scalar
        def _(act):
            order.root(act)
            g1.deviation(act)
            act.wait_ge(g1.s_affine, g1.READY)
            act.wait_ge(s_pad, 1)
            for b in range(B):
                for half in range(2):
                    channels = slice(CB * half, CB * half + CB)
                    act.activation(image[channels, 1, b, 1 - half:HW + 1 - half, :],
                                   psum[channels, y_banks + b // 2, (b % 2) * N:(b % 2) * N + N].rearrange("p (y x) -> p y x", y=HW),
                                   ACT.Relu, bias=g1.shift[channels, b:b + 1], scale=g1.scale[channels, b:b + 1]).then_inc(s_img, 1)
            act.wait_ge(s_img, 2 * B)
            act.activation(image[:, 0, :, :, 1:HW], image[:, 1, :, :, 0:HW - 1], ACT.Copy).then_inc(s_moved, 1)
            act.wait_ge(s_oms, 1)
            act.activation(mask[:], om[:, :, 2 * TAPS:], ACT.Sigmoid).then_inc(s_mask, 1)
            for b in range(B):
                hats = hat[:, NT * b:NT * b + NT].rearrange("p t k i -> p (t k i)")
                act.wait_ge(s_dist, b + 1)
                act.activation(hats, hats, ACT.Abs).then_inc(s_abs, 1)
                act.wait_ge(s_abs, b + 1)
                act.activation(hats, hats, ACT.Relu, bias=1.0, scale=-1.0).then_inc(s_tent, 1)

            def take_mixed(i):
                b, s = i // NT, i % NT
                act.wait_ge(s_mix, i + 1)
                act.activation(mixed[:, b, s, :, :].rearrange("p k o -> p (k o)").rearrange("p (a n) -> p a n", a=2),
                               psum[:, 4:6, 0:TAPS * CB // 2], ACT.Copy).then_inc(s_mo, 1)

            for b in range(B):
                for j in range(BANKS):
                    if j in MIX_BEFORE:
                        take_mixed(NT * b + MIX_BEFORE.index(j))
                    J = BANKS * b + j
                    if J % 2 == 0:
                        act.wait_ge(s_tr, J + 1)
                        act.activation(weights_t[:, b, GROUP * j:GROUP * j + GROUP, :].rearrange("p a n -> p (a n)"),
                                       psum[:, J % 4, :], ACT.Copy).then_inc(s_ea, 1)
            g2.deviation(act)
            act.wait_ge(g2.s_affine, g2.READY)
            for i in range(B // 2):
                act.activation(r2[:, i, :], deformed[:, i, :], ACT.Relu,
                               bias=g2.shift[:, i:i + 1], scale=g2.scale[:, i:i + 1]).then_inc(s_r2, 1)
            g3.deviation(act)
            act.wait_ge(g3.s_affine, g3.READY)
            for i in range(CT * B):
                act.wait_ge(s_pre, i + 1)
                act.activation(k.x1[:].rearrange("p t b n -> p (t b) n")[:, i, :], pre[:, i, :], ACT.Relu,
                               bias=g3.shift[:, i:i + 1]).then_inc(s_x1, 1)
            g4.deviation(act)
            act.wait_ge(g4.s_affine, g4.READY)
            for i in range(1, CT * B, 2):
                act.activation(k.h[:].rearrange("p t b n -> p (t b) n")[:, i, :],
                               k.x1[:].rearrange("p t b n -> p (t b) n")[:, i, :], ACT.Identity,
                               bias=g4.shift[:, i:i + 1], scale=g4.scale[:, i:i + 1]).then_inc(s_h1, 1)

        @block.tensor
        def _(pe):
            pe.wait_ge(s_w1, 16)
            pe.wait_ge(s_x, 16)
            for half in range(2):
                for t in range(CT):
                    last = pe.matmul(psum[:, y_banks + half, :], w1[:, t, :],
                                     x[:, t, 2 * half:2 * half + 2, :].rearrange("p b n -> p (b n)"),
                                     start=(t == 0), stop=(t == CT - 1))
                last.then_inc(s_c1, 1)
            pe.wait_ge(s_w, LOADED)
            g1.group_mean(pe, psum[:, 4, 0:2 * B], pair[:])
            pe.wait_ge(s_moved, 2)

            def rows(dx, b, y):
                return image[:, dx, b, y:y + HW // NT, :].rearrange("p y x -> p (y x)")

            for T in range(TT):
                b, y0 = T // NT, (T % NT) * HW // NT
                for both in range(2):
                    for dx in range(3):
                        last = pe.matmul(psum[:, 5, 27 * T:27 * T + 27], rows(dx, b, y0 + 2 * both), w_off[:, both, dx, :],
                                         start=(both == 0 and dx == 0), stop=(both == 1 and dx == 2))
            last.then_inc(s_om, 1)

            def mix(i):
                b, s = i // NT, i % NT
                if i >= 1:
                    pe.wait_ge(s_mo, i)
                else:
                    pe.wait_ge(s_oms, 1)
                for a in range(2):
                    last = pe.matmul(psum[:, 4 + a, 0:TAPS * CB // 2], rows(1, b, 1 + s * HW // NT),
                                     w2[:, a * TAPS * CB // 2:(a + 1) * TAPS * CB // 2], start=True, stop=True)
                last.then_inc(s_mix, 1)

            def sample(i):
                pe.wait_ge(s_mo, NT * (2 * i + 2))
                pe.wait_ge(s_ea, (BANKS * (2 * i + 2) + 1) // 2)
                pe.wait_ge(s_ed, BANKS * (2 * i + 2) // 2)
                for tap in range(NT * TAPS):
                    for half in range(2):
                        b = 2 * i + half
                        last = pe.matmul(psum[CB * half:CB * half + CB, y_banks + i, 0:N],
                                         mixed[:, b, tap // TAPS, tap % TAPS, :], weights_t[:, b, tap, :],
                                         start=(tap == 0), stop=(tap == NT * TAPS - 1))
                last.then_inc(s_y, 1)

            for b in range(B):
                for j in range(BANKS):
                    if j in MIX_BEFORE:
                        mix(NT * b + MIX_BEFORE.index(j))
                    if j == 0:
                        pe.wait_ge(s_wd, b + 1)
                        pe.wait_ge(s_wp, b + 1)
                    J = BANKS * b + j
                    if J >= 4:
                        pe.wait_ge(s_ea if J % 2 == 0 else s_ed, (J - 4) // 2 + 1)
                    for a in range(GROUP):
                        s, tap = (GROUP * j + a) // TAPS, (GROUP * j + a) % TAPS
                        for t in range(NT):
                            last = pe.transpose(psum[:, J % 4, a * N + P * t:a * N + P * t + P],
                                                weights[:, b % 2, t, tap, P * s:P * s + P], k.ident_sb[:])
                    last.then_inc(s_tr, 1)
                if b == B // 2 - 1:
                    sample(0)
            sample(1)
            g2.group_mean(pe, psum[:, 4, 0:B], pair[:])
            pe.wait_ge(s_r2, B // 2)
            for t in range(CT):
                for b in range(B):
                    last = pe.matmul(psum[:, 2 * t + b // 2, (b % 2) * N:(b % 2) * N + N], w3[:, b % 2, P * t:P * t + P],
                                     r2[:, b // 2, :], start=True, stop=True)
                    if b % 2:
                        last.then_inc(s_c3, 1)
            g3.group_mean(pe, psum[:, 4, 0:2 * CT * B], k.avg8_sb[:])
            g4.group_mean(pe, psum[:, 5, 0:2 * CT * B], k.avg8_sb[:])


def selective_scan(nc, sem, sbuf, psum, k):
    QROWS = 32
    DEEP = 3
    ROWS = 3 * S
    with ExitStack() as ctx:
        def sb(name, shape, dt=F32):
            return ctx.enter_context(nc.sbuf_tensor(name, shape, dt))

        w_in = sb("w_in", [P, CT, 3 * C])
        b_in = sb("b_in", [P, 3 * CT])
        dw = sb("dw", [P, CT, 4])
        w_dbc = sb("w_dbc", [P, CT, 2 * (2 * S + 1)])
        b_dbc = sb("b_dbc", [P, 2 * (2 * S + 1)])
        a_log = sb("a_log", [P, HEADS * S])
        d_skip = sb("d_skip", [P, HEADS])
        w_out = sb("w_out", [P, CT, C])
        b_out = sb("b_out", [P, C])
        select = sb("select", [3 * QROWS, ROWS, P], BF16)

        xs = sb("xs", [P, CT, B, N + 2])
        res, gate, x_perm, y_scan = (k.ring_late[:, i * CT * TOK:(i + 1) * CT * TOK].rearrange("p (t n) -> p t n", t=CT)
                                     for i in range(4))
        conv = y_scan.rearrange("p t (b n) -> p t b n", b=B)
        xf = sb("xf", [P, CT, TOK])
        xf_t = sb("xf_t", [P, TT, C])
        order = k.order
        order_t = sb("order_t", [P, HEADS, NT, N])
        dbc = sb("dbc", [P, TT, HEADS, 2 * S + 1])
        warm = sb("warm", [P, 3 * CT])
        soft = sb("soft", [P, 6, TT, HEADS])
        a_neg = sb("a_neg", [P, HEADS * S])
        rows = sb("rows", [P, TT, HEADS, 3, QROWS])
        parts = sb("parts", [3 * QROWS, HEADS, TOK], BF16)
        rest = sb("rest", [3 * QROWS, TOK])
        dtb = sb("dtb", [P, DEEP, BANK])
        u = sb("u", [P, DEEP, BANK])
        state = sb("state", [P, DEEP, BANK])
        prod = sb("prod", [P, DEEP, BANK])
        y_t = xf_t
        y = x_perm
        silu_out = u

        s_w_in = sem("l1_first_weights_loaded")
        s_w = sem("l1_weights_loaded")
        s_zero = sem("l1_zeroed")
        s_in = sem("in_proj")
        s_silu = sem("in_proj_silu")
        s_gate = sem("gate_silu")
        s_cv = sem("depthwise_steps")
        s_xf = sem("xf_ready")
        s_xt = sem("xf_transposed")
        s_xto = sem("xf_t_out")
        s_ot = sem("order_transposed")
        s_oto = sem("order_t_out")
        s_dbc = sem("dbc_product")
        s_so = sem("softplus_dve")
        s_ab = sem("softplus_absolute")
        s_sa = sem("softplus_act")
        s_rows = sem("rows_ready")
        s_rp = sem("rows_permuted")
        s_hi = sem("high_part")
        s_rest = sem("rest_of_parts")
        s_mid = sem("middle_part")
        s_parts = sem("parts_ready")
        s_xp = sem("x_permuted")
        s_xpo = sem("x_perm_out")
        s_bdt = sem("dt_b_spread")
        s_bda = sem("decay_spread")
        s_bc = sem("c_spread")
        s_dtb = sem("dtb_out")
        s_u = sem("scan_input")
        s_scan = sem("scanned")
        s_cm = sem("times_c")
        s_acc = sem("summed_over_states")
        s_ys = sem("y_scan_out")
        s_yt = sem("y_transposed")
        s_yto = sem("y_t_out")
        s_un = sem("y_unpermuted")
        s_y = sem("gating_steps")
        s_op = sem("out_proj")
        s_ob = sem("out_proj_biased")
        s_so2 = sem("out_proj_silu")
        s_x1t = sem("residual_transposed")
        s_x1o = sem("residual_out")
        s_t = sem("tokens_ready")

        BANKS_IN = (0, 2, 0, 2, 6, 2)
        PAIRS = HEADS * B // 2
        STEPS = PAIRS * S
        block = ctx.enter_context(nc.Block())
        DT, AB, EX, U1, LN, TMP = range(6)

        @block.sync
        def _(sp):
            for dst, src in ((w_in, k.dram["w_in"]), (b_in, k.dram["b_in"]), (dw, k.dram["dw"])):
                sp.dma_start(dst[:], src).then_inc(s_w_in, 16)
            for dst, src in ((w_dbc, k.dram["w_dbc"]), (b_dbc, k.dram["b_dbc"]), (a_log, k.dram["a_log"]), (d_skip, k.dram["d_skip"]),
                             (w_out, k.dram["w_out"]), (b_out, k.dram["b_out"]), (select, k.dram["select"])):
                sp.dma_start(dst[:], src).then_inc(s_w, 16)
            for n in range(RING_CHUNKS // 2):
                load_chunk(sp, k, k.dram["f2_experts"], 1, n, k.s_ring2)

        LOADED = 16 * 7

        @block.gpsimd
        def _(pool):
            pool.memset(xs[:, :, :, 0:1], 0.0).then_inc(s_zero, 1)
            pool.memset(xs[:, :, :, N + 1:N + 2], 0.0).then_inc(s_zero, 1)
            pool.memset(rows[:], 0.0).then_inc(s_zero, 1)
            for h in range(HEADS):
                pool.wait_ge(s_parts, h + 1)
                for q in range(3):
                    last = pool.memset(parts[QROWS * q:QROWS * q + S, h, :].rearrange("p (b n) -> p b n", b=B)[:, :, 0:1], 0.0)
                last.then_inc(s_zero, 1)
            for i in range(STEPS):
                h, half = i // S // 2, i // S % 2
                if i % (2 * S) == 0:
                    pool.wait_ge(s_xpo, h + 1)
                pool.wait_ge(s_dtb, i + 1)
                if i >= DEEP:
                    pool.wait_ge(s_scan, i - DEEP + 1)
                pool.tensor_tensor(u[:, i % DEEP, :], dtb[:, i % DEEP, :], x_perm[:, h, BANK * half:BANK * half + BANK],
                                   ALU.mult).then_inc(s_u, 1)

        @block.vector
        def _(dve):
            for h in range(HEADS):
                dve.wait_ge(s_ot, h + 1)
                dve.tensor_copy(order_t[:, h].rearrange("p t n -> p (t n)"), psum[:, 4 + h, :]).then_inc(s_oto, 1)
            dve.wait_ge(s_w_in, 16 * 3)
            for t in range(CT):
                dve.wait_ge(s_silu, t + 1)
                dve.wait_ge(s_zero, 2)
                dve.tensor_scalar(conv[:, t], xs[:, t, :, 0:N], dw[:, t, 0:1], dw[:, t, 3:4], ALU.mult, ALU.add).then_inc(s_cv, 1)
                dve.wait_ge(s_cv, 3 * t + 1)
                dve.scalar_tensor_tensor(conv[:, t], xs[:, t, :, 1:N + 1], dw[:, t, 1:2], conv[:, t],
                                         ALU.mult, ALU.add).then_inc(s_cv, 1)
                dve.wait_ge(s_cv, 3 * t + 2)
                dve.scalar_tensor_tensor(conv[:, t], xs[:, t, :, 2:N + 2], dw[:, t, 2:3], conv[:, t],
                                         ALU.mult, ALU.add).then_inc(s_cv, 1)
            dve.wait_ge(s_dbc, 1)
            W = HEADS * (2 * S + 1)
            dve.wait_ge(s_w, LOADED)
            dve.tensor_tensor(dbc[:].rearrange("p t h j -> p t (h j)"), psum[:, 6, 0:TT * W].rearrange("p (t w) -> p t w", w=W),
                              b_dbc[:].unsqueeze(1).broadcast_to([P, TT, W]), ALU.add).then_inc(s_so, 1)
            dve.wait_ge(s_so, 1)
            dve.scalar_tensor_tensor(soft[:, AB], dbc[:, :, :, 0], -1.0, dbc[:, :, :, 0], ALU.mult, ALU.max).then_inc(s_ab, 1)
            dve.wait_ge(s_sa, 2)
            dve.tensor_scalar(soft[:, U1], soft[:, EX], 1.0, None, ALU.add).then_inc(s_so, 1)
            dve.wait_ge(s_sa, 3)
            dve.tensor_scalar(soft[:, U1], soft[:, U1], 1.0, None, ALU.subtract).then_inc(s_so, 1)
            dve.tensor_tensor(soft[:, LN], soft[:, LN], soft[:, EX], ALU.mult).then_inc(s_so, 1)
            dve.wait_ge(s_so, 4)
            dve.tensor_scalar(soft[:, AB], soft[:, U1], 1e-30, None, ALU.max).then_inc(s_so, 1)
            dve.wait_ge(s_so, 5)
            dve.reciprocal(soft[:, TMP], soft[:, AB]).then_inc(s_so, 1)
            dve.wait_ge(s_so, 6)
            dve.tensor_tensor(soft[:, LN], soft[:, LN], soft[:, TMP], ALU.mult).then_inc(s_so, 1)
            dve.scalar_tensor_tensor(soft[:, EX], soft[:, U1], 0.0, soft[:, EX], ALU.is_equal, ALU.mult).then_inc(s_so, 1)
            dve.wait_ge(s_so, 8)
            dve.tensor_tensor(soft[:, LN], soft[:, LN], soft[:, EX], ALU.add).then_inc(s_so, 1)
            dve.wait_ge(s_so, 9)
            dve.scalar_tensor_tensor(soft[:, DT], dbc[:, :, :, 0], 0.0, soft[:, LN], ALU.max, ALU.add).then_inc(s_so, 1)
            dve.wait_ge(s_so, 10)
            dve.wait_ge(s_zero, 3)
            dt_wide = soft[:, DT].unsqueeze(3).broadcast_to([P, TT, HEADS, S])
            dve.tensor_tensor(rows[:, :, :, 0, 0:S], dt_wide,
                              a_neg[:].rearrange("p (h s) -> p h s", h=HEADS).unsqueeze(1).broadcast_to([P, TT, HEADS, S]),
                              ALU.mult).then_inc(s_rows, 1)
            dve.tensor_tensor(rows[:, :, :, 0, S:2 * S], dt_wide, dbc[:, :, :, 1:1 + S], ALU.mult).then_inc(s_rows, 1)
            dve.tensor_copy(rows[:, :, :, 0, 2 * S:3 * S], dbc[:, :, :, 1 + S:]).then_inc(s_rows, 1)
            dve.wait_ge(s_sa, 4)
            dve.wait_ge(s_rows, 3)
            for q in (1, 2):
                for h in range(HEADS):
                    dve.tensor_copy(rows[:, :, h, q, 0:ROWS], rows[:, :, h, 0, 0:ROWS]).then_inc(s_rows, 1)
            for h in range(HEADS):
                dve.wait_ge(s_hi, h + 1)
                if h:
                    dve.wait_ge(s_parts, 1)
                permuted = psum[0:3 * QROWS, 2 * h:2 * h + 2, :].rearrange("p a n -> p (a n)")
                dve.tensor_tensor(rest[:], permuted, parts[:, h, :], ALU.subtract).then_inc(s_rest, 1)
                dve.wait_ge(s_mid, h + 1)
                dve.tensor_tensor(parts[2 * QROWS:3 * QROWS, h, :], rest[2 * QROWS:3 * QROWS], parts[2 * QROWS:3 * QROWS, h, :],
                                  ALU.subtract).then_inc(s_parts, 1)
            def times_c(i):
                dve.wait_ge(s_scan, i + 1)
                dve.wait_ge(s_bc, i + 1)
                if i >= DEEP:
                    dve.wait_ge(s_acc, i - DEEP + 1)
                dve.tensor_tensor(prod[:, i % DEEP, :], state[:, i % DEEP, :], psum[:, 4 + i % 2, :], ALU.mult).then_inc(s_cm, 1)

            for i in range(STEPS):
                dve.wait_ge(s_bda, i + 1)
                dve.wait_ge(s_u, i + 1)
                if i >= DEEP:
                    dve.wait_ge(s_cm, i - DEEP + 1)
                dve.tensor_tensor_scan(state[:, i % DEEP, :], psum[:, i % 2, :], u[:, i % DEEP, :], 0.0,
                                       ALU.mult, ALU.add).then_inc(s_scan, 1)
                if i >= 1:
                    times_c(i - 1)
            times_c(STEPS - 1)
            for i in range(TT // 2):
                dve.wait_ge(s_x1t, i + 1)
                dve.tensor_copy(k.t[:, 2 * i:2 * i + 2, :].rearrange("p a n -> p (a n)"), psum[:, i, :]).then_inc(s_x1o, 1)
            dve.wait_ge(s_silu, 3 * CT)
            dve.wait_ge(s_gate, CT)
            for half in range(2):
                for h in range(HEADS):
                    i = HEADS * half + h
                    cols = slice(BANK * half, BANK * half + BANK)
                    dve.wait_ge(s_un, i + 1)
                    dve.scalar_tensor_tensor(y[:, h, cols], xf[:, h, cols], d_skip[:, h:h + 1], psum[:, 4 + 2 * h + half, :],
                                             ALU.mult, ALU.add).then_inc(s_y, 1)
                    dve.wait_ge(s_y, 3 * i + 1)
                    dve.tensor_tensor(y[:, h, cols], y[:, h, cols], gate[:, h, cols], ALU.mult).then_inc(s_y, 1)
                    dve.wait_ge(s_y, 3 * i + 2)
                    dve.tensor_tensor(y[:, h, cols], y[:, h, cols], res[:, h, cols], ALU.add).then_inc(s_y, 1)

            def add_bias(i):
                dve.wait_ge(s_op, i + 1)
                if i >= DEEP:
                    dve.wait_ge(s_t, i - DEEP + 1)
                dve.tensor_tensor(silu_out[:, i % DEEP, :].rearrange("p (a c) -> p a c", a=2),
                                  psum[:, i, :].rearrange("p (a c) -> p a c", a=2),
                                  b_out[:].unsqueeze(1).broadcast_to([P, 2, C]), ALU.add).then_inc(s_ob, 1)

            def add_tokens(i):
                dve.wait_ge(s_so2, i + 1)
                tokens = k.t[:, 2 * i:2 * i + 2, :].rearrange("p a n -> p (a n)")
                dve.tensor_tensor(tokens, tokens, silu_out[:, i % DEEP, :], ALU.add).then_inc(s_t, 1)

            dve.wait_ge(s_x1o, TT // 2)
            add_bias(0)
            for i in range(1, TT // 2):
                add_bias(i)
                add_tokens(i - 1)
            add_tokens(TT // 2 - 1)

        def scanned(act, pair):
            h, half = pair // 2, pair % 2
            act.wait_ge(s_acc, S * (pair + 1))
            act.activation(y_scan[:, h, BANK * half:BANK * half + BANK], psum[:, 6 + pair % 2, :],
                           ACT.Copy).then_inc(s_ys, 1)

        @block.scalar
        def _(act):
            act.wait_ge(s_w_in, 16 * 3)
            act.activation(warm[:], b_in[:], ACT.Silu)

            def silu_in(i):
                act.wait_ge(s_in, i + 1)
                source = psum[:, BANKS_IN[i]:BANKS_IN[i] + 2, :].rearrange("p a n -> p (a n)")
                if i < CT:
                    target = xs[:, i, :, 1:N + 1]
                    source = source.rearrange("p (b n) -> p b n", b=B)
                    act.wait_ge(s_zero, 2)
                else:
                    target = (res if i < 2 * CT else gate)[:, i % CT, :]
                act.activation(target, source, ACT.Silu, bias=b_in[:, i:i + 1]).then_inc(s_silu, 1)

            for i in range(2 * CT):
                silu_in(i)
                if i >= CT:
                    act.wait_ge(s_cv, 3 * (i - CT + 1))
                    act.activation(xf[:, i - CT, :], conv[:, i - CT].rearrange("p b n -> p (b n)"), ACT.Silu).then_inc(s_xf, 1)
            act.wait_ge(s_w, LOADED)
            act.activation(a_neg[:], a_log[:], ACT.Exp).then_inc(s_sa, 1)
            act.wait_ge(s_ab, 1)
            act.activation(soft[:, EX], soft[:, AB], ACT.Exp, scale=-1.0).then_inc(s_sa, 1)
            for i in range(TT // 2):
                act.wait_ge(s_xt, i + 1)
                act.activation(xf_t[:, 2 * i:2 * i + 2, :].rearrange("p a n -> p (a n)"), psum[:, i, :], ACT.Copy).then_inc(s_xto, 1)
            act.wait_ge(s_so, 2)
            act.activation(soft[:, LN], soft[:, U1], ACT.Ln).then_inc(s_sa, 1)
            act.wait_ge(s_rows, 1)
            act.activation(rows[:, :, :, 0, 0:S], rows[:, :, :, 0, 0:S], ACT.Exp, scale=-1.0).then_inc(s_sa, 1)
            for i in range(2 * CT, 3 * CT):
                silu_in(i)
            def take_channels(h):
                act.wait_ge(s_xp, h + 1)
                act.activation(x_perm[:, h, :], psum[:, 4 + 2 * h:6 + 2 * h, :].rearrange("p a n -> p (a n)"),
                               ACT.Copy).then_inc(s_xpo, 1)

            for h in range(HEADS):
                act.wait_ge(s_rp, h + 1)
                act.activation(parts[:, h, :], psum[0:3 * QROWS, 2 * h:2 * h + 2, :].rearrange("p a n -> p (a n)"),
                               ACT.Copy).then_inc(s_hi, 1)
                if h:
                    take_channels(h - 1)
                act.wait_ge(s_rest, h + 1)
                act.activation(parts[QROWS:2 * QROWS, h, :], rest[QROWS:2 * QROWS], ACT.Copy)
                act.activation(parts[2 * QROWS:3 * QROWS, h, :], rest[2 * QROWS:3 * QROWS], ACT.Copy).then_inc(s_mid, 1)
            take_channels(HEADS - 1)
            for i in range(STEPS):
                act.wait_ge(s_bdt, i + 1)
                if i >= DEEP:
                    act.wait_ge(s_u, i - DEEP + 1)
                act.activation(dtb[:, i % DEEP, :], psum[:, 2 + i % 2, :], ACT.Copy).then_inc(s_dtb, 1)
                if i in (4, 5):
                    act.activation(gate[:, i - 4, :], gate[:, i - 4, :], ACT.Silu).then_inc(s_gate, 1)
                if i % S == 4 and i > S:
                    scanned(act, i // S - 1)
            scanned(act, PAIRS - 1)
            for i in range(TT // 2):
                act.wait_ge(s_yt, i + 1)
                act.activation(y_t[:, 2 * i:2 * i + 2, :].rearrange("p a n -> p (a n)"), psum[:, i, :], ACT.Copy).then_inc(s_yto, 1)
            for i in range(TT // 2):
                act.wait_ge(s_ob, i + 1)
                act.activation(silu_out[:, i % DEEP, :], silu_out[:, i % DEEP, :], ACT.Silu).then_inc(s_so2, 1)

        @block.tensor
        def _(pe):
            for h in range(HEADS):
                for r in range(NT):
                    for t in range(NT):
                        last = pe.transpose(psum[:, 4 + h, N * r + P * t:N * r + P * t + P],
                                            order[:, h, t, P * r:P * r + P], k.ident_sb[:])
                last.then_inc(s_ot, 1)

            def project_in(i):
                for half in range(2):
                    for t in range(CT):
                        last = pe.matmul(psum[:, BANKS_IN[i] + half, :], w_in[:, t, P * i:P * i + P],
                                         k.h[:, t, 2 * half:2 * half + 2, :].rearrange("p b n -> p (b n)"),
                                         start=(t == 0), stop=(t == CT - 1))
                last.then_inc(s_in, 1)

            pe.wait_ge(s_w_in, 16 * 3)
            for i in range(2 * CT):
                if i >= 2:
                    pe.wait_ge(s_silu, i - 1)
                project_in(i)
            pe.wait_ge(s_xf, CT)
            pe.wait_ge(s_w, LOADED)
            W = HEADS * (2 * S + 1)
            for T in range(TT):
                for t in range(CT):
                    last = pe.matmul(psum[:, 6, W * T:W * T + W], xf[:, t, P * T:P * T + P], w_dbc[:, t, :],
                                     start=(t == 0), stop=(t == CT - 1))
            last.then_inc(s_dbc, 1)
            pe.wait_ge(s_silu, 2 * CT)
            for i in range(TT // 2):
                for a in range(2):
                    for t in range(CT):
                        last = pe.transpose(psum[:, i, C * a + P * t:C * a + P * t + P],
                                            xf[:, t, P * (2 * i + a):P * (2 * i + a) + P], k.ident_sb[:])
                last.then_inc(s_xt, 1)
            pe.wait_ge(s_so, 1)
            pe.wait_ge(s_xto, TT // 2)
            for i in range(2 * CT, 3 * CT):
                project_in(i)
            pe.wait_ge(s_rows, 3 + 2 * HEADS)
            pe.wait_ge(s_oto, HEADS)
            for h in range(HEADS):
                if h == 1:
                    pe.wait_ge(s_silu, 3 * CT)
                for b in range(B):
                    for t in range(NT):
                        last = pe.matmul(psum[0:3 * QROWS, 2 * h + b // 2, N * (b % 2):N * (b % 2) + N],
                                         rows[:, NT * b + t, h].rearrange("p q j -> p (q j)"), order[:, h, t, :],
                                         start=(t == 0), stop=(t == NT - 1))
                last.then_inc(s_rp, 1)
            for h in range(HEADS):
                for b in range(B):
                    for t in range(NT):
                        last = pe.matmul(psum[:, 4 + 2 * h + b // 2, N * (b % 2):N * (b % 2) + N],
                                         xf_t[:, NT * b + t, P * h:P * h + P], order[:, h, t, :],
                                         start=(t == 0), stop=(t == NT - 1))
                last.then_inc(s_xp, 1)
            pe.wait_ge(s_zero, 3 + HEADS)
            pe.wait_ge(s_xpo, HEADS)
            pe.wait_ge(s_parts, HEADS)

            def sum_states(i):
                pair, s = i // S, i % S
                pe.wait_ge(s_cm, i + 1)
                if pair >= 2 and s == 0:
                    pe.wait_ge(s_ys, pair - 1)
                pe.matmul(psum[:, 6 + pair % 2, :], k.ident_sb[:], prod[:, i % DEEP, :],
                          start=(s == 0), stop=(s == S - 1)).then_inc(s_acc, 1)

            def spread(i, row, bank, done):
                h, half = i // S // 2, i // S % 2
                pe.matmul(psum[:, bank + i % 2, :], select[:, row * S + i % S, :],
                          parts[:, h, BANK * half:BANK * half + BANK], start=True, stop=True).then_inc(done, 1)

            spread(0, 1, 2, s_bdt)
            spread(1, 1, 2, s_bdt)
            spread(0, 0, 0, s_bda)
            for i in range(STEPS):
                if i + 2 < STEPS:
                    pe.wait_ge(s_dtb, i + 1)
                    spread(i + 2, 1, 2, s_bdt)
                if i + 1 < STEPS:
                    if i >= 1:
                        pe.wait_ge(s_scan, i)
                    spread(i + 1, 0, 0, s_bda)
                if i >= 2:
                    pe.wait_ge(s_cm, i - 1)
                spread(i, 2, 4, s_bc)
                if i >= 2:
                    sum_states(i - 2)
            sum_states(STEPS - 2)
            sum_states(STEPS - 1)
            pe.wait_ge(s_scan, STEPS)
            for i in range(TT // 2):
                for a in range(2):
                    for t in range(CT):
                        last = pe.transpose(psum[:, i, C * a + P * t:C * a + P * t + P],
                                            k.x1[:, t].rearrange("p b n -> p (b n)")[:, P * (2 * i + a):P * (2 * i + a) + P],
                                            k.ident_sb[:])
                last.then_inc(s_x1t, 1)
            pe.wait_ge(s_ys, PAIRS)
            for i in range(TT // 2):
                pe.wait_ge(s_x1o, i + 1)
                for a in range(2):
                    for h in range(HEADS):
                        last = pe.transpose(psum[:, i, C * a + P * h:C * a + P * h + P],
                                            y_scan[:, h, P * (2 * i + a):P * (2 * i + a) + P], k.ident_sb[:])
                last.then_inc(s_yt, 1)
            for half in range(2):
                pe.wait_ge(s_yto, TT // 4 * (half + 1))
                for h in range(HEADS):
                    for b in range(2 * half, 2 * half + 2):
                        for t in range(NT):
                            last = pe.matmul(psum[:, 4 + 2 * h + half, N * (b % 2):N * (b % 2) + N],
                                             y_t[:, NT * b + t, P * h:P * h + P], order_t[:, h, t, :],
                                             start=(t == 0), stop=(t == NT - 1))
                    last.then_inc(s_un, 1)
            for i in range(TT // 2):
                pe.wait_ge(s_y, 3 * HEADS * (i // 2 + 1))
                for a in range(2):
                    T = 2 * i + a
                    for t in range(CT):
                        last = pe.matmul(psum[:, i, C * a:C * a + C], y[:, t, P * T:P * T + P], w_out[:, t, :],
                                         start=(t == 0), stop=(t == CT - 1))
                last.then_inc(s_op, 1)


class LayerNorm:

    def __init__(self, name, sb, sem, eps):
        self.eps = eps
        self.raw = sb(f"{name}_raw", [P, TT, 6])
        self.moments = sb(f"{name}_moments", [P, TT, 2])
        self.var = sb(f"{name}_var", [P, TT])
        self.sd = sb(f"{name}_sd", [P, TT])
        self.rstd = sb(f"{name}_rstd", [P, TT])
        self.s_raw = sem(f"{name}_raw")
        self.s_moments = sem(f"{name}_moments")
        self.s_sd = sem(f"{name}_sd")
        self.s_rstd = sem(f"{name}_rstd")
        self.s_out = sem(f"{name}_out")

    def statistics(self, dve, t):
        for T in range(TT):
            dve.bn_stats(self.raw[:, T, :], t[:, T, :]).then_inc(self.s_raw, 1)
        for T in range(TT):
            dve.wait_ge(self.s_raw, T + 1)
            last = dve.bn_aggr(self.moments[:, T, :], self.raw[:, T, :])
        last.then_inc(self.s_moments, 1)
        dve.wait_ge(self.s_moments, 1)
        dve.tensor_scalar(self.var[:], self.moments[:, :, 1], self.eps, None, ALU.add).then_inc(self.s_moments, 1)

    def deviation(self, act):
        act.wait_ge(self.s_moments, 2)
        act.activation(self.sd[:], self.var[:], ACT.Sqrt).then_inc(self.s_sd, 1)

    def normalise(self, dve, t, out):
        dve.wait_ge(self.s_sd, 1)
        dve.reciprocal(self.rstd[:], self.sd[:]).then_inc(self.s_rstd, 1)
        dve.wait_ge(self.s_rstd, 1)
        for T in range(TT):
            dve.tensor_scalar(out[:, T, :], t[:, T, :], self.moments[:, T, 0:1], self.rstd[:, T:T + 1],
                              ALU.subtract, ALU.mult).then_inc(self.s_out, 1)


COMBOS = ((0, 0), (0, 1), (0, 2), (1, 0), (1, 1), (2, 0))
STACK = len(COMBOS) * HD
MAXROWS = 2
GROUP = 8
GROUPS = B * AH // GROUP
SLOTS_G = 4


def image_and_half(g):
    return 2 * (g // 4) + g % 2, g // 2 % 2


FIRST_MAXIMA = GROUP + GROUP // 2


VALUES_AFTER = (1, 4, GROUP, GROUP + 2)


def maxima_ahead(i):
    catching_up = GROUP // 2
    first = FIRST_MAXIMA + 3 * min(i, catching_up) + 2 * max(i - catching_up, 0)
    return range(first, min(first + (3 if i < catching_up else 2), GROUP * GROUPS))


def maxima_complete(i):
    for g in range(1, GROUPS):
        if i > 0 and GROUP * g + GROUP - 1 in maxima_ahead(i - 1):
            return g
    return 0


def attention(nc, sem, sbuf, psum, k, w, causal, tag, prefetch):
    with ExitStack() as ctx:
        def sb(name, shape, dt=F32):
            return ctx.enter_context(nc.sbuf_tensor(f"{tag}_{name}", shape, dt))

        def sm(name):
            return sem(f"{tag}_{name}")

        wqkv = sb("wqkv", [P, CT, 3 * C])
        w_proj = sb("w_proj", [P, CT, C])
        b_proj = sb("b_proj", [1, C])
        ones = sb("ones_row", [1, P])
        ident16 = sb("ident16", [P, P], BF16)
        bans = sb("bans", [P, 3, P], BF16)
        h_t = k.x1[:].rearrange("p t b n -> p t (b n)")
        normed = k.h[:].rearrange("p t b n -> p (t b n)").rearrange("p (t c) -> p t c", c=C)
        rest = sb("rest", [P, 2, TOK])
        parts = sb("parts", [P, CT, 2, 3, TOK], BF16)
        stack_q = sb("stack_q", [STACK + MAXROWS, SLOTS_G, GROUP, N], BF16)
        stack_k = sb("stack_k", [STACK + MAXROWS, SLOTS_G, GROUP, N], BF16)
        values = sb("values", [P, TT, AH, 2 * HD])
        maxima = sb("maxima", [P, GROUPS, NT, GROUP])
        negated = sb("negated", [GROUP, SLOTS_G, MAXROWS, N], BF16)
        expo = sb("expo", [P, 2, 2, BANK])
        ctxn = rest[:, 0, :].rearrange("p (b t n) -> p b t n", b=2, t=CT)
        raw = rest[:, 1, :].rearrange("p (g n) -> p g n", g=2)
        inverse = sb("inverse", [P, 2, NT, GROUP])
        ctx_t = sb("ctx_t", [P, 2, NT, P])
        ln = LayerNorm(f"{tag}_ln", sb, sem, 1e-5)

        s_w = sm("weights_loaded")
        s_ones = sm("constants_set")
        s_ht = sm("h_transposed")
        s_hto = [sm("h_t_out_by_act"), sm("h_t_out_by_dve")]
        s_qk = sm("qk_projected")
        s_hi = sm("high_part")
        s_r = sm("remainder")
        s_mid = sm("middle_part")
        s_lo = sm("low_part")
        s_v = sm("v_projected")
        s_vo = sm("v_out")
        s_pd = sm("parts_in_dram")
        s_st = [sm(f"stack_loaded_{i}") for i in range(SLOTS_G)]
        s_sc = sm("scores_for_max")
        s_mx = sm("maxima")
        s_mt = sm("maxima_transposed")
        s_nh = sm("negated_high")
        s_nl = sm("negated_low")
        s_mr = [sm("max_rows_even"), sm("max_rows_odd")]
        s_s2 = sm("scores_less_max")
        s_ex = sm("exponentials")
        s_av = sm("values_weighted")
        s_raw = sm("contexts_out")
        s_ct = sm("contexts_transposed")
        s_inv = sm("denominators_inverted")
        s_div = sm("contexts_divided")
        s_cb = sm("contexts_turned_back")
        s_cn = sm("contexts_ready")
        s_pj = sm("projected")
        s_res = sm("residual_added")

        UNITS = GROUP // 2
        n1 = P if causal else 0
        WIDTH = 2 * N - n1
        block = ctx.enter_context(nc.Block())

        @block.sync
        def _(sp):
            for dst, src in ((wqkv, w["wqkv"]), (w_proj, w["w_proj"]), (b_proj, w["b_proj"]), (ones, k.dram["ones"]),
                             (ident16, k.dram["ident16"]), (bans, k.dram["bans"])):
                sp.dma_start(dst[:], src).then_inc(s_w, 16)

            def load_stacks(g):
                b, half = image_and_half(g)
                for which, stack in enumerate((stack_q, stack_k)):
                    sp.dma_start(stack[0:STACK, g % SLOTS_G],
                                 k.stacks_dram[which, :, GROUP * half:GROUP * half + GROUP, N * b:N * b + N]
                                 ).then_inc(s_st[g % SLOTS_G], 16)

            for i in range(2 * CT):
                t, which = i // 2, i % 2
                for part, done in enumerate((s_hi, s_mid, s_lo)):
                    sp.wait_ge(done, i + 1)
                    for c, combo in enumerate(COMBOS):
                        if combo[which] == part:
                            sp.dma_start(k.stacks_dram[which, HD * c:HD * c + HD, GROUP * t:GROUP * t + GROUP].rearrange("d h n -> h d n"),
                                         parts[:, t, which, part]).then_inc(s_pd, 16)
                if which:
                    sp.wait_ge(s_pd, 16 * len(COMBOS) * (i + 1))
                    for g in range(2 * t, 2 * t + 2):
                        load_stacks(g)

            for g in range(GROUPS - 1):
                sp.wait_ge(s_s2, UNITS * g + 1)
                prefetch(sp, g)
                if g >= 1 and g + 3 < GROUPS:
                    load_stacks(g + 3)

        @block.gpsimd
        def _(pool):
            pool.memset(values[:, :, :, HD:], 1.0).then_inc(s_ones, 1)
            pool.wait_ge(s_ones, 1)
            pool.memset(stack_k[STACK:, :, :, :], 1.0).then_inc(s_ones, 1)
            for g in range(GROUPS):
                pool.wait_ge(s_nl, g + 1)
                pool.wait_ge(s_nh, g + 1)
                for q in range(MAXROWS):
                    pool.dma_start(stack_q[STACK + q:STACK + q + 1, g % SLOTS_G], negated[:, g % SLOTS_G, q, :]
                                   ).then_inc(s_mr[g % 2], 16)

        @block.vector
        def _(dve):
            ln.statistics(dve, k.t)
            ln.normalise(dve, k.t, normed)
            for i in range(TT // 2):
                dve.wait_ge(s_ht, i + 1)
                if i % 2:
                    dve.tensor_copy(h_t[:, :, N * i:N * i + N], psum[:, i, :].rearrange("p (t n) -> p t n", t=CT)).then_inc(s_hto[1], 1)
            for i in range(2 * CT):
                source = psum[:, 2 * (i % 2):2 * (i % 2) + 2, :].rearrange("p a n -> p (a n)")
                t, which = i // 2, i % 2
                dve.wait_ge(s_hi, i + 1)
                dve.tensor_tensor(rest[:, i % 2, :], source, parts[:, t, which, 0, :], ALU.subtract).then_inc(s_r, 1)
                dve.wait_ge(s_mid, i + 1)
                dve.tensor_tensor(parts[:, t, which, 2, :], rest[:, i % 2, :], parts[:, t, which, 1, :],
                                  ALU.subtract).then_inc(s_lo, 1)

            def take_max(i):
                g, h = i // GROUP, i % GROUP
                dve.wait_ge(s_sc, i + 1)
                dve.tensor_reduce(maxima[:, g, :, h], psum[:, i % 2, :].rearrange("p (t m) -> p t m", t=NT),
                                  AX_X, ALU.max).then_inc(s_mx, 1)

            def negate(g):
                dve.wait_ge(s_nh, g + 1)
                dve.scalar_tensor_tensor(negated[:, g % SLOTS_G, 1, :], psum[0:GROUP, 0, 0:N], -1.0,
                                         negated[:, g % SLOTS_G, 0, :], ALU.mult, ALU.subtract).then_inc(s_nl, 1)

            def divide(g):
                turned = psum[:, 6 + g % 2, :].rearrange("p (a h d) -> p a h d", a=NT, h=GROUP)
                dve.wait_ge(s_ct, g + 1)
                dve.reciprocal(inverse[:, g % 2], turned[:, :, :, HD]).then_inc(s_inv, 1)
                dve.wait_ge(s_inv, g + 1)
                dve.tensor_tensor(ctx_t[:, g % 2].rearrange("p a (h d) -> p a h d", d=HD), turned[:, :, :, 0:HD],
                                  inverse[:, g % 2].unsqueeze(3).broadcast_to([P, NT, GROUP, HD]), ALU.mult).then_inc(s_div, 1)

            def add_residual(g):
                b, _ = image_and_half(g)
                dve.wait_ge(s_pj, b + 1)
                tile = k.t[:, NT * b:NT * b + NT, :].rearrange("p a n -> p (a n)")
                dve.tensor_tensor(tile, tile, psum[:, 6 + g % 2, :], ALU.add).then_inc(s_res, 1)

            for i in range(FIRST_MAXIMA):
                take_max(i)
                if i == GROUP - 1:
                    negate(0)
            for g in range(GROUPS):
                for unit in range(UNITS):
                    i = UNITS * g + unit
                    if maxima_complete(i):
                        negate(maxima_complete(i))
                    if unit == 0 and g >= 2 and image_and_half(g - 2)[1]:
                        add_residual(g - 2)
                    if unit == 1 and g >= 1:
                        divide(g - 1)
                    for ahead in maxima_ahead(i):
                        take_max(ahead)
            add_residual(GROUPS - 2)
            divide(GROUPS - 1)
            add_residual(GROUPS - 1)

        @block.scalar
        def _(act):
            ln.deviation(act)
            for i in range(0, TT // 2, 2):
                act.wait_ge(s_ht, i + 1)
                act.activation(h_t[:, :, N * i:N * i + N], psum[:, i, :].rearrange("p (t n) -> p t n", t=CT),
                               ACT.Copy).then_inc(s_hto[0], 1)
            for i in range(2 * CT):
                source = psum[:, 2 * (i % 2):2 * (i % 2) + 2, :].rearrange("p a n -> p (a n)")
                t, which = i // 2, i % 2
                act.wait_ge(s_qk, i + 1)
                act.activation(parts[:, t, which, 0, :], source, ACT.Copy).then_inc(s_hi, 1)
                act.wait_ge(s_r, i + 1)
                act.activation(parts[:, t, which, 1, :], rest[:, i % 2, :], ACT.Copy).then_inc(s_mid, 1)

            def take_values(i):
                act.wait_ge(s_v, i + 1)
                act.activation(values[:, 2 * i:2 * i + 2, :, 0:HD],
                               psum[:, 4 + i, :].rearrange("p (a h d) -> p a h d", a=2, h=AH), ACT.Copy).then_inc(s_vo, 1)

            for i in range(TT // 2 - 1):
                take_values(i)

            def negate(g):
                act.wait_ge(s_mt, g + 1)
                act.activation(negated[:, g % SLOTS_G, 0, :], psum[0:GROUP, 0, 0:N], ACT.Copy, scale=-1.0).then_inc(s_nh, 1)

            def take_contexts(g):
                act.wait_ge(s_av, UNITS * (g + 1))
                act.activation(raw[:, g % 2, :], psum[:, 6 + g % 2, :], ACT.Copy).then_inc(s_raw, 1)

            def take_back(g):
                b, half = image_and_half(g)
                act.wait_ge(s_cb, g + 1)
                act.activation(ctxn[:, b % 2, half, :], psum[:, 6 + g % 2, 0:N], ACT.Copy).then_inc(s_cn, 1)

            negate(0)
            take_values(TT // 2 - 1)
            for g in range(GROUPS):
                for unit in range(UNITS):
                    i = UNITS * g + unit
                    if maxima_complete(i):
                        negate(maxima_complete(i))
                    act.wait_ge(s_s2, i + 1)
                    if i >= 2:
                        act.wait_ge(s_av, i - 1)
                    act.activation(expo[:, i % 2, :, 0:WIDTH], psum[:, 2 + 2 * (i % 2):4 + 2 * (i % 2), 0:WIDTH],
                                   ACT.Exp, scale=HD ** -0.5).then_inc(s_ex, 1)
                    if unit == 0 and g >= 1:
                        take_contexts(g - 1)
                    if unit == 2 and g >= 1:
                        take_back(g - 1)
            take_contexts(GROUPS - 1)
            take_back(GROUPS - 1)

        @block.tensor
        def _(pe):
            for i in range(TT // 2):
                pe.wait_ge(ln.s_out, 2 * i + 2)
                for t in range(CT):
                    for a in range(2):
                        last = pe.transpose(psum[:, i, N * t + P * a:N * t + P * a + P],
                                            normed[:, 2 * i + a, P * t:P * t + P], k.ident_sb[:])
                last.then_inc(s_ht, 1)
            pe.wait_ge(s_w, 16 * 6)
            for i in range(2 * CT):
                t_out, which = i // 2, i % 2
                column = C * which + P * t_out
                if i >= 2:
                    pe.wait_ge(s_r, i - 1)
                for half in range(2):
                    if i == 0:
                        pe.wait_ge(s_hto[0], half + 1)
                        pe.wait_ge(s_hto[1], half + 1)
                    for t in range(CT):
                        last = pe.matmul(psum[:, 2 * (i % 2) + half, :], wqkv[:, t, column:column + P],
                                         h_t[:, t, BANK * half:BANK * half + BANK], start=(t == 0), stop=(t == CT - 1))
                last.then_inc(s_qk, 1)

            def project_values(T):
                for t in range(CT):
                    last = pe.matmul(psum[:, 4 + T // 2, C * (T % 2):C * (T % 2) + C], h_t[:, t, P * T:P * T + P],
                                     wqkv[:, t, 2 * C:], start=(t == 0), stop=(t == CT - 1))
                if T % 2:
                    last.then_inc(s_v, 1)

            for T in range(TT // 2):
                project_values(T)
            pe.wait_ge(s_r, 2 * CT)

            free_of_maxima = (-1, 0)

            def scores_for_max(i):
                g, h = i // GROUP, i % GROUP
                slot = g % SLOTS_G
                if h == 0:
                    pe.wait_ge(s_st[slot], 16 * 2 * (g // SLOTS_G + 1))
                if i >= 2:
                    pe.wait_ge(s_mx, i - 1)
                if i == free_of_maxima[0]:
                    pe.wait_ge(s_nl, free_of_maxima[1])
                for t in range(NT):
                    keys = P if causal and t == 0 else N
                    out = psum[:, i % 2, N * t:N * t + keys]
                    last = pe.matmul(out, stack_q[0:STACK, slot, h, P * t:P * t + P],
                                     stack_k[0:STACK, slot, h, 0:keys], start=True, stop=not causal)
                    if causal:
                        last = pe.matmul(psum[:, i % 2, N * t + P * t:N * t + P * t + P], ident16[:], bans[:, 0, :],
                                         start=False, stop=True)
                        if t == 0:
                            pe.matmul(psum[:, i % 2, P:N], ident16[:], bans[:, 2, :], start=True, stop=True)
                last.then_inc(s_sc, 1)

            def turn_maxima(g, taken):
                nonlocal free_of_maxima
                free_of_maxima = (taken, g + 1)
                pe.wait_ge(s_mx, taken)
                for t in range(NT):
                    last = pe.transpose(psum[0:GROUP, 0, P * t:P * t + P], maxima[:, g, t, :], k.ident_sb[:])
                last.then_inc(s_mt, 1)

            def scores_less_max(i):
                g, unit = i // UNITS, i % UNITS
                slot = g % SLOTS_G
                if unit == 0:
                    pe.wait_ge(s_mr[g % 2], 16 * MAXROWS * (g // 2 + 1))
                if i >= 2:
                    pe.wait_ge(s_ex, i - 1)
                for j in range(2):
                    h, bank = 2 * unit + j, 2 + 2 * (i % 2) + j
                    for m in range(NT):
                        first = n1 if m else 0
                        col = N * m
                        last = pe.matmul(psum[:, bank, col:col + N - first],
                                         stack_k[:, slot, h, P * m:P * m + P], stack_q[:, slot, h, first:N],
                                         start=True, stop=not causal)
                        if causal:
                            last = pe.matmul(psum[:, bank, col:col + P], ident16[:], bans[:, 1, :], start=False, stop=True)
                last.then_inc(s_s2, 1)

            def weigh_values(i):
                g, unit = i // UNITS, i % UNITS
                b, half = image_and_half(g)
                pe.wait_ge(s_ex, i + 1)
                if unit == 0 and g >= 2:
                    pe.wait_ge(s_cn, g - 1)
                    image, projected = image_and_half(g - 2)
                    if projected:
                        pe.wait_ge(s_res, image + 1)
                for j in range(2):
                    h = 2 * unit + j
                    q, col = 32 * (h % 4), N * (h // 4)
                    for m in range(NT):
                        first = n1 if m else 0
                        last = pe.matmul(psum[q:q + 32, 6 + g % 2, col + first:col + N],
                                         values[:, NT * b + m, GROUP * half + h, :], expo[:, i % 2, j, N * m:N * m + N - first],
                                         start=(m == 0), stop=(m == NT - 1))
                last.then_inc(s_av, 1)

            def turn_contexts(g):
                pe.wait_ge(s_raw, g + 1)
                for a in range(NT):
                    for j in range(NT):
                        last = pe.transpose(psum[:, 6 + g % 2, N * a + P * j:N * a + P * j + P],
                                            raw[:, g % 2, N * j + P * a:N * j + P * a + P], k.ident_sb[:])
                last.then_inc(s_ct, 1)

            def turn_back(g):
                pe.wait_ge(s_div, g + 1)
                for a in range(NT):
                    last = pe.transpose(psum[:, 6 + g % 2, P * a:P * a + P], ctx_t[:, g % 2, a, :], k.ident_sb[:])
                last.then_inc(s_cb, 1)

            def project(g):
                b, _ = image_and_half(g)
                pe.wait_ge(s_cn, g + 1)
                for a in range(NT):
                    out = psum[:, 6 + g % 2, C * a:C * a + C]
                    for t in range(CT):
                        pe.matmul(out, ctxn[:, b % 2, t, P * a:P * a + P], w_proj[:, t, :], start=(t == 0), stop=False)
                    last = pe.matmul(out, ones[:], b_proj[:], start=False, stop=True)
                last.then_inc(s_pj, 1)

            for i in range(FIRST_MAXIMA):
                scores_for_max(i)
                if i == GROUP - 1:
                    turn_maxima(0, GROUP)
                if i in VALUES_AFTER:
                    project_values(TT // 2 + VALUES_AFTER.index(i))
            pe.wait_ge(s_ones, 2)
            pe.wait_ge(s_vo, TT // 2)
            for g in range(GROUPS):
                for unit in range(UNITS):
                    i = UNITS * g + unit
                    scores_less_max(i)
                    if maxima_complete(i):
                        turn_maxima(maxima_complete(i), maxima_ahead(i - 1).stop)
                    if i:
                        weigh_values(i - 1)
                    if unit == 1 and g >= 1:
                        turn_contexts(g - 1)
                    if unit == 2 and g >= 1:
                        turn_back(g - 1)
                    if unit == 3 and g >= 1 and image_and_half(g - 1)[1]:
                        project(g - 1)
                    for ahead in maxima_ahead(i):
                        scores_for_max(ahead)
            weigh_values(UNITS * GROUPS - 1)
            turn_contexts(GROUPS - 1)
            turn_back(GROUPS - 1)
            project(GROUPS - 1)


CHUNK = 512
CHUNK_COLS = 2 * CT * CHUNK + CHUNK // P * C
RING_CHUNKS = 6
PAIRED = (MAXBLK + 1) // 2 * 2


def above_zero(count):
    return not isinstance(count, int) or count > 0


def load_chunk(sp, k, weights, chunks, n, loaded):
    place = CHUNK_COLS * (n % RING_CHUNKS)
    column = CHUNK_COLS * (n % chunks)
    sp.dma_start(k.ring[:, place:place + CHUNK_COLS], weights[n // chunks, :, column:column + CHUNK_COLS]).then_inc(loaded, 16)


def experts_ffn(nc, sem, sbuf, psum, k, w, chunks, s_loaded, tag, finish=None):
    RING_EXPERTS = RING_CHUNKS // chunks
    with ExitStack() as ctx:
        def sb(name, shape, dt=F32):
            return ctx.enter_context(nc.sbuf_tensor(f"{tag}_{name}", shape, dt))

        def sm(name):
            return sem(f"{tag}_{name}")

        gate_w = sb("gate_w", [P, CT, E])
        iota_e = sb("iota_e", [P, E])
        iota_b = sb("iota_b", [P, PAIRED])
        steps = sb("steps", [P, TT])
        earlier = sb("earlier", [P, 2, P], BF16)
        h_t = k.x1[:].rearrange("p t b n -> p t (b n)")
        normed = k.h[:].rearrange("p t b n -> p (t b n)").rearrange("p (t c) -> p t c", c=C)
        logits = sb("logits", [P, TT, E])
        top = sb("top", [P, TT, E])
        top_at = sb("top_at", [P, TT, E], U32)
        choice = sb("choice", [P, TT, 2])
        chosen = sb("chosen", [P, 2, TT, E])
        either = sb("either", [P, TT, E], BF16)
        share = sb("share", [P, 4, TT])
        count = sb("count", [P, E])
        over = sb("over", [P, E, TT])
        blocks = sb("blocks", [P, E])
        block_end = sb("block_end", [P, E])
        unit = sb("unit", [P, E])
        base = sb("base", [P, E])
        place = sb("place", [P, TT, E])
        taken = sb("taken", [P, 2, TT, E])
        slot = sb("slot", [P, 2, TT])
        edges = sb("edges", [P, PAIRED + 1])
        iota_p = sb("iota_p", [P, P])
        labels = sb("labels", [P, 2, TT, 2])
        behind = sb("behind", [P, 2, TT, PAIRED + 1])
        in_block = sb("in_block", [P, 2, TT, PAIRED])
        at_row = sb("at_row", [P, 2, TT])
        row_hot = sb("row_hot", [P, 2, TT, P], BF16)
        label_hot = sb("label_hot", [P, 2, TT, 2, PAIRED], BF16)
        unused = sb("unused", [P, PAIRED])
        number = sb("number", [P, PAIRED])
        own_slot = sb("own_slot", [P, PAIRED])
        from_row = sb("from_row", [P, PAIRED], U32)
        to_row = sb("to_row", [P, PAIRED], U32)
        past = sb("past", [P, PAIRED, E])
        expert = sb("expert", [P, 3, PAIRED])
        table = sb("table", [P, 2, PAIRED], I32)
        free_at = sb("free_at", [P, E], I32)
        from_now = sb("from_now", [P, 2], U32)
        to_now = sb("to_now", [P, 2], U32)
        xs = sb("xs", [P, 2, C])
        x_t = sb("x_t", [P, 2, CT, P])
        silu = sb("silu", [P, 2, CHUNK])
        gated = sb("gated", [P, 2, CHUNK])
        gated_t = sb("gated_t", [P, 2, CHUNK])
        y = sb("y", [P, 2, C])
        got = k.ring[:, 0:2 * TT * C].rearrange("p (t k c) -> p t k c", t=TT, k=2)
        ln = LayerNorm(f"{tag}_ln", sb, sem, 1e-5)

        s_w = sm("weights_loaded")
        s_ht = sm("h_transposed")
        s_hto = sm("h_t_out")
        s_lg = sm("logits")
        s_r = sm("router_steps")
        s_exp = sm("router_exp")
        s_rank = sm("ranks_and_counts")
        s_blk = sm("one_hot_blocks")
        s_hot = sm("one_hot_rows")
        s_lab = sm("labels_by_block")
        s_turn = sm("slots_turned_around")
        s_slot = sm("slots_ready")
        s_table = sm("table_ready")
        s_nd = sm("rows_in_dram")
        s_fn = sm("from_now_set")
        s_tn = sm("to_now_set")
        s_x = [sm("x_loaded_even"), sm("x_loaded_odd")]
        s_xt = sm("x_transposed")
        s_xto = sm("x_t_out")
        s_up = sm("up_products")
        s_si = sm("silu")
        s_g = sm("gated")
        s_gt = sm("gated_transposed")
        s_gto = sm("gated_t_out")
        s_dn = sm("down_products")
        s_y = sm("y_out")
        s_yd = [sm("y_stored_even"), sm("y_stored_odd")]
        s_got = [sm(f"results_gathered_{i}") for i in range(4)]
        s_t = sm("tokens_updated")
        s_ft = sm("final_transposed")
        s_fo = sm("final_out")
        s_st = sm("output_stored")

        X_BANK, Y_BANK, G_BANK = 7, 6, 4
        block = ctx.enter_context(nc.Block())
        PAIRS = (MAXBLK - 1) // 2
        assert MAXBLK % 2 == 1

        @block.sync
        def _(sp):
            for dst, src in ((gate_w, w["gate"]), (iota_e, k.dram["iota_e"]), (iota_b, k.dram["iota_b"]), (steps, k.dram["steps"]),
                             (earlier, k.dram["earlier"]), (edges, k.dram["edges"]), (iota_p, k.dram["iota_p"]),
                             (labels, k.dram["labels"]), (own_slot, k.dram["own_slot"])):
                sp.dma_start(dst[:], src).then_inc(s_w, 16)
            sp.wait_ge(ln.s_out, TT)
            for c in range(2):
                sp.dma_start(k.rows_in[0:2 * TOK].rearrange("(t k p) c -> k p t c", k=2, p=P)[c], normed).then_inc(s_nd, 16)
            sp.wait_ge(s_table, 1)
            for e in range(RING_EXPERTS, E):
                done = sp.value_load(free_at[0:1, e - RING_EXPERTS:e - RING_EXPERTS + 1], min_val=1, max_val=MAXBLK)
                sp.wait_ge(s_loaded, 16 * chunks * e)
                sp.wait_ge(s_y, done)
                for n in range(chunks * e, chunks * e + chunks):
                    load_chunk(sp, k, w["experts"], chunks, n, s_loaded)
            sp.wait_ge(s_yd[0], 16 * (MAXBLK + 1) // 2)
            sp.wait_ge(s_yd[1], 16 * (MAXBLK // 2))
            for i in range(TT // 2):
                sp.dma_start(got[:, 2 * i:2 * i + 2],
                             k.rows_out[4 * P * i:4 * P * i + 4 * P].rearrange("(t k p) c -> p t k c", k=2, p=P)).then_inc(s_got[i], 16)
            if finish is not None:
                for i in range(TT // 2):
                    sp.wait_ge(s_fo, i + 1)
                    sp.dma_start(finish[i], k.x1[:, :, i, :]).then_inc(s_st, 16)
                sp.wait_ge(s_st, 16 * TT // 2)

        @block.gpsimd
        def _(pool):
            pool.wait_ge(s_w, 16 * 9)
            pool.wait_ge(s_blk, 1)
            for c in range(2):
                for value in range(2):
                    pool.tensor_tensor(label_hot[:, c, :, value, :], in_block[:, c],
                                       labels[:, c, :, value].unsqueeze(2).broadcast_to([P, TT, PAIRED]), ALU.mult).then_inc(s_lab, 1)
            pool.wait_ge(s_slot, 1)
            pool.wait_ge(s_nd, 32)

            def load_x(j, odd, turned=None):
                if turned is not None:
                    pool.wait_ge(s_xt, turned)
                pool.tensor_copy(from_now[:, odd:odd + 1], from_row[:, bass.ds(j, 1)]).then_inc(s_fn, 1)
                pool.wait_ge(s_fn, j + 1)
                pool.nop(nofuse=True)
                pool.indirect_dma_start(out=xs[:, odd, :], out_offset=None, in_=k.rows_in,
                                        in_offset=bass.IndirectOffsetOnAxis(ap=from_now[:, odd:odd + 1], axis=0)
                                        ).then_inc(s_x[odd], 16)

            def store_y(j, odd):
                pool.wait_ge(s_y, j + 1)
                pool.tensor_copy(to_now[:, odd:odd + 1], to_row[:, bass.ds(j, 1)]).then_inc(s_tn, 1)
                pool.wait_ge(s_tn, j + 1)
                pool.nop(nofuse=True)
                pool.indirect_dma_start(out=k.rows_out, out_offset=bass.IndirectOffsetOnAxis(ap=to_now[:, odd:odd + 1], axis=0),
                                        in_=y[:, odd, :], in_offset=None).then_inc(s_yd[odd], 16)

            load_x(0, 0)
            load_x(1, 1)
            for j in (2, 3):
                load_x(j, j % 2, j - 1)

            def turn(i, more=True):
                for odd in (1, 0):
                    j = 2 * i + (1 if odd else 2)
                    if more:
                        load_x(j + 3, 1 - odd, j + 2)
                    store_y(j - 1, 1 - odd)

            turn(0)
            with pool.Fori(1, PAIRS - 1) as i:
                turn(i)
            turn(PAIRS - 1, more=False)
            store_y(MAXBLK - 1, 0)

        @block.vector
        def _(dve):
            ln.statistics(dve, k.t)
            ln.normalise(dve, k.t, normed)
            for i in range(1, TT // 2, 2):
                dve.wait_ge(s_ht, i + 1)
                dve.tensor_copy(h_t[:, :, N * i:N * i + N], psum[:, i, :].rearrange("p (t n) -> p t n", t=CT)).then_inc(s_hto, 1)
            n = 0

            def step(ins):
                nonlocal n
                n += 1
                ins.then_inc(s_r, 1)
                dve.wait_ge(s_r, n)

            dve.wait_ge(s_lg, 1)
            step(dve.tensor_copy(logits[:].rearrange("p t e -> p (t e)"), psum[:, 4, 0:TT * E]))
            for T in range(TT):
                last = dve.max(top[:, T, :], logits[:, T, :])
            step(last)
            for T in range(TT):
                last = dve.max_index(top_at[:, T, :], top[:, T, :], logits[:, T, :])
            step(last)
            step(dve.tensor_tensor(share[:, 0, :], top[:, :, 1], top[:, :, 0], ALU.subtract))
            step(dve.tensor_copy(choice[:], top_at[:, :, 0:2]))
            every = [P, TT, E]
            for c in range(2):
                step(dve.tensor_tensor(chosen[:, c], iota_e[:].unsqueeze(1).broadcast_to(every),
                                       choice[:, :, c].unsqueeze(2).broadcast_to(every), ALU.is_equal))
            step(dve.tensor_tensor(either[:], chosen[:, 0], chosen[:, 1], ALU.add))
            dve.wait_ge(s_exp, 1)
            step(dve.tensor_scalar(share[:, 1, :], share[:, 0, :], 1.0, None, ALU.add))
            step(dve.reciprocal(share[:, 2, :], share[:, 1, :]))
            step(dve.tensor_tensor(share[:, 3, :], share[:, 0, :], share[:, 2, :], ALU.mult))
            dve.wait_ge(s_rank, 1)
            step(dve.tensor_copy(count[:], psum[:, 6, 0:E]))
            wide = [P, E, TT]
            step(dve.tensor_tensor(over[:], count[:].unsqueeze(2).broadcast_to(wide),
                                   steps[:].unsqueeze(1).broadcast_to(wide), ALU.is_gt))
            step(dve.tensor_reduce(blocks[:], over[:], AX_X, ALU.add))
            step(dve.tensor_scalar(blocks[:], blocks[:], 1.0, None, ALU.max))
            step(dve.memset(unit[:], 1.0))
            step(dve.tensor_tensor_scan(block_end[:], unit[:], blocks[:], 0.0, ALU.mult, ALU.add))
            step(dve.tensor_tensor(base[:], block_end[:], blocks[:], ALU.subtract))
            step(dve.tensor_scalar(base[:], base[:], float(P), None, ALU.mult))
            step(dve.tensor_tensor(place[:], psum[:, 5, 0:TT * E].rearrange("p (t e) -> p t e", t=TT),
                                   base[:].unsqueeze(1).broadcast_to(every), ALU.add))
            for c in range(2):
                step(dve.tensor_tensor(taken[:, c], place[:], chosen[:, c], ALU.mult))
            step(dve.tensor_reduce(slot[:].rearrange("p c t -> p (c t)"), taken[:].rearrange("p c t e -> p (c t) e"),
                                   AX_X, ALU.add))
            dve.wait_ge(s_w, 16 * 9)
            flat = "p c t b -> p (c t) b"
            many = slot[:].rearrange("p c t -> p (c t)").unsqueeze(2)
            step(dve.tensor_tensor(behind[:].rearrange(flat), many.broadcast_to([P, 2 * TT, PAIRED + 1]),
                                   edges[:].unsqueeze(1).broadcast_to([P, 2 * TT, PAIRED + 1]), ALU.is_ge))
            dve.tensor_tensor(in_block[:], behind[:, :, :, 0:PAIRED], behind[:, :, :, 1:], ALU.subtract).then_inc(s_blk, 1)
            step(dve.tensor_reduce(at_row[:].rearrange("p c t -> p (c t)"), behind[:, :, :, 1:].rearrange(flat), AX_X, ALU.add))
            step(dve.scalar_tensor_tensor(at_row[:], at_row[:], float(-P), slot[:], ALU.mult, ALU.add))
            for c in range(2):
                dve.tensor_tensor(row_hot[:, c], iota_p[:].unsqueeze(1).broadcast_to([P, TT, P]),
                                  at_row[:, c].unsqueeze(2).broadcast_to([P, TT, P]), ALU.is_equal).then_inc(s_hot, 1)
            dve.wait_ge(s_turn, 1)
            tile_of, token_of = psum[:, 7, 0:PAIRED], psum[:, 7, PAIRED:2 * PAIRED]
            step(dve.tensor_copy(number[:], token_of))
            step(dve.scalar_tensor_tensor(unused[:], tile_of, 1.0, own_slot[:], ALU.is_lt, ALU.mult))
            step(dve.scalar_tensor_tensor(number[:], tile_of, float(P), number[:], ALU.mult, ALU.add))
            step(dve.tensor_scalar(from_row[:], number[:], float(-P), 0.0, ALU.add, ALU.max))
            dve.scalar_tensor_tensor(to_row[:], number[:], float(-P), unused[:], ALU.add, ALU.add).then_inc(s_slot, 1)
            wide = [P, PAIRED, E]
            step(dve.tensor_tensor(past[:], block_end[:].unsqueeze(1).broadcast_to(wide),
                                   iota_b[:].unsqueeze(2).broadcast_to(wide), ALU.is_le))
            step(dve.tensor_reduce(expert[:, 0, :], past[:], AX_X, ALU.add))
            step(dve.tensor_scalar(expert[:, 0, :], expert[:, 0, :], float(E - 1), None, ALU.min))
            step(dve.tensor_scalar(expert[:, 1, :], expert[:, 0, :], float(RING_EXPERTS), float(-RING_EXPERTS),
                                   ALU.is_ge, ALU.mult))
            step(dve.tensor_tensor(expert[:, 1, :], expert[:, 0, :], expert[:, 1, :], ALU.add))
            for turn in range(2, (E - 1) // RING_EXPERTS + 1):
                step(dve.tensor_scalar(expert[:, 2, :], expert[:, 0, :], float(turn * RING_EXPERTS),
                                       float(-RING_EXPERTS), ALU.is_ge, ALU.mult))
                step(dve.tensor_tensor(expert[:, 1, :], expert[:, 1, :], expert[:, 2, :], ALU.add))
            step(dve.tensor_scalar(table[:, 0, :], expert[:, 1, :], float(chunks * CHUNK_COLS), None, ALU.mult))
            step(dve.tensor_scalar(expert[:, 2, :], expert[:, 0, :], 1.0, float(RING_EXPERTS), ALU.add, ALU.max))
            step(dve.tensor_scalar(table[:, 1, :], expert[:, 2, :], 16.0 * chunks, None, ALU.mult))
            dve.tensor_copy(free_at[:], block_end[:]).then_inc(s_table, 1)

            def gate(q, b):
                dve.wait_ge(s_up, 2 * q + 2)
                dve.wait_ge(s_si, q + 1)
                dve.tensor_tensor(gated[:, b, :], silu[:, b, :], psum[:, 2 * b + 1, :], ALU.mult).then_inc(s_g, 1)

            def take_x(j, b):
                loads = dve.value_load(table[0:1, 1, bass.ds(j, 1)], min_val=16 * chunks, max_val=16 * chunks * E)
                dve.wait_ge(s_loaded, loads)
                dve.wait_ge(s_xt, j + 1)
                dve.tensor_copy(x_t[:, b].rearrange("p t n -> p (t n)"), psum[:, X_BANK, 0:C]).then_inc(s_xto, 1)

            def take_y(j, b, stored):
                dve.wait_ge(s_dn, chunks * (j + 1))
                if above_zero(stored):
                    dve.wait_ge(s_yd[b], stored)
                dve.tensor_copy(y[:, b, :], psum[:, Y_BANK, 0:C]).then_inc(s_y, 1)

            dve.wait_ge(s_table, 1)
            take_x(0, 0)
            if chunks == 2:
                gate(0, 0)
            gate(chunks - 1, chunks - 1)
            take_x(1, 1)
            def turn(i):
                for odd in (1, 0):
                    j = 2 * i + (1 if odd else 2)
                    if chunks == 2:
                        gate(2 * j, 0)
                        take_y(j - 1, 1 - odd, 16 * i)
                        gate(2 * j + 1, 1)
                        take_x(j + 1, 1 - odd)
                    else:
                        gate(j, odd)
                        take_x(j + 1, 1 - odd)
                        take_y(j - 1, 1 - odd, 16 * i)

            turn(0)
            with dve.Fori(1, PAIRS) as i:
                turn(i)
            take_y(MAXBLK - 1, 0, 16 * PAIRS)
            for i in range(TT // 2):
                dve.wait_ge(s_got[i], 16)
                for c in range(2):
                    for a in range(2):
                        T = 2 * i + a
                        if c:
                            dve.wait_ge(s_t, 4 * i + a + 1)
                        dve.scalar_tensor_tensor(k.t[:, T, :], got[:, T, c, :], share[:, 2 + c, T:T + 1], k.t[:, T, :],
                                                 ALU.mult, ALU.add).then_inc(s_t, 1)

        @block.scalar
        def _(act):
            ln.deviation(act)
            for i in range(0, TT // 2, 2):
                act.wait_ge(s_ht, i + 1)
                act.activation(h_t[:, :, N * i:N * i + N], psum[:, i, :].rearrange("p (t n) -> p t n", t=CT),
                               ACT.Copy).then_inc(s_hto, 1)
            act.wait_ge(s_r, 4)
            act.activation(share[:, 0, :], share[:, 0, :], ACT.Exp).then_inc(s_exp, 1)

            def silu_of(q, b):
                act.wait_ge(s_up, 2 * q + 1)
                act.activation(silu[:, b, :], psum[:, 2 * b, :], ACT.Silu).then_inc(s_si, 1)

            def take_gated(q, b):
                act.wait_ge(s_gt, q + 1)
                act.activation(gated_t[:, b, :], psum[:, G_BANK + b, :], ACT.Copy).then_inc(s_gto, 1)

            silu_of(0, 0)
            if chunks == 2:
                take_gated(0, 0)
                silu_of(1, 1)
            def turn(i):
                for odd in (1, 0):
                    j = 2 * i + (1 if odd else 2)
                    for c in range(chunks):
                        b = c if chunks == 2 else odd
                        take_gated(chunks * j + c - 1, 1 - b)
                        silu_of(chunks * j + c, b)

            turn(0)
            with act.Fori(1, PAIRS) as i:
                turn(i)
            take_gated(chunks * MAXBLK - 1, chunks - 1)
            if finish is not None:
                for i in range(TT // 2):
                    act.wait_ge(s_ft, i + 1)
                    act.activation(k.x1[:, :, i, :], psum[:, i, :].rearrange("p (t n) -> p t n", t=CT), ACT.Copy).then_inc(s_fo, 1)

        @block.tensor
        def _(pe):
            for i in range(TT // 2):
                pe.wait_ge(ln.s_out, 2 * i + 2)
                for t in range(CT):
                    for a in range(2):
                        last = pe.transpose(psum[:, i, N * t + P * a:N * t + P * a + P],
                                            normed[:, 2 * i + a, P * t:P * t + P], k.ident_sb[:])
                last.then_inc(s_ht, 1)
            pe.wait_ge(s_w, 16 * 9)
            pe.wait_ge(s_hto, TT // 2)
            for T in range(TT):
                for t in range(CT):
                    last = pe.matmul(psum[:, 4, E * T:E * T + E], h_t[:, t, P * T:P * T + P], gate_w[:, t, :],
                                     start=(t == 0), stop=(t == CT - 1))
            last.then_inc(s_lg, 1)
            pe.wait_ge(s_r, 8)
            ranks = psum[:, 5, 0:TT * E]
            pe.matmul(ranks, earlier[:, 0, :], either[:].rearrange("p t e -> p (t e)"), start=True, stop=False)
            for T in range(TT - 1):
                pe.matmul(ranks[:, E * (T + 1):].rearrange("p (t e) -> p t e", e=E), earlier[:, 1, :],
                          either[:, T:T + 1, :].broadcast_to([P, TT - 1 - T, E]), start=False, stop=(T == TT - 2))
            for T in range(TT):
                last = pe.matmul(psum[:, 6, 0:E], earlier[:, 1, :], either[:, T, :], start=(T == 0), stop=(T == TT - 1))
            last.then_inc(s_rank, 1)
            for c in range(2):
                pe.wait_ge(s_hot, c + 1)
                pe.wait_ge(s_lab, 2 * (c + 1))
                for T in range(TT):
                    last = pe.matmul(psum[:, 7, 0:2 * PAIRED], row_hot[:, c, T, :], label_hot[:, c, T].rearrange("p l b -> p (l b)"),
                                     start=(c == 0 and T == 0), stop=(c == 1 and T == TT - 1))
            last.then_inc(s_turn, 1)
            pe.wait_ge(s_table, 1)

            def turn_x(j, b, loads):
                pe.wait_ge(s_x[b], loads)
                if above_zero(j):
                    pe.wait_ge(s_xto, j)
                for t in range(CT):
                    last = pe.transpose(psum[:, X_BANK, P * t:P * t + P], xs[:, b, P * t:P * t + P], k.ident_sb[:])
                last.then_inc(s_xt, 1)

            def up(q, xb, b, at, c):
                for side in range(2):
                    for t in range(CT):
                        start = CHUNK_COLS * c + CHUNK * (CT * side + t)
                        last = pe.matmul(psum[:, 2 * b + side, :], x_t[:, xb, t, :],
                                         k.ring[:, bass.ds(at + start, CHUNK)], start=(t == 0), stop=(t == CT - 1))
                    last.then_inc(s_up, 1)

            def turn_gated(q, b):
                pe.wait_ge(s_g, q + 1)
                for a in range(CHUNK // P):
                    last = pe.transpose(psum[:, G_BANK + b, P * a:P * a + P], gated[:, b, P * a:P * a + P], k.ident_sb[:])
                last.then_inc(s_gt, 1)

            def down(q, b, at, c):
                pe.wait_ge(s_gto, q + 1)
                for a in range(CHUNK // P):
                    start = CHUNK_COLS * c + 2 * CT * CHUNK + C * a
                    last = pe.matmul(psum[:, Y_BANK, 0:C], gated_t[:, b, P * a:P * a + P],
                                     k.ring[:, bass.ds(at + start, C)], start=(c == 0 and a == 0),
                                     stop=(c == chunks - 1 and a == CHUNK // P - 1))
                last.then_inc(s_dn, 1)

            def ring_column(j):
                return pe.value_load(table[0:1, 0, bass.ds(j, 1)], min_val=0,
                                     max_val=(RING_EXPERTS - 1) * chunks * CHUNK_COLS)

            pe.wait_ge(s_slot, 1)
            at = ring_column(0)
            turn_x(0, 0, 16)
            pe.wait_ge(s_xto, 1)
            up(0, 0, 0, at, 0)
            if chunks == 2:
                turn_gated(0, 0)
                up(1, 0, 1, at, 1)
            turn_x(1, 1, 16)
            if chunks == 2:
                down(0, 0, at, 0)

            def turn(i):
                at = ring_column(2 * i)
                for odd in (1, 0):
                    j = 2 * i + (1 if odd else 2)
                    at_before, at = at, ring_column(j)
                    for c in range(chunks):
                        b = c if chunks == 2 else odd
                        q = chunks * j + c
                        turn_gated(q - 1, 1 - b)
                        if c == 0:
                            pe.wait_ge(s_xto, j + 1)
                        up(q, odd, b, at, c)
                        if c == chunks - 1:
                            turn_x(j + 1, 1 - odd, 16 * (i + 2))
                            before = j if chunks == 2 else j - 1
                            if above_zero(before):
                                pe.wait_ge(s_y, before)
                        if c == 0:
                            down(q - 1, 1 - b, at_before, chunks - 1)
                        else:
                            down(q - 1, 1 - b, at, c - 1)

            turn(0)
            with pe.Fori(1, PAIRS) as i:
                turn(i)
            at = ring_column(MAXBLK - 1)
            turn_gated(chunks * MAXBLK - 1, chunks - 1)
            pe.wait_ge(s_y, MAXBLK - 1)
            down(chunks * MAXBLK - 1, chunks - 1, at, chunks - 1)
            if finish is not None:
                for i in range(TT // 2):
                    pe.wait_ge(s_t, 4 * (i + 1))
                    for t in range(CT):
                        for a in range(2):
                            last = pe.transpose(psum[:, i, N * t + P * a:N * t + P * a + P],
                                                k.t[:, 2 * i + a, P * t:P * t + P], k.ident_sb[:])
                    last.then_inc(s_ft, 1)



class Shared:
    pass


def _host_arrays(inputs):
    bf16 = mybir.dt.np(BF16)
    f = {n: np.asarray(a) for n, a in inputs.items()}
    a = {}

    def tiles(m, rows=P):
        return np.ascontiguousarray(m.reshape((m.shape[0] // rows, rows) + m.shape[1:]).swapaxes(0, 1))

    def per_image(v):
        return np.repeat(v[..., None], B, axis=-1)

    a["x"] = np.ascontiguousarray(f["x"].reshape(B, CT, P, N).transpose(2, 1, 0, 3))
    a["w1"] = np.tile(tiles(f["L0_conv_w1"].reshape(CB, C).T), (1, 1, 2))
    w_off = f["L0_conv_w_off"].reshape(27, CB, 3, 3).transpose(2, 1, 3, 0)
    a["w_off"] = np.stack([np.concatenate([w_off[0], w_off[1]]), np.concatenate([w_off[2], np.zeros_like(w_off[2])])], 1)
    a["b_off"] = np.tile(f["L0_conv_b_off"].reshape(1, 27), (P, 1))
    w2 = f["L0_conv_w2"].reshape(CB, CB, TAPS).transpose(1, 2, 0).reshape(CB, TAPS * CB)
    a["w2"] = np.concatenate([w2, np.zeros_like(w2)])
    w3 = f["L0_conv_w3"].reshape(C, CB).T
    a["w3"] = np.stack([np.concatenate([w3, np.zeros_like(w3)]), np.concatenate([np.zeros_like(w3), w3])], 1)
    gn64 = per_image(np.stack([f["L0_conv_" + n] for n in ("gn1_scale", "gn1_bias", "gn2_scale", "gn2_bias")], 1))
    a["gn64"] = np.concatenate([gn64, gn64])
    a["gn256"] = np.stack([per_image(tiles(f["L0_conv_" + n])).reshape(P, CT * B) for n in ("gn3_scale", "gn3_bias")], 1)
    a["ident"] = np.eye(P, dtype=np.float32)
    a["pair"] = np.kron(np.eye(P // 2), np.full((2, 2), 0.5)).astype(np.float32)
    a["avg8"] = np.kron(np.eye(P // 8), np.full((8, 8), 0.125)).astype(np.float32)
    n = np.arange(N).reshape(NT, P)
    taps = np.arange(TAPS)
    gx = (n % HW)[:, :, None] + taps % 3 - 1
    gy = (n // HW)[:, :, None] + taps // 3 - 1
    grid = np.concatenate([gx, gy], -1).transpose(1, 0, 2)
    a["grid"] = np.tile(grid, (1, B, 1)).astype(np.float32)
    a["iota"] = np.tile(np.arange(HW, dtype=np.float32), (P, 1))
    a["ones"] = np.ones((1, P), np.float32)

    l1 = {n[8:]: m for n, m in f.items() if n.startswith("L1_conv_")}
    a["w_in"] = tiles(l1["in_proj_w"].T)
    a["b_in"] = tiles(l1["in_proj_b"])
    a["dw"] = tiles(np.concatenate([l1["dw_w"].reshape(C, 3), l1["dw_b"].reshape(C, 1)], 1))
    a["w_dbc"] = tiles(l1["dbc_w"].T)
    for name, key in (("a_log", "A_log"), ("d_skip", "Dparam"), ("b_dbc", "dbc_b"), ("b_out", "out_proj_b")):
        a[name] = np.tile(l1[key].reshape(1, -1), (P, 1))
    a["mobius"] = np.tile(l1["mobius"].reshape(1, HEADS, 4), (P, 1, 1))
    a["w_out"] = tiles(l1["out_proj_w"].T)
    side = np.linspace(-1.0, 1.0, HW, dtype=np.float32)
    points = np.stack([np.tile(side, HW), np.repeat(side, HW)])
    own = points.reshape(2, NT, P).transpose(2, 0, 1)
    a["z"] = np.concatenate([np.tile(points, (P, 1, 1)), own], -1)
    a["before"] = (np.arange(N) < n.T[:, :, None]).astype(np.float32)
    a["iota_n"] = np.tile(np.arange(N, dtype=np.float32), (P, 1))
    order = np.arange(P)
    forbid = np.float32(-1e30)
    above = np.where(order[None, :] > order[:, None], forbid, 0.0)
    a["bans"] = np.stack([above, above.T, np.full((P, P), forbid)], 1).astype(bf16)
    a["ident16"] = np.eye(P).astype(bf16)

    a["a2_wqkv"] = tiles(f["L2_attn_w_qkv"])
    a["a2_w_proj"] = tiles(f["L2_attn_w_proj"])
    a["a2_b_proj"] = f["L2_attn_b_proj"].reshape(1, C)
    a["a3_wqkv"] = tiles(np.concatenate([f["L3_attn_" + n] for n in ("Wq", "Wk", "Wv")], 1))
    a["a3_w_proj"] = tiles(f["L3_attn_Wo"])
    a["a3_b_proj"] = f["L3_attn_bo"].reshape(1, C)

    def experts(first, second, last):
        def cols(m, c, part):
            m = m[:, :, CHUNK * c:CHUNK * c + CHUNK] if part < 2 else m[:, CHUNK * c:CHUNK * c + CHUNK, :]
            return m.reshape(E, m.shape[1] // P, P, m.shape[2]).transpose(0, 2, 1, 3).reshape(E, P, -1)

        chunks = first.shape[2] // CHUNK
        return np.concatenate([cols(m, c, part) for c in range(chunks) for part, m in enumerate((first, second, last))], -1)

    a["f2_gate"] = tiles(f["L2_ffn_gate_w"].T)
    a["f2_experts"] = experts(*(f["L2_ffn_" + n].transpose(0, 2, 1) for n in ("w1", "w3", "w2")))
    a["f3_gate"] = tiles(f["L3_ffn_Wg"])
    a["f3_experts"] = experts(*(f["L3_ffn_" + n] for n in ("W1", "W2", "W3")))
    a["iota_e"] = np.tile(np.arange(E, dtype=np.float32), (P, 1))
    a["iota_b"] = np.tile(np.arange(PAIRED, dtype=np.float32), (P, 1))
    a["edges"] = np.tile(np.arange(0, (PAIRED + 1) * P, P, dtype=np.float32), (P, 1))
    a["iota_p"] = np.tile(np.arange(P, dtype=np.float32), (P, 1))
    tile_and_choice = 1 + 2 * np.arange(TT)[None, :] + np.arange(2)[:, None]
    a["labels"] = np.stack([np.tile(tile_and_choice, (P, 1, 1)), np.tile(np.arange(P)[:, None, None], (1, 2, TT))],
                           -1).astype(np.float32)
    a["own_slot"] = (2 * TOK + P + np.arange(PAIRED * P).reshape(PAIRED, P).T).astype(np.float32)
    a["steps"] = np.tile(np.arange(0, TOK, P, dtype=np.float32), (P, 1))
    a["earlier"] = np.stack([order[:, None] < order[None, :], np.ones((P, P))], 1).astype(bf16)
    rows = np.arange(96)[:, None]
    a["select"] = np.repeat((rows % 32 == np.arange(3 * S))[:, :, None], P, 2).astype(bf16)
    return {n: np.ascontiguousarray(m) for n, m in a.items()}


def build(nc, k, out):
    with ExitStack() as ctx:
        def sem(name):
            return ctx.enter_context(nc.semaphore(name))

        def sb(name, shape, dt=F32):
            return ctx.enter_context(nc.sbuf_tensor(name, shape, dt))

        psum = ctx.enter_context(nc.psum_tensor("psum", [P, 8, BANK], F32))
        k.ident_sb = sb("ident_sb", [P, P])
        k.avg8_sb = sb("avg8_sb", [P, P])
        k.x1 = sb("x1", [P, CT, B, N])
        k.h = sb("h", [P, CT, B, N])
        k.t = sb("t", [P, TT, C])
        k.order = k.t[:].rearrange("p t c -> p (t c)")[:, 0:HEADS * NT * N].rearrange("p (h t n) -> p h t n", h=HEADS, n=N)
        k.ring = sb("ring", [P, RING_CHUNKS * CHUNK_COLS])
        k.ring_late = k.ring[:, RING_CHUNKS // 2 * CHUNK_COLS:]
        k.stacks_dram = nc.dram_tensor("stacks_dram", (2, STACK, AH, TOK), BF16, kind="Internal").ap()
        k.rows_in = nc.dram_tensor("rows_in", (2 * TOK, C), F32, kind="Internal").ap()
        k.rows_out = nc.dram_tensor("rows_out", (2 * TOK + PAIRED * P, C), F32, kind="Internal").ap()
        k.s_ring2 = sem("layer_2_experts_loaded")
        k.s_ring3 = sem("layer_3_experts_loaded")
        a2 = dict(wqkv=k.dram["a2_wqkv"], w_proj=k.dram["a2_w_proj"], b_proj=k.dram["a2_b_proj"])
        a3 = dict(wqkv=k.dram["a3_wqkv"], w_proj=k.dram["a3_w_proj"], b_proj=k.dram["a3_b_proj"])
        f2 = dict(gate=k.dram["f2_gate"], experts=k.dram["f2_experts"])
        f3 = dict(gate=k.dram["f3_gate"], experts=k.dram["f3_experts"])
        stores = [out[b].rearrange("(t p) y x -> p t (y x)", p=P) for b in range(B)]

        def own(name):
            return nc.alloc_semaphore(name=name)

        def prefetcher(name, chunks, wanted, loaded):
            def prefetch(sp, i):
                if i < len(wanted):
                    load_chunk(sp, k, k.dram[name], chunks, wanted[i], loaded)
            return prefetch

        with nc.cleanup_on_exit():
            deformable_conv(nc, own, sb, psum, k)
        with nc.cleanup_on_exit():
            selective_scan(nc, own, sb, psum, k)
        with nc.cleanup_on_exit():
            attention(nc, own, sb, psum, k, a2, False, "a2",
                      prefetcher("f2_experts", 1, range(RING_CHUNKS // 2, RING_CHUNKS), k.s_ring2))
        with nc.cleanup_on_exit():
            experts_ffn(nc, own, sb, psum, k, f2, 1, k.s_ring2, "f2")
        with nc.cleanup_on_exit():
            attention(nc, own, sb, psum, k, a3, True, "a3",
                      prefetcher("f3_experts", 2, range(RING_CHUNKS), k.s_ring3))
        with nc.cleanup_on_exit():
            experts_ffn(nc, own, sb, psum, k, f3, 2, k.s_ring3, "f3", stores)


def _prepare(inputs):
    arrays = _host_arrays(inputs)
    return {f"in_{n}": m for n, m in arrays.items()}


def _declare(nc, arrays):
    k = Shared()
    k.dram = {n[3:]: nc.dram_tensor(n, m.shape, mybir.dt.from_np(m.dtype), kind="ExternalInput").ap()
              for n, m in arrays.items()}
    return k


def kernel(**inputs):
    import concourse.bacc as bacc
    from concourse.bass_utils import run_bass_kernel_spmd

    nc = bacc.Bacc("TRN2", target_bir_lowering=False, num_devices=1)
    arrays = _prepare(inputs)
    k = _declare(nc, arrays)
    out = nc.dram_tensor("out", (B, C, HW, HW), F32, kind="ExternalOutput").ap()
    build(nc, k, out)
    result = run_bass_kernel_spmd(nc, [arrays], core_ids=[0])
    return result.results[0]["out"]
```
